# Optimizing a Trainium2 kernel written in Bass

```python
import numpy as np
import jax
import jax.numpy as jnp

def _softmax(x, axis=-1):
    return jax.nn.softmax(x, axis=axis)

def _gelu(x):
    return jax.nn.gelu(x, approximate=True)

def _silu(x):
    return jax.nn.silu(x)

def _sigmoid(x):
    return jax.nn.sigmoid(x)

def _layernorm(x, axis=-1, eps=1e-05):
    m = jnp.mean(x, axis=axis, keepdims=True)
    v = jnp.var(x, axis=axis, keepdims=True)
    return (x - m) / jnp.sqrt(v + eps)

def _scatter_add(tgt, idx, src, axis=0):
    return tgt.at[idx].add(src)

def _segment_sum(src, seg, n):
    return jax.ops.segment_sum(src, seg, n)
kernel_name = 'mk_decoder_preln_d2_seqx_r4_7f8960'

def setup_inputs(seed: int=0):
    np.random.seed(seed)
    _w = jnp.asarray

    def _rec_inputs():
        import jax
        import jax.numpy as jnp
        _rk = jax.random.key(seed)
        x = -0.0002928 + 1 * jax.random.normal(jax.random.fold_in(_rk, 1), (16, 512, 256), jnp.float32)
        _lenS = 512 - jax.random.randint(jax.random.fold_in(_rk, 7), (16,), 0, max(1, 512 // 4) + 1, jnp.int32)
        _lenS2 = 64 - jax.random.randint(jax.random.fold_in(_rk, 8), (16,), 0, max(1, 64 // 4) + 1, jnp.int32)
        _ctx_1024P = jax.random.normal(jax.random.fold_in(_rk, 11), (16, 16, 256), jnp.float32)
        _ctx_1024c = jax.random.dirichlet(jax.random.fold_in(_rk, 511), 0.3 * jnp.ones((16,), jnp.float32), (16, 64))
        _ctx_1024t = jnp.einsum('bsk,bkd->bsd', _ctx_1024c, _ctx_1024P)
        _ctx_1024t = _ctx_1024t * jax.lax.rsqrt(jnp.mean(jnp.square(_ctx_1024t)) + 1e-12) * 0.953939
        ctx_1024 = -1.39393e-06 + 0.999914 * (_ctx_1024t + 0.3 * jax.random.normal(jax.random.fold_in(_rk, 611), (16, 64, 256), jnp.float32))
        fside_BxSxS2_0 = jax.random.uniform(jax.random.fold_in(_rk, 13), (16, 512, 64), jnp.float32, 0.0, 1)
        _validS = jnp.arange(512)[None, :] < _lenS[:, None]
        _validS2 = jnp.arange(64)[None, :] < _lenS2[:, None]
        _causal = jnp.tril(jnp.ones((512, 512), dtype=bool))
        mask_BxSxS2_bf1 = jnp.ones((16, 512, 64), dtype=bool)
        mask_BxSxS2_ik1 = jnp.where(jnp.broadcast_to(_validS2[:, None, :], (16, 512, 64)), 1, 0).astype(jnp.int32)
        return (x, ctx_1024, fside_BxSxS2_0, mask_BxSxS2_bf1, mask_BxSxS2_ik1)
    x, ctx_1024, fside_BxSxS2_0, mask_BxSxS2_bf1, mask_BxSxS2_ik1 = _rec_inputs()

    def _L0_attn_setup():
        import jax, jax.numpy as jnp
        import numpy as np
        B, L, D = (4, 2048, 256)
        N = D
        EPS = 1e-05

        def _ssm_scan(a, x):

            def combine(c1, c2):
                a1, b1 = c1
                a2, b2 = c2
                return (a1 * a2, a2 * b1 + b2)
            _, h = jax.lax.associative_scan(combine, (a, x), axis=1)
            return h
        key = jax.random.key(seed)
        ks = jax.random.split(key, 9)
        s = 1.0 / np.sqrt(D)
        return {'x': jax.random.normal(ks[0], (B, L, D), dtype=jnp.float32), 'norm_w': jnp.ones((D,), dtype=jnp.float32), 'A_w': jax.random.uniform(ks[1], (N, D), minval=-s, maxval=s), 'A_b': jax.random.uniform(ks[2], (N,), minval=-s, maxval=s), 'B_w': jax.random.uniform(ks[3], (N, D), minval=-s, maxval=s), 'C_w': jax.random.uniform(ks[4], (N, D), minval=-s, maxval=s), 'D_w': jax.random.uniform(ks[5], (N, D), minval=-s, maxval=s), 'out_w': jax.random.uniform(ks[6], (D, N), minval=-s, maxval=s), 'out_b': jax.random.uniform(ks[7], (D,), minval=-s, maxval=s)}
    _L0_attn_all = _L0_attn_setup()
    _L0_attn_in = {k: v for k, v in _L0_attn_all.items() if k in ('norm_w', 'A_w', 'A_b', 'B_w', 'C_w', 'D_w', 'out_w', 'out_b')}
    del _L0_attn_all

    def _L0_xattn_setup():
        import jax, jax.numpy as jnp
        import numpy as np
        D_MODEL = 256
        NUM_HEADS = 16
        D_H = D_MODEL // NUM_HEADS

        def _xavier(key, out_f, in_f):
            limit = np.sqrt(6.0 / (in_f + out_f))
            return jax.random.uniform(key, (out_f, in_f), jnp.float32, -limit, limit)
        key = jax.random.key(seed)
        ks = jax.random.split(key, 8)
        B, S = (2, 512)
        q = jax.random.normal(ks[0], (B, S, D_MODEL), jnp.float32)
        k = jax.random.normal(ks[1], (B, S, D_MODEL), jnp.float32)
        v = jax.random.normal(ks[2], (B, S, D_MODEL), jnp.float32)
        attn_mask = jnp.ones((B, S, S), dtype=bool)
        Wq = _xavier(ks[3], D_MODEL, D_MODEL)
        bq = jnp.zeros((D_MODEL,), jnp.float32)
        Wk = _xavier(ks[4], D_MODEL, D_MODEL)
        bk = jnp.zeros((D_MODEL,), jnp.float32)
        Wv = _xavier(ks[5], D_MODEL, D_MODEL)
        bv = jnp.zeros((D_MODEL,), jnp.float32)
        Wo = _xavier(ks[6], D_MODEL, D_MODEL)
        bo = jnp.zeros((D_MODEL,), jnp.float32)
        return {'q': q, 'k': k, 'v': v, 'attn_mask': attn_mask, 'Wq': Wq, 'bq': bq, 'Wk': Wk, 'bk': bk, 'Wv': Wv, 'bv': bv, 'Wo': Wo, 'bo': bo}
    _L0_xattn_all = _L0_xattn_setup()
    _L0_xattn_in = {k: v for k, v in _L0_xattn_all.items() if k in ('Wq', 'bq', 'Wk', 'bk', 'Wv', 'bv', 'Wo', 'bo')}
    del _L0_xattn_all

    def _L0_ffn_setup():
        import jax, jax.numpy as jnp
        import numpy as np
        key = jax.random.key(seed)
        k1, k2, k3, k4, k5 = jax.random.split(key, 5)
        d_in, d_out, r = (256, 256, 32)
        x = jax.random.normal(k1, (8, 2048, d_in), dtype=jnp.float32)
        W = jax.random.normal(k2, (d_out, d_in), dtype=jnp.float32) * (1.0 / np.sqrt(d_in))
        b = jax.random.normal(k3, (d_out,), dtype=jnp.float32) * 0.01
        V_r = jax.random.normal(k4, (d_in, r), dtype=jnp.float32) * (1.0 / np.sqrt(d_in))
        C = jax.random.normal(k5, (d_out, r), dtype=jnp.float32) * (1.0 / np.sqrt(r))
        return {'x': x, 'W': W, 'b': b, 'V_r': V_r, 'C': C}
    _L0_ffn_all = _L0_ffn_setup()
    _L0_ffn_in = {k: v for k, v in _L0_ffn_all.items() if k in ('W', 'b', 'V_r', 'C')}
    del _L0_ffn_all

    def _L1_attn_setup():
        import jax, jax.numpy as jnp
        import numpy as np
        from jax import lax
        B, S, D = (16, 256, 256)
        PE = 20
        NB = 3
        EPS = 1e-12

        def _lstm(x, W_ih, W_hh, b_ih, b_hh):
            b, _, _ = x.shape
            H = W_hh.shape[1]
            xg = jnp.einsum('bsd,gd->bsg', x, W_ih) + b_ih + b_hh

            def step(carry, xg_t):
                h, c = carry
                g = xg_t + h @ W_hh.T
                i, f, gg, o = jnp.split(g, 4, axis=-1)
                c = jax.nn.sigmoid(f) * c + jax.nn.sigmoid(i) * jnp.tanh(gg)
                h = jax.nn.sigmoid(o) * jnp.tanh(c)
                return ((h, c), h)
            init = (jnp.zeros((b, H), x.dtype), jnp.zeros((b, H), x.dtype))
            _, hs = lax.scan(step, init, xg.transpose(1, 0, 2))
            return hs.transpose(1, 0, 2)

        def _forward(x, W_ih, W_hh, b_ih, b_hh, W_mu, b_mu, W_sig, b_sig):
            b, s, d = x.shape
            pw = _lstm(x, W_ih, W_hh, b_ih, b_hh)
            mu_w = jax.nn.relu(jnp.einsum('bsp,np->bsn', pw, W_mu) + b_mu)
            sigma = jax.nn.sigmoid(jnp.einsum('bsp,op->bso', pw, W_sig) + b_sig)[..., 0]
            j_idx = jnp.arange(s, dtype=x.dtype)

            def mu_step(prev_mu, inputs):
                w_t, j = inputs
                mu = w_t[:, 0] * prev_mu + w_t[:, 1] / s + w_t[:, 2] * (j + 1.0) / s
                return (mu, mu)
            _, mus = lax.scan(mu_step, jnp.zeros((b,), x.dtype), (mu_w.transpose(1, 0, 2), j_idx))
            mu = mus.T
            i_idx = jnp.arange(s, dtype=x.dtype)
            rel = i_idx[None, :] / (j_idx[:, None] + 1.0)
            mask = i_idx[None, :] <= j_idx[:, None]
            w = jnp.exp(-(rel[None] - mu[:, :, None]) ** 2 / (2.0 * sigma[:, :, None] ** 2))
            w = jnp.where(mask[None], w, 0.0)
            norm = jnp.sqrt(jnp.sum(w * w, axis=-1, keepdims=True))
            w = w / jnp.maximum(norm, EPS)
            context = jnp.einsum('bji,bid->bjd', w, x)
            return context
        key = jax.random.key(seed)
        ks = jax.random.split(key, 10)
        s = lambda *sh: 0.05
        inp = {'x': jax.random.normal(ks[0], (B, S, D), dtype=jnp.float32), 'W_ih': jax.random.normal(ks[1], (4 * PE, D), dtype=jnp.float32) * 0.02, 'W_hh': jax.random.normal(ks[2], (4 * PE, PE), dtype=jnp.float32) * 0.02, 'b_ih': jax.random.normal(ks[3], (4 * PE,), dtype=jnp.float32) * 0.02, 'b_hh': jax.random.normal(ks[4], (4 * PE,), dtype=jnp.float32) * 0.02, 'W_mu': jax.random.normal(ks[5], (NB, PE), dtype=jnp.float32) * 0.1, 'b_mu': jax.random.normal(ks[6], (NB,), dtype=jnp.float32) * 0.1, 'W_sig': jax.random.normal(ks[7], (1, PE), dtype=jnp.float32) * 0.1, 'b_sig': jax.random.normal(ks[8], (1,), dtype=jnp.float32) * 0.1}
        return inp
    _L1_attn_all = _L1_attn_setup()
    _L1_attn_in = {k: v for k, v in _L1_attn_all.items() if k in ('W_ih', 'W_hh', 'b_ih', 'b_hh', 'W_mu', 'b_mu', 'W_sig', 'b_sig')}
    del _L1_attn_all

    def _L1_xattn_setup():
        import jax, jax.numpy as jnp
        import numpy as np
        NUM_HEADS = 16
        HIDDEN = 256
        B, S = (2, 512)

        def _split_heads(x, H):
            b, s, d = x.shape
            return x.reshape(b, s, H, d // H).transpose(0, 2, 1, 3)
        key = jax.random.key(seed)
        ks = jax.random.split(key, 14)
        D = HIDDEN
        scale = 1.0 / np.sqrt(D)
        inp = {'query': jax.random.normal(ks[0], (B, S, D), jnp.float32), 'key_in': jax.random.normal(ks[1], (B, S, D), jnp.float32), 'value': jax.random.normal(ks[2], (B, S, D), jnp.float32), 'group_prob': jax.random.uniform(ks[3], (B, S, S), jnp.float32), 'mask': jax.random.randint(ks[4], (B, S, S), 0, 2, jnp.int32), 'wq_k': jax.random.normal(ks[5], (D, D), jnp.float32) * scale, 'wq_b': jnp.zeros((D,), jnp.float32), 'wk_k': jax.random.normal(ks[6], (D, D), jnp.float32) * scale, 'wk_b': jnp.zeros((D,), jnp.float32), 'wv_k': jax.random.normal(ks[7], (D, D), jnp.float32) * scale, 'wv_b': jnp.zeros((D,), jnp.float32), 'wo_k': jax.random.normal(ks[8], (D, D), jnp.float32) * scale, 'wo_b': jnp.zeros((D,), jnp.float32)}
        return inp
    _L1_xattn_all = _L1_xattn_setup()
    _L1_xattn_in = {k: v for k, v in _L1_xattn_all.items() if k in ('wq_k', 'wq_b', 'wk_k', 'wk_b', 'wv_k', 'wv_b', 'wo_k', 'wo_b')}
    del _L1_xattn_all

    def _L1_ffn_setup():
        import jax, jax.numpy as jnp
        import numpy as np
        DIM = 256
        MLP_MULT = 4
        NUM_EXPERTS = 8
        EXPERT_HIDDEN = MLP_MULT * DIM // NUM_EXPERTS
        key = jax.random.key(seed)
        k_x, k_r, k_fc, k_pj = jax.random.split(key, 4)
        x = jax.random.normal(k_x, (4, 1024, DIM), dtype=jnp.float32)
        w_router = jax.random.normal(k_r, (NUM_EXPERTS, DIM), dtype=jnp.float32) * (1.0 / np.sqrt(DIM))
        w_fc = jax.random.normal(k_fc, (NUM_EXPERTS, EXPERT_HIDDEN, DIM), dtype=jnp.float32) * (1.0 / np.sqrt(DIM))
        w_proj = jax.random.normal(k_pj, (NUM_EXPERTS, DIM, EXPERT_HIDDEN), dtype=jnp.float32) * (1.0 / np.sqrt(EXPERT_HIDDEN))
        return {'x': x, 'w_router': w_router, 'w_fc': w_fc, 'w_proj': w_proj}
    _L1_ffn_all = _L1_ffn_setup()
    _L1_ffn_in = {k: v for k, v in _L1_ffn_all.items() if k in ('w_router', 'w_fc', 'w_proj')}
    del _L1_ffn_all
    return {'x': x, 'ctx_1024': ctx_1024, 'fside_BxSxS2_0': fside_BxSxS2_0, 'mask_BxSxS2_bf1': mask_BxSxS2_bf1, 'mask_BxSxS2_ik1': mask_BxSxS2_ik1, 'L0_attn_norm_w': _L0_attn_in['norm_w'], 'L0_attn_A_w': _L0_attn_in['A_w'], 'L0_attn_A_b': _L0_attn_in['A_b'], 'L0_attn_B_w': _L0_attn_in['B_w'], 'L0_attn_C_w': _L0_attn_in['C_w'], 'L0_attn_D_w': _L0_attn_in['D_w'], 'L0_attn_out_w': _L0_attn_in['out_w'], 'L0_attn_out_b': _L0_attn_in['out_b'], 'L0_xattn_Wq': _L0_xattn_in['Wq'], 'L0_xattn_bq': _L0_xattn_in['bq'], 'L0_xattn_Wk': _L0_xattn_in['Wk'], 'L0_xattn_bk': _L0_xattn_in['bk'], 'L0_xattn_Wv': _L0_xattn_in['Wv'], 'L0_xattn_bv': _L0_xattn_in['bv'], 'L0_xattn_Wo': _L0_xattn_in['Wo'], 'L0_xattn_bo': _L0_xattn_in['bo'], 'L0_ffn_W': _L0_ffn_in['W'], 'L0_ffn_b': _L0_ffn_in['b'], 'L0_ffn_V_r': _L0_ffn_in['V_r'], 'L0_ffn_C': _L0_ffn_in['C'], 'L1_attn_W_ih': _L1_attn_in['W_ih'], 'L1_attn_W_hh': _L1_attn_in['W_hh'], 'L1_attn_b_ih': _L1_attn_in['b_ih'], 'L1_attn_b_hh': _L1_attn_in['b_hh'], 'L1_attn_W_mu': _L1_attn_in['W_mu'], 'L1_attn_b_mu': _L1_attn_in['b_mu'], 'L1_attn_W_sig': _L1_attn_in['W_sig'], 'L1_attn_b_sig': _L1_attn_in['b_sig'], 'L1_xattn_wq_k': _L1_xattn_in['wq_k'], 'L1_xattn_wq_b': _L1_xattn_in['wq_b'], 'L1_xattn_wk_k': _L1_xattn_in['wk_k'], 'L1_xattn_wk_b': _L1_xattn_in['wk_b'], 'L1_xattn_wv_k': _L1_xattn_in['wv_k'], 'L1_xattn_wv_b': _L1_xattn_in['wv_b'], 'L1_xattn_wo_k': _L1_xattn_in['wo_k'], 'L1_xattn_wo_b': _L1_xattn_in['wo_b'], 'L1_ffn_w_router': _L1_ffn_in['w_router'], 'L1_ffn_w_fc': _L1_ffn_in['w_fc'], 'L1_ffn_w_proj': _L1_ffn_in['w_proj']}

def reference(x, ctx_1024, fside_BxSxS2_0, mask_BxSxS2_bf1, mask_BxSxS2_ik1, L0_attn_norm_w, L0_attn_A_w, L0_attn_A_b, L0_attn_B_w, L0_attn_C_w, L0_attn_D_w, L0_attn_out_w, L0_attn_out_b, L0_xattn_Wq, L0_xattn_bq, L0_xattn_Wk, L0_xattn_bk, L0_xattn_Wv, L0_xattn_bv, L0_xattn_Wo, L0_xattn_bo, L0_ffn_W, L0_ffn_b, L0_ffn_V_r, L0_ffn_C, L1_attn_W_ih, L1_attn_W_hh, L1_attn_b_ih, L1_attn_b_hh, L1_attn_W_mu, L1_attn_b_mu, L1_attn_W_sig, L1_attn_b_sig, L1_xattn_wq_k, L1_xattn_wq_b, L1_xattn_wk_k, L1_xattn_wk_b, L1_xattn_wv_k, L1_xattn_wv_b, L1_xattn_wo_k, L1_xattn_wo_b, L1_ffn_w_router, L1_ffn_w_fc, L1_ffn_w_proj):
    import jax
    import jax.numpy as jnp

    def _L0_attn_ref(x, norm_w, A_w, A_b, B_w, C_w, D_w, out_w, out_b):
        import jax, jax.numpy as jnp
        import numpy as np
        B, L, D = (4, 2048, 256)
        N = D
        EPS = 1e-05

        def _ssm_scan(a, x):

            def combine(c1, c2):
                a1, b1 = c1
                a2, b2 = c2
                return (a1 * a2, a2 * b1 + b2)
            _, h = jax.lax.associative_scan(combine, (a, x), axis=1)
            return h
        residual = x
        norm = jnp.sqrt(jnp.mean(x * x, axis=-1, keepdims=True) + EPS)
        xn = x * (norm_w / norm)
        a = jax.nn.sigmoid(jnp.einsum('bld,nd->bln', xn, A_w) + A_b)
        b = jnp.einsum('bld,nd->bln', xn, B_w)
        c = jax.nn.sigmoid(jnp.einsum('bld,nd->bln', xn, C_w))
        d = jax.nn.sigmoid(jnp.einsum('bld,nd->bln', xn, D_w))
        h = c * _ssm_scan(a, d * b)
        y = jnp.einsum('bln,dn->bld', h, out_w) + out_b
        return y + residual

    def _L0_xattn_ref(q, k, v, attn_mask, Wq, bq, Wk, bk, Wv, bv, Wo, bo):
        import jax, jax.numpy as jnp
        import numpy as np
        D_MODEL = 256
        NUM_HEADS = 16
        D_H = D_MODEL // NUM_HEADS

        def _xavier(key, out_f, in_f):
            limit = np.sqrt(6.0 / (in_f + out_f))
            return jax.random.uniform(key, (out_f, in_f), jnp.float32, -limit, limit)
        B, S, _ = q.shape
        H, Dh = (NUM_HEADS, D_H)
        Q = jnp.einsum('bsd,ed->bse', q, Wq) + bq
        K = jnp.einsum('bsd,ed->bse', k, Wk) + bk
        V = jnp.einsum('bsd,ed->bse', v, Wv) + bv
        Qm = Q.reshape(B, S, H, Dh).transpose(0, 2, 1, 3)
        Km = K.reshape(B, -1, H, Dh).transpose(0, 2, 1, 3)
        Vm = V.reshape(B, -1, H, Dh).transpose(0, 2, 1, 3)
        scores = jnp.einsum('bhqd,bhkd->bhqk', Qm, Km) / jnp.sqrt(jnp.float32(Dh))
        fill = jnp.finfo(scores.dtype).min
        scores = jnp.where(attn_mask[:, None, :, :], scores, fill)
        attn = jax.nn.softmax(scores, axis=-1)
        A = jnp.einsum('bhqk,bhkd->bhqd', attn, Vm)
        A = A.transpose(0, 2, 1, 3).reshape(B, S, H * Dh)
        O = jnp.einsum('bsd,ed->bse', A, Wo) + bo
        return O

    def _L0_ffn_ref(x, W, b, V_r, C):
        import jax, jax.numpy as jnp
        import numpy as np
        base = jnp.einsum('bsd,od->bso', x, W) + b
        correction = jnp.einsum('bsr,or->bso', jnp.einsum('bsd,dr->bsr', x, V_r), C)
        return base + correction

    def _L1_attn_ref(x, W_ih, W_hh, b_ih, b_hh, W_mu, b_mu, W_sig, b_sig):
        import jax, jax.numpy as jnp
        import numpy as np
        from jax import lax
        B, S, D = (16, 256, 256)
        PE = 20
        NB = 3
        EPS = 1e-12

        def _lstm(x, W_ih, W_hh, b_ih, b_hh):
            b, _, _ = x.shape
            H = W_hh.shape[1]
            xg = jnp.einsum('bsd,gd->bsg', x, W_ih) + b_ih + b_hh

            def step(carry, xg_t):
                h, c = carry
                g = xg_t + h @ W_hh.T
                i, f, gg, o = jnp.split(g, 4, axis=-1)
                c = jax.nn.sigmoid(f) * c + jax.nn.sigmoid(i) * jnp.tanh(gg)
                h = jax.nn.sigmoid(o) * jnp.tanh(c)
                return ((h, c), h)
            init = (jnp.zeros((b, H), x.dtype), jnp.zeros((b, H), x.dtype))
            _, hs = lax.scan(step, init, xg.transpose(1, 0, 2))
            return hs.transpose(1, 0, 2)

        def _forward(x, W_ih, W_hh, b_ih, b_hh, W_mu, b_mu, W_sig, b_sig):
            b, s, d = x.shape
            pw = _lstm(x, W_ih, W_hh, b_ih, b_hh)
            mu_w = jax.nn.relu(jnp.einsum('bsp,np->bsn', pw, W_mu) + b_mu)
            sigma = jax.nn.sigmoid(jnp.einsum('bsp,op->bso', pw, W_sig) + b_sig)[..., 0]
            j_idx = jnp.arange(s, dtype=x.dtype)

            def mu_step(prev_mu, inputs):
                w_t, j = inputs
                mu = w_t[:, 0] * prev_mu + w_t[:, 1] / s + w_t[:, 2] * (j + 1.0) / s
                return (mu, mu)
            _, mus = lax.scan(mu_step, jnp.zeros((b,), x.dtype), (mu_w.transpose(1, 0, 2), j_idx))
            mu = mus.T
            i_idx = jnp.arange(s, dtype=x.dtype)
            rel = i_idx[None, :] / (j_idx[:, None] + 1.0)
            mask = i_idx[None, :] <= j_idx[:, None]
            w = jnp.exp(-(rel[None] - mu[:, :, None]) ** 2 / (2.0 * sigma[:, :, None] ** 2))
            w = jnp.where(mask[None], w, 0.0)
            norm = jnp.sqrt(jnp.sum(w * w, axis=-1, keepdims=True))
            w = w / jnp.maximum(norm, EPS)
            context = jnp.einsum('bji,bid->bjd', w, x)
            return context
        return _forward(x, W_ih, W_hh, b_ih, b_hh, W_mu, b_mu, W_sig, b_sig)

    def _L1_xattn_ref(query, key_in, value, group_prob, mask, wq_k, wq_b, wk_k, wk_b, wv_k, wv_b, wo_k, wo_b):
        import jax, jax.numpy as jnp
        import numpy as np
        NUM_HEADS = 16
        HIDDEN = 256
        B, S = (2, 512)

        def _split_heads(x, H):
            b, s, d = x.shape
            return x.reshape(b, s, H, d // H).transpose(0, 2, 1, 3)
        H = NUM_HEADS
        dh = query.shape[-1] // H
        q = _split_heads(query @ wq_k + wq_b, H)
        k = _split_heads(key_in @ wk_k + wk_b, H)
        v = _split_heads(value @ wv_k + wv_b, H)
        logits = jnp.einsum('bhqd,bhkd->bhqk', q, k) / jnp.sqrt(jnp.asarray(dh, q.dtype))
        neg = (1.0 - mask.astype(q.dtype)) * -1000000000.0
        logits = logits + neg[:, None, :, :]
        attn = jax.nn.softmax(logits, axis=-1)
        attn = attn * group_prob[:, None, :, :]
        out = jnp.einsum('bhqk,bhkd->bhqd', attn, v)
        out = out.transpose(0, 2, 1, 3).reshape(query.shape[0], -1, H * dh)
        return out @ wo_k + wo_b

    def _L1_ffn_ref(x, w_router, w_fc, w_proj):
        import jax, jax.numpy as jnp
        import numpy as np
        DIM = 256
        MLP_MULT = 4
        NUM_EXPERTS = 8
        EXPERT_HIDDEN = MLP_MULT * DIM // NUM_EXPERTS
        logits = jnp.einsum('bsd,ed->bse', jax.lax.stop_gradient(x), w_router)
        weights = jax.nn.softmax(logits, axis=-1)
        indices = jnp.argmax(weights, axis=-1)
        onehot = jax.nn.one_hot(indices, NUM_EXPERTS, dtype=x.dtype)
        h = jnp.einsum('bsd,ehd->bseh', x, w_fc)
        h = jnp.where(h >= 0, h, 0.5 * h)
        h = h * h
        out = jnp.einsum('bseh,edh,bse->bsd', h, w_proj, onehot)
        return out
    x = x + _L0_attn_ref(_layernorm(x, axis=-1), L0_attn_norm_w, L0_attn_A_w, L0_attn_A_b, L0_attn_B_w, L0_attn_C_w, L0_attn_D_w, L0_attn_out_w, L0_attn_out_b)
    x = x + _L0_xattn_ref(_layernorm(x, axis=-1), ctx_1024, ctx_1024, mask_BxSxS2_bf1, L0_xattn_Wq, L0_xattn_bq, L0_xattn_Wk, L0_xattn_bk, L0_xattn_Wv, L0_xattn_bv, L0_xattn_Wo, L0_xattn_bo)
    x = x + _L0_ffn_ref(_layernorm(x, axis=-1), L0_ffn_W, L0_ffn_b, L0_ffn_V_r, L0_ffn_C)
    x = x + _L1_attn_ref(_layernorm(x, axis=-1), L1_attn_W_ih, L1_attn_W_hh, L1_attn_b_ih, L1_attn_b_hh, L1_attn_W_mu, L1_attn_b_mu, L1_attn_W_sig, L1_attn_b_sig)
    x = x + _L1_xattn_ref(_layernorm(x, axis=-1), ctx_1024, ctx_1024, fside_BxSxS2_0, mask_BxSxS2_ik1, L1_xattn_wq_k, L1_xattn_wq_b, L1_xattn_wk_k, L1_xattn_wk_b, L1_xattn_wv_k, L1_xattn_wv_b, L1_xattn_wo_k, L1_xattn_wo_b)
    x = x + _L1_ffn_ref(_layernorm(x, axis=-1), L1_ffn_w_router, L1_ffn_w_fc, L1_ffn_w_proj)
    return x

_drawn_inputs = setup_inputs


def setup_inputs(seed=0):
    import zlib

    import numpy as np

    out = dict(_drawn_inputs(seed))
    spreads = {'L0_attn_norm_w': (1.0, 0.6),
     'L0_xattn_bq': (0.0, 0.1),
     'L0_xattn_bk': (0.0, 2.0),
     'L0_xattn_bv': (0.0, 0.1),
     'L0_xattn_bo': (0.0, 0.1),
     'L1_xattn_wq_b': (0.0, 0.535),
     'L1_xattn_wk_b': (0.0, 2.0),
     'L1_xattn_wv_b': (0.0, 0.1),
     'L1_xattn_wo_b': (0.0, 0.1)}
    factors = {'L0_attn_A_w': 3.209,
     'L0_attn_A_b': 25.282,
     'L1_attn_W_ih': 3.056,
     'L1_attn_W_hh': 8.0,
     'L1_attn_b_ih': 7.941,
     'L1_attn_b_hh': 8.0,
     'L1_attn_W_mu': 3.811,
     'L1_attn_W_sig': 3.526,
     'L1_attn_b_mu': 4.251}
    for name, (base, spread) in spreads.items():
        noise = np.random.default_rng([zlib.crc32(name.encode()), seed]).standard_normal(out[name].shape)
        drawn = base * np.exp(spread * noise) if base else spread * noise
        out[name] = jnp.asarray(drawn.astype(out[name].dtype))
    for name, factor in factors.items():
        out[name] = (out[name] * factor).astype(out[name].dtype)
    return out
```

```python
from contextlib import ExitStack

import concourse.bass as bass
from concourse import mybir

ALU = mybir.AluOpType
ACT = mybir.ActivationFunctionType
F32 = mybir.dt.float32
BF16 = mybir.dt.bfloat16
AX_X = mybir.AxisListType.X

P = 128
B, S, D = 16, 512, 256
SK, H = 64, 16
GB = 4
NC_, NG = S // P, B // GB
NT = GB * P
NH = D // P
NP = H // 2
HD = D // H
PE_ = 20
NE = 8
STEPS = P // NG
EPS = 1e-5
FMAX = 3.4028234663852886e38
VW = 2 * HD + 2


class LayerNorm:

    def __init__(self, name, sb, sem):
        self.stats, self.mv = sb(f"{name}_stats", [P, GB, 6]), sb(f"{name}_mv", [P, GB, 2])
        self.ve, self.rstd = sb(f"{name}_ve", [P, 2, GB]), sb(f"{name}_rstd", [P, 2, GB])
        self.tmp = sb(f"{name}_tmp", [P, 3, GB])
        self.small, self.inv, self.normed = sem(f"{name}_small"), sem(f"{name}_inv"), sem(f"{name}_normed")
        self.turned, self.landed = sem(f"{name}_turned"), sem(f"{name}_landed")


class Attention:

    def __init__(self, name, sem):
        self.q, self.q_ready, self.kbd = sem(f"{name}_q"), sem(f"{name}_q_ready"), sem(f"{name}_kbd")
        self.scores, self.masked, self.top = sem(f"{name}_scores"), sem(f"{name}_masked"), sem(f"{name}_top")
        self.shifted, self.exped, self.summed = sem(f"{name}_shifted"), sem(f"{name}_exped"), sem(f"{name}_summed")
        self.gated, self.turned, self.exT = sem(f"{name}_gated"), sem(f"{name}_turned"), sem(f"{name}_exT")
        self.pv, self.inv, self.o = sem(f"{name}_pv"), sem(f"{name}_inv"), sem(f"{name}_o")
        self.o_turned, self.oT, self.proj = sem(f"{name}_o_turned"), sem(f"{name}_oT"), sem(f"{name}_proj")
        self.base, self.done, self.v_load = sem(f"{name}_base"), sem(f"{name}_done"), sem(f"{name}_v_load")
        self.m_load, self.neg = sem(f"{name}_m_load"), sem(f"{name}_neg")


def positive(value):
    return not (isinstance(value, int) and value <= 0)


def chunk_units(engine, c, body):
    if c == 0:
        body(0, 0, 0)
    with engine.Fori(1 if c == 0 else 0, NG) as g:
        body(c, g, NG * c + g)


def decoder_program(nc, a, out):
    ctx = ExitStack()
    with ctx:
        def sb(name, shape, dt=F32):
            return ctx.enter_context(nc.sbuf_tensor(name, shape, dt))

        def ps(name, shape, dt=F32):
            return ctx.enter_context(nc.psum_tensor(name, shape, dt))

        def sem(name):
            return ctx.enter_context(nc.semaphore(name))

        x3_dram = nc.dram_tensor("x3_dram", [B, S, D], F32, kind="Internal").ap()
        xln_dram = nc.dram_tensor("xln_dram", [B, S, D], F32, kind="Internal").ap()
        v_dram = nc.dram_tensor("v_dram", [2, B, P, NP * VW], F32, kind="Internal").ap()

        ident = sb("ident", [P, P])
        tri = sb("tri", [P, P])
        headmask = sb("headmask", [P, NE])
        rank = sb("rank", [P, NE])
        neghalf = sb("neghalf", [P, GB])
        sel = sb("sel", [NE, NE, P], BF16)

        posl = sb("posl", [64, NC_, P])
        jrow = sb("jrow", [1, 2, S])
        wA = sb("wA", [P, NH, D])
        wB = sb("wB", [P, NH, D])
        wC = sb("wC", [P, NH, D])
        wD = sb("wD", [P, NH, D])
        wOut = sb("wOut", [P, NH, D])
        wQ = [sb(f"wQ{l}", [P, NH, D]) for l in range(2)]
        wO = [sb(f"wO{l}", [P, NH, D]) for l in range(2)]
        wF = sb("wF", [P, NH, D])
        wih = sb("wih", [P, NH, 96])
        wcat = sb("wcat", [P, 80])
        wms = sb("wms", [P, P])
        wR = sb("wR", [P, NH, NE])
        wfc = sb("wfc", [P, NH, NE * P])
        wpj = sb("wpj", [P, NE, D])
        normw = sb("normw", [P, NH])
        biasA = sb("biasA", [P, NH])
        biasQ = [sb(f"biasQ{l}", [P, NH]) for l in range(2)]
        biasK = [sb(f"biasK{l}", [P, NH]) for l in range(2)]
        biasG = sb("biasG", [96, 2])
        rowOut = sb("rowOut", [P, D])
        rowO = [sb(f"rowO{l}", [P, D]) for l in range(2)]
        rowF = sb("rowF", [P, D])
        KT = [sb(f"KT{l}", [P, NH, B, SK]) for l in range(2)]
        ones = sb("ones", [P, 1])

        R = sb("R", [P, B, S])
        slots = sb("slots", [P, STEPS + 2, B])
        gates = sb("gates", [B, 5 * PE_])
        uprod = sb("uprod", [B, 2 * PE_])
        tcell = sb("tcell", [B, PE_])
        hnew = sb("hnew", [32, 32])
        carry = sb("carry", [P, NH, B])
        mcarry = sb("mcarry", [1, B])

        xin = sb("xin", [P, GB, D])
        xres = sb("xres", [P, GB, D])
        xnat = sb("xnat", [P, GB, D])
        xT = sb("xT", [P, NH, NT])
        qT = sb("qT", [P, NH, NT])
        kbd = [sb(f"kbd{i}", [P, NH, NE, SK]) for i in range(2)]
        vg = sb("vg", [P, GB, NP * VW])
        ex = [sb(f"ex{i}", [P, H, SK]) for i in range(2)]
        exT = sb("exT", [P, 2, 4, P])
        sel32 = exT[0:NE, :, :, :].rearrange("p j a t -> p (j a) t")
        onat = sb("onat", [P, GB, D])
        mx = sb("mx", [P, H])
        rs = sb("rs", [P, H])
        neg = sb("neg", [P, GB, SK])
        gp = sb("gp", [P, GB, SK])
        mask8 = sb("mask8", [P, GB, SK], mybir.dt.uint8)
        mask32 = sb("mask32", [P, GB, SK], mybir.dt.int32)
        scratch = sb("scratch", [P, 3, NH * GB * (P + 1)])
        sA, sU, sH = (scratch[:, j, :].rearrange("p (a t) -> p a t", t=P + 1) for j in range(3))
        tD = sb("tD", [P, NT])
        tC = sb("tC", [P, NH, NT])
        xln = sb("xln", [P, NC_, GB, D])
        wT = sb("wT", [P, NT])
        wsq = sb("wsq", [P, NT])
        flat = scratch[:, :, :].rearrange("p j n -> p (j n)")
        zrow = flat[0:1, 0:5 * NT].rearrange("p (j n) -> p j n", j=5)
        mrow = sb("mrow", [1, 3, GB * (P + 1)])
        urow = sb("urow", [64, NT])
        nrm = sb("nrm", [P, 2, GB])
        lg = sb("lg", [P, 4, GB, NE])
        lmx = sb("lmx", [P, 2, GB])
        ohT = sb("ohT", [NE, NT], BF16)
        hr, hm, hm2, hq0, hq1 = (flat[:, j * NT:(j + 1) * NT] for j in range(5))
        hq = [hq0, hq1]
        ctxA = xln[:, 0:2, :, :].rearrange("p i b d -> p (i b d)").rearrange("p (h b k) -> p h b k", h=NH, b=B)

        pa = ps("pa", [P, 2 * NT])
        pb = ps("pb", [P, NT])
        pc = ps("pc", [P, NT])
        pg = ps("pg", [P, NT])

        ln = [LayerNorm(f"ln{i}", sb, sem) for i in range(6)]
        at = [Attention(f"at{i}", sem) for i in range(2)]
        w_load, prep_in, prep_pe, prep_ev, prep_v, prep_done = (
            sem(n) for n in ("w_load", "prep_in", "prep_pe", "prep_ev", "prep_v", "prep_done"))
        v_store = [sem(f"v_store{i}") for i in range(GB)]
        wf_pe, wf_ev = sem("wf_pe"), sem("wf_ev")
        x_load, base_ready, p_ready, t_act, u_ready, a_ready, s_carry, s_scan, g_ready, y_ready, x1_ready = (
            sem(n) for n in ("x_load", "base_ready", "p_ready", "t_act", "u_ready", "a_ready", "s_carry",
                             "s_scan", "g_ready", "y_ready", "x1_ready"))
        c_ready, f_proj, f_base, x3_ready, xg_pe, xg_ready, x3_store, xln_store = (
            sem(n) for n in ("c_ready", "f_proj", "f_base", "x3_ready", "xg_pe", "xg_ready", "x3_store", "xln_store"))
        l_in, l_pe, l_tanh, l_u, l_c, l_tc, l_h, l_t, l_out = (
            sem(n) for n in ("l_in", "l_pe", "l_tanh", "l_u", "l_c", "l_tc", "l_h", "l_t", "l_out"))
        x3_load, xln_load, z_pe, z_small, z_exp, u_rows, pos_pe, pos_sq, pos_w, pos_m, pos_w2, ctx_pe, n_a, n_b, x4_ready = (
            sem(n) for n in ("x3_load", "xln_load", "z_pe", "z_small", "z_exp", "u_rows",
                             "pos_pe", "pos_sq", "pos_w", "pos_m", "pos_w2", "ctx_pe", "n_a", "n_b", "x4_ready"))
        r_pe, r_small, r_exp, r_oh, oh_pe, oh_ev, fc_pe, sel_pe, fc_relu, fc_sum, fc_mask, fc_sq, moe_pe, x6_ready, o_store = (
            sem(n) for n in ("r_pe", "r_small", "r_exp", "r_oh", "oh_pe", "oh_ev", "fc_pe", "sel_pe",
                             "fc_relu", "fc_sum", "fc_mask", "fc_sq", "moe_pe", "x6_ready", "o_store"))

        halves = lambda w: w.rearrange("(h p) n -> p h n", p=P)
        unit = lambda t, c, g: t[bass.ds(GB * g, GB), c * P:(c + 1) * P, :].rearrange("b t d -> t b d")
        NLOAD = 0
        loads = [
            (ident[:, :], a["c_ident"]), (tri[:, :], a["c_tri"]), (headmask[:, :], a["c_headmask"]),
            (rank[:, :], a["c_rank"]), (sel32[:, :, :], a["c_sel"]), (posl[:, :, :], a["c_posl"]),
            (jrow[:, :, :], a["c_jrow"]),
            (wA[:, :, :], halves(a["A_w"])), (wB[:, :, :], halves(a["B_w"])), (wC[:, :, :], halves(a["C_w"])),
            (wD[:, :, :], halves(a["D_w"])), (wOut[:, :, :], halves(a["out_w"])),
            (wQ[0][:, :, :], halves(a["Wq"])), (wQ[1][:, :, :], halves(a["wq_k"])),
            (wO[0][:, :, :], halves(a["Wo"])), (wO[1][:, :, :], halves(a["wo_k"])),
            (wF[:, :, :], halves(a["W"])), (wR[:, :, :], halves(a["w_router"])), (wih[:, :, :], halves(a["W_ih"])), (biasG[:, :], a["b_gates"]),
            (wfc[:, :, :], halves(a["w_fc"])), (wpj[:, :, :], a["w_proj"]),
            (normw[:, :], a["norm_w"]),
            (biasA[:, :], a["A_b"]),
            (biasQ[0][:, :], a["bq"]),
            (biasQ[1][:, :], a["wq_b"]),
            (biasK[0][:, :], a["bk"]),
            (biasK[1][:, :], a["wk_b"]),
            (rowOut[:, :], a["out_b"].rearrange("(o n) -> o n", o=1).broadcast_to([P, D])),
            (rowO[0][:, :], a["bo"].rearrange("(o n) -> o n", o=1).broadcast_to([P, D])),
            (rowO[1][:, :], a["wo_b"].rearrange("(o n) -> o n", o=1).broadcast_to([P, D])),
            (rowF[:, :], a["b"].rearrange("(o n) -> o n", o=1).broadcast_to([P, D])),
            (ctxA[:, :, :, :], a["ctx"].rearrange("(h p) b k -> p h b k", p=P)),
            (xin[:, 0:NH, :], halves(a["Wk"])), (xin[:, 2:2 + NH, :], halves(a["Wv"])),
            (xres[:, 0:NH, :], halves(a["wk_k"])), (xres[:, 2:2 + NH, :], halves(a["wv_k"])),
            (onat[:, 0, :], a["bv"].rearrange("(o n) -> o n", o=1).broadcast_to([P, D])),
            (onat[:, 1, :], a["wv_b"].rearrange("(o n) -> o n", o=1).broadcast_to([P, D])),
            (onat[0:32, 2, :], a["C"]), (onat[0:32, 3, :], a["V_r"]),
        ]
        late_loads = [
            (wcat[0:80, :], a["c_gatesel"]), (wcat[96:116, :], a["W_hh"]),
            (wms[80:81, :], a["b_mu_sig"]), (wms[96:116, :], a["W_mu_sig"]),
        ]
        NLOAD = 16 * (len(loads) + len(late_loads))
        block = ctx.enter_context(nc.Block())

        @block.sync
        def _(sp):
            for dst, src in loads:
                sp.dma_start(dst, src).then_inc(w_load, 16)
            sp.wait_ge(prep_in, 3)
            for dst, src in late_loads:
                sp.dma_start(dst, src).then_inc(w_load, 16)
            for l in range(2):
                for b in range(B):
                    n = l * B + b
                    sp.wait_ge(prep_v, 2 * n + 2)
                    sp.dma_start(v_dram[l, b, :, :], vg[:, n % GB, :]).then_inc(v_store[n % GB], 16)

            def unit_loads(l, c, g, n):
                if positive(GB * n):
                    sp.wait_ge(at[l].pv, GB * n)
                if l == 1:
                    if positive(GB * n):
                        sp.wait_ge(at[1].gated, GB * n)
                if positive(n):
                    sp.wait_ge(at[l].neg, n)
                sp.dma_start(vg[:, :, :], v_dram[l, bass.ds(GB * g, GB), :, :].rearrange("b p n -> p b n")
                             ).then_inc(at[l].v_load, 16)
                if l == 0:
                    sp.dma_start(mask8[:, :, :], unit(a["mask0"], c, g)).then_inc(at[0].m_load, 16)
                else:
                    sp.dma_start(mask32[:, :, :], unit(a["mask1"], c, g)).then_inc(at[1].m_load, 16)
                    sp.dma_start(gp[:, :, :], unit(a["fside"], c, g)).then_inc(at[1].m_load, 16)

            for i in range(GB):
                sp.wait_ge(v_store[i], 16 * (2 * B // GB))
            sp.wait_ge(prep_done, 1)
            def layer0(c, g, n):
                if positive(n):
                    sp.wait_ge(base_ready, n)
                if positive(n):
                    sp.wait_ge(ln[0].normed, n)
                sp.dma_start(xin[:, :, :], unit(a["x"], c, g)).then_inc(x_load, 16)
                unit_loads(0, c, g, n)
                sp.wait_ge(ln[3].normed, n + 1)
                sp.dma_start(unit(xln_dram, c, g), xnat[:, :, :]).then_inc(xln_store, 16)
                sp.dma_start(unit(x3_dram, c, g), xres[:, :, :]).then_inc(x3_store, 16)

            for c in range(NC_):
                chunk_units(sp, c, layer0)
            sp.wait_ge(xln_store, 16 * NC_ * NG)
            sp.wait_ge(x3_store, 16 * NC_ * NG)
            sp.wait_ge(at[0].pv, GB * NC_ * NG)
            def layer1(c, g, n):
                if positive(n):
                    sp.wait_ge(x4_ready, n)
                sp.dma_start(xin[:, :, :], unit(x3_dram, c, g)).then_inc(x3_load, 16)
                for i in range(c + 1):
                    sp.dma_start(xln[:, i, :, :], unit(xln_dram, i, g)).then_inc(xln_load, 16)
                unit_loads(1, c, g, n)
                sp.wait_ge(x6_ready, n + 1)
                sp.dma_start(unit(out, c, g), xres[:, :, :]).then_inc(o_store, 16)

            for c in range(NC_):
                chunk_units(sp, c, layer1)
            sp.wait_ge(o_store, 16 * NC_ * NG)

        def ln_dve(dve, s, n, src, used=None, used_at=0, rms=False):
            k = 9 if rms else 3
            for b in range(GB):
                i = dve.bn_stats(s.stats[:, b, :], src[:, b, :])
            i.then_inc(s.small, 1)
            dve.wait_ge(s.small, k * n + 1)
            dve.memset(s.tmp[:, 0, 0:1], 0.0)
            for b in range(GB):
                i = dve.bn_aggr(s.mv[:, b, :], s.stats[:, b, :])
            i.then_inc(s.small, 1)
            dve.wait_ge(s.small, k * n + 2)
            dve.tensor_scalar(s.ve[:, 0, :], s.mv[:, :, 1], EPS, None, ALU.add).then_inc(s.small, 1)
            dve.wait_ge(s.inv, (2 if rms else 1) * n + 1)
            scale = s.rstd[:, 0, :]
            if rms:
                dve.tensor_tensor(s.tmp[:, 0, :], s.rstd[:, 0, :], s.rstd[:, 0, :], ALU.mult).then_inc(s.small, 1)
                dve.wait_ge(s.small, k * n + 4)
                dve.tensor_tensor(s.tmp[:, 1, :], s.tmp[:, 0, :], s.mv[:, :, 1], ALU.mult).then_inc(s.small, 1)
                dve.wait_ge(s.small, k * n + 5)
                dve.tensor_scalar(s.ve[:, 1, :], s.tmp[:, 1, :], EPS, None, ALU.add).then_inc(s.small, 1)
                dve.tensor_tensor(s.tmp[:, 2, :], s.mv[:, :, 0], s.rstd[:, 0, :], ALU.mult).then_inc(s.small, 1)
                dve.tensor_scalar(s.tmp[:, 0, :], s.rstd[:, 0, :], 1.0, None, ALU.add).then_inc(s.small, 1)
                dve.wait_ge(s.inv, 2 * n + 2)
                dve.tensor_tensor(s.tmp[:, 1, :], s.rstd[:, 0, :], s.rstd[:, 1, :], ALU.mult).then_inc(s.small, 1)
                dve.wait_ge(s.small, 9 * n + 9)
                scale = s.tmp[:, 1, :]
            if used is not None:
                if positive(used_at):
                    dve.wait_ge(used, used_at)
            for b in range(GB):
                i = dve.tensor_scalar(xnat[:, b, :], src[:, b, :], s.mv[:, b, 0:1], scale[:, b:b + 1],
                                      ALU.subtract, ALU.mult)
            i.then_inc(s.normed, 1)

        def ln_pool(pool, s, n, rms=False):
            pool.wait_ge(s.small, (9 if rms else 3) * n + 3)
            pool.tensor_tensor(s.rstd[:, 0, :], s.ve[:, 0, :], neghalf[:, :], ALU.pow).then_inc(s.inv, 1)
            if rms:
                pool.wait_ge(s.small, 9 * n + 6)
                pool.tensor_tensor(s.rstd[:, 1, :], s.ve[:, 1, :], neghalf[:, :], ALU.pow).then_inc(s.inv, 1)

        def turn_pe(pe, src, ready, ready_at, done, free, free_at):
            pe.wait_ge(ready, ready_at)
            for h, bank in enumerate((pb, pc)):
                if free is not None:
                    if positive(free_at[h]):
                        pe.wait_ge(free[h], free_at[h])
                for b in range(GB):
                    i = pe.transpose(bank[:, b * P:(b + 1) * P], src[:, b, h * P:(h + 1) * P], ident[:, :])
                i.then_inc(done, 1)

        def turn_act(act, n, turned, landed, dst):
            for h, bank in enumerate((pb, pc)):
                act.wait_ge(turned, 2 * n + h + 1)
                act.activation(dst[:, h, :], bank[:, :], ACT.Identity).then_inc(landed, 1)

        def project_nat(pe, act_t, w, done, start=True, stop=True):
            for b in range(GB):
                for k in range(NH):
                    i = pe.matmul(pa[:, b * D:(b + 1) * D], act_t[:, k, b * P:(b + 1) * P], w[:, k, :],
                                  start=(k == 0), stop=(k == NH - 1))
            i.then_inc(done, 1)

        def attn_pe(pe, t, l, n, s):
            pe.wait_ge(s.landed, 2 * n + 2)
            for m in range(NH):
                for k in range(NH):
                    i = pe.matmul(pa[:, m * NT:(m + 1) * NT], wQ[l][:, k, m * P:(m + 1) * P], xT[:, k, :],
                                  start=(k == 0), stop=(k == NH - 1))
                i.then_inc(t.q, 1)
            pe.wait_ge(t.q_ready, 2 * n + 2)
            pe.wait_ge(t.v_load, 16 * n + 16)

            def scores(b):
                pe.wait_ge(t.kbd, GB * n + b + 1)
                if b:
                    if positive(GB * n + b):
                        pe.wait_ge(t.masked, GB * n + b)
                for h in range(NH):
                    i = pe.matmul(pa[:, h * NT:(h + 1) * NT], qT[:, h, b * P:(b + 1) * P],
                                  kbd[b % 2][:, h, :, :].rearrange("p a k -> p (a k)"), start=True, stop=True)
                i.then_inc(t.scores, 1)

            scores(0)
            for b in range(GB):
                if b + 1 < GB:
                    scores(b + 1)
                pe.wait_ge(t.exped if l == 0 else t.gated, GB * n + b + 1)
                for j in range(2):
                    if b or j:
                        if positive(2 * (GB * n + b) + j):
                            pe.wait_ge(t.exT, 2 * (GB * n + b) + j)
                    for p in range(4):
                        src = ex[b % 2][:, 8 * j + 2 * p:8 * j + 2 * p + 2, :].rearrange("p a k -> p (a k)")
                        i = pe.transpose(pb[:, p * P:(p + 1) * P], src, ident[:, :])
                    i.then_inc(t.turned, 1)
                if b:
                    if positive(GB * n + b):
                        pe.wait_ge(t.o, GB * n + b)
                for j in range(2):
                    pe.wait_ge(t.exT, 2 * (GB * n + b) + j + 1)
                    for p in range(4):
                        q = 4 * j + p
                        i = pe.matmul(pc[:, q * VW:(q + 1) * VW], exT[:, j, p, :], vg[:, b, q * VW:(q + 1) * VW],
                                      start=True, stop=True)
                i.then_inc(t.pv, 1)
            turn_pe(pe, onat, t.o, GB * n + GB, t.o_turned, None, None)
            pe.wait_ge(t.oT, 2 * n + 2)
            pe.wait_ge(t.masked, GB * n + GB)
            project_nat(pe, xT, wO[l], t.proj)

        def attn_act(act, t, l, n):
            for m in range(NH):
                act.wait_ge(t.q, 2 * n + m + 1)
                act.activation(qT[:, m, :], pa[:, m * NT:(m + 1) * NT], ACT.Identity,
                               bias=biasQ[l][:, m:m + 1], scale=0.25).then_inc(t.q_ready, 1)

            def exp(b):
                act.wait_ge(t.shifted, GB * n + b + 1)
                act.activation(ex[b % 2][:, :, :], ex[b % 2][:, :, :], ACT.Exp).then_inc(t.exped, 1)

            exp(0)
            for b in range(GB):
                if b + 1 < GB and l == 0:
                    exp(b + 1)
                for j in range(2):
                    act.wait_ge(t.turned, 2 * (GB * n + b) + j + 1)
                    if b:
                        if positive(GB * n + b):
                            act.wait_ge(t.pv, GB * n + b)
                    act.activation(exT[:, j, :, :], pb[:, :].rearrange("p (a t) -> p a t", a=4),
                                   ACT.Identity).then_inc(t.exT, 1)
                if b + 1 < GB and l == 1:
                    exp(b + 1)
            turn_act(act, n, t.o_turned, t.oT, xT)

        def attn_dve(dve, t, l, n):
            if l == 0:
                dve.wait_ge(t.m_load, 16 * n + 16)
                if positive(GB * n):
                    dve.wait_ge(t.masked, GB * n)
                dve.tensor_scalar(neg[:, :, :], mask8[:, :, :], 1.0, FMAX, ALU.subtract, ALU.mult).then_inc(t.neg, 1)
            else:
                dve.wait_ge(t.m_load, 32 * n + 32)
                dve.tensor_scalar(neg[:, :, :], mask32[:, :, :], 1.0, 1e9, ALU.subtract, ALU.mult).then_inc(t.neg, 1)
            dve.wait_ge(t.neg, n + 1)

            def mask_and_max(b):
                dve.wait_ge(t.scores, GB * n + b + 1)
                if positive(max(0, 2 * (b - 1)) + 2 * GB * n):
                    dve.wait_ge(t.turned, max(0, 2 * (b - 1)) + 2 * GB * n)
                dve.tensor_tensor(ex[b % 2][:, :, :], pa[:, :].rearrange("p (a k) -> p a k", a=H),
                                  neg[:, b:b + 1, :].broadcast_to([P, H, SK]), ALU.add).then_inc(t.masked, 1)
                dve.wait_ge(t.masked, GB * n + b + 1)
                if positive(GB * n + b):
                    dve.wait_ge(t.shifted, GB * n + b)
                dve.tensor_reduce(mx[:, :], ex[b % 2][:, :, :], AX_X, ALU.max).then_inc(t.top, 1)

            mask_and_max(0)
            for b in range(GB):
                if l == 1:
                    dve.wait_ge(t.exped, GB * n + b + 1)
                    if positive(GB * n + b):
                        dve.wait_ge(t.inv, GB * n + b)
                    dve.tensor_reduce(mx2[:, :], ex[b % 2][:, :, :], AX_X, ALU.add).then_inc(t.summed, 1)
                    dve.wait_ge(t.summed, GB * n + b + 1)
                    if positive(GB * n + b):
                        dve.wait_ge(t.o, GB * n + b)
                    dve.reciprocal(rs[:, :], mx2[:, :]).then_inc(t.inv, 1)
                if b + 1 < GB:
                    mask_and_max(b + 1)
                dve.wait_ge(t.pv, GB * n + b + 1)
                o = pc[:, 0:NP * VW].rearrange("p (q w) -> p q w", w=VW)
                if l == 0:
                    if positive(GB * n + b):
                        dve.wait_ge(t.o, GB * n + b)
                    dve.reciprocal(rs[:, :].rearrange("p (q e) -> p q e", e=2), o[:, :, 2 * HD:VW]).then_inc(t.inv, 1)
                dve.wait_ge(t.inv, GB * n + b + 1)
                if positive(2 * n):
                    dve.wait_ge(t.o_turned, 2 * n)
                for e in range(2):
                    i = dve.tensor_tensor(
                        onat[:, b, :].rearrange("p (q e w) -> p q e w", e=2, w=HD)[:, :, e, :],
                        o[:, :, e * HD:(e + 1) * HD],
                        rs[:, e::2].rearrange("p (q o) -> p q o", o=1).broadcast_to([P, NP, HD]), ALU.mult)
                i.then_inc(t.o, 1)

        def attn_pool(pool, t, l, n, g, row):
            def keys(b):
                if b >= 2:
                    if positive(GB * n + b - 1):
                        pool.wait_ge(t.scores, GB * n + b - 1)
                else:
                    if positive(GB * n):
                        pool.wait_ge(t.scores, GB * n)
                for h in range(NH):
                    i = pool.tensor_tensor(
                        kbd[b % 2][:, h, :, :], KT[l][:, h, bass.ds(GB * g + b, 1), :].broadcast_to([P, NE, SK]),
                        headmask[:, :].rearrange("p (a o) -> p a o", o=1).broadcast_to([P, NE, SK]), ALU.mult)
                i.then_inc(t.kbd, 1)

            keys(0)
            keys(1)
            for b in range(GB):
                pool.wait_ge(t.top, GB * n + b + 1)
                pool.tensor_tensor(ex[b % 2][:, :, :], ex[b % 2][:, :, :],
                                   mx[:, :].rearrange("p (a o) -> p a o", o=1).broadcast_to([P, H, SK]),
                                   ALU.subtract).then_inc(t.shifted, 1)
                if b + 2 < GB:
                    keys(b + 2)
                if l == 1:
                    pool.wait_ge(t.summed, GB * n + b + 1)
                    pool.tensor_tensor(ex[b % 2][:, :, :], ex[b % 2][:, :, :],
                                       gp[:, b:b + 1, :].broadcast_to([P, H, SK]), ALU.mult).then_inc(t.gated, 1)
            add_row(pool, row, t.base)

        def add_row(pool, row, done):
            pool.tensor_tensor(xres[:, :, :], xres[:, :, :],
                               row[:, :].rearrange("p (o d) -> p o d", o=1).broadcast_to([P, GB, D]),
                               ALU.add).then_inc(done, 1)

        def add_psum(dve, done):
            dve.tensor_tensor(xres[:, :, :], pa[:, :].rearrange("p (b d) -> p b d", b=GB), xres[:, :, :],
                              ALU.add).then_inc(done, 1)

        mx2 = sb("mx2", [P, H])

        @block.tensor
        def _(pe):
            pe.wait_ge(w_load, NLOAD)
            for h in range(NH):
                i = pe.matmul(pa[:, h * D:(h + 1) * D], onat[0:32, 3, h * P:(h + 1) * P], onat[0:32, 2, :],
                              start=True, stop=True)
            i.then_inc(wf_pe, 1)
            k_w, v_w = (xin[:, 0:2, :], xres[:, 0:2, :]), (xin[:, 2:4, :], xres[:, 2:4, :])
            n = 0
            for l in range(2):
                for m in range(NH):
                    for j in range(2):
                        bank = (pb, pc)[n % 2]
                        if n >= 2:
                            pe.wait_ge(prep_ev, n - 1)
                        for k in range(NH):
                            i = pe.matmul(bank[:, :], k_w[l][:, k, m * P:(m + 1) * P],
                                          ctxA[:, k, 8 * j:8 * j + 8, :].rearrange("p b k -> p (b k)"),
                                          start=(k == 0), stop=(k == NH - 1))
                        i.then_inc(prep_pe, 1)
                        n += 1
            pe.wait_ge(prep_ev, n)
            for l in range(2):
                for b in range(B):
                    v = l * B + b
                    if v >= 2:
                        pe.wait_ge(prep_v, 2 * v - 2)
                    for e in range(2):
                        for k in range(NH):
                            i = pe.matmul((pb, pc)[v % 2][64 * e:64 * e + 64, 0:D], ctxA[:, k, b, :], v_w[l][:, k, :],
                                          start=(k == 0), stop=(k == NH - 1))
                    i.then_inc(prep_pe, 1)
            pe.wait_ge(prep_v, 4 * B)
            pe.wait_ge(prep_done, 1)

            def layer0(c, g, n):
                s = ln[0]
                turn_pe(pe, xnat, s.normed, n + 1, s.turned, (xg_ready, ln[3].landed), (n, 2 * n))
                pe.wait_ge(s.landed, 2 * n + 2)
                for m in range(NH):
                    for j, (w, bank) in enumerate(((wD, pa[:, 0:NT]), (wB, pa[:, NT:2 * NT]), (wA, pb), (wC, pc))):
                        if m:
                            if j == 0:
                                pe.wait_ge(t_act, 6 * n + 1)
                            elif j == 1:
                                pe.wait_ge(u_ready, 2 * n + 1)
                            else:
                                if positive(6 * n + j):
                                    pe.wait_ge(t_act, 6 * n + j)
                        for k in range(NH):
                            i = pe.matmul(bank[:, 0:NT] if j > 1 else bank, w[:, k, m * P:(m + 1) * P], xT[:, k, :],
                                          start=(k == 0), stop=(k == NH - 1))
                        i.then_inc(p_ready, 1)
                pe.wait_ge(g_ready, n + 1)
                project_nat(pe, tC, wOut, y_ready)
                turn_pe(pe, xnat, ln[1].normed, n + 1, ln[1].turned, None, None)
                attn_pe(pe, at[0], 0, n, ln[1])
                turn_pe(pe, xnat, ln[2].normed, n + 1, ln[2].turned, None, None)
                pe.wait_ge(ln[2].landed, 2 * n + 2)
                project_nat(pe, xT, wF, f_proj)
                turn_pe(pe, xnat, ln[3].normed, n + 1, ln[3].turned, None, None)
                pe.wait_ge(ln[3].landed, 2 * n + 2)
                for k in range(NH):
                    i = pe.matmul(pb[0:96, :], wih[:, k, :], xT[:, k, :], start=(k == 0), stop=(k == NH - 1))
                i.then_inc(xg_pe, 1)

            for c in range(NC_):
                chunk_units(pe, c, layer0)

            def lstm(n):
                for s in range(STEPS):
                    if s % 8 == 0:
                        pe.wait_ge(l_in, 4 * n + s // 8 + 1)
                    pe.wait_ge(l_t, STEPS * n + s + 1)
                    pe.matmul(pg[0:B, 0:80], slots[:, s, :], wcat[:, :], start=True, stop=True).then_inc(l_pe, 1)

            lstm(0)
            with pe.Fori(1, NC_ * NG) as n:
                lstm(n)

            def layer1(c, g, n):
                pos0 = sum(range(1, c + 1)) * NG
                pe.wait_ge(l_out, 4 * NG * NC_)
                if positive(n):
                    pe.wait_ge(oh_ev, n)
                pe.matmul(pc[:, :], wms[:, :], R[:, bass.ds(GB * g, GB), c * P:(c + 1) * P],
                          start=True, stop=True).then_inc(z_pe, 1)
                pe.wait_ge(u_rows, 2 * n + 2)
                if positive(n):
                    pe.wait_ge(x6_ready, n)
                pe.wait_ge(xln_load, 16 * (pos0 + (c + 1) * (g + 1)))
                for i_ in range(c + 1):
                    t = pos0 + (c + 1) * g + i_
                    if positive(t):
                        pe.wait_ge(pos_sq, t)
                    pe.matmul(pb[:, :], posl[:, i_, :], urow[:, :], start=True, stop=True).then_inc(pos_pe, 1)
                    pe.wait_ge(pos_w2, t + 1)
                    for b in range(GB):
                        w_b = wT[:, b * P:(b + 1) * P]
                        pe.matmul(pa[:, b * D:(b + 1) * D], w_b, xln[:, i_, b, :],
                                  start=(i_ == 0 and b % 2 == 0), stop=(i_ == c), skip_group_check=True)
                    for b in range(GB):
                        i = pe.matmul(pc[:, b:b + 1], wsq[:, b * P:(b + 1) * P], ones[:, :],
                                      start=(i_ == 0 and b == 0), stop=(i_ == c), skip_group_check=True)
                    i.then_inc(ctx_pe, 1)
                pe.wait_ge(n_a, n + 1)
                turn_pe(pe, xnat, ln[4].normed, n + 1, ln[4].turned, None, None)
                attn_pe(pe, at[1], 1, n, ln[4])
                turn_pe(pe, xnat, ln[5].normed, n + 1, ln[5].turned, None, None)
                pe.wait_ge(ln[5].landed, 2 * n + 2)
                for b in range(GB):
                    for k in range(NH):
                        i = pe.matmul(pc[:, b * NE:(b + 1) * NE], xT[:, k, b * P:(b + 1) * P], wR[:, k, :],
                                      start=(k == 0), stop=(k == NH - 1))
                i.then_inc(r_pe, 1)
                pe.wait_ge(r_oh, n + 1)
                for b in range(GB):
                    i = pe.transpose(pb[0:NE, b * P:(b + 1) * P], lg[:, 3, b, :], ident[:, :])
                i.then_inc(oh_pe, 1)
                pe.wait_ge(oh_ev, n + 1)

                def expert_in(e):
                    if e:
                        if positive(NE * n + e):
                            pe.wait_ge(fc_sum, NE * n + e)
                    for k in range(NH):
                        i = pe.matmul(pb[:, :], wfc[:, k, e * P:(e + 1) * P], xT[:, k, :],
                                      start=(k == 0), stop=(k == NH - 1))
                    i.then_inc(fc_pe, 1)
                    if e:
                        if positive(NE * n + e):
                            pe.wait_ge(fc_mask, NE * n + e)
                    pe.matmul(pc[:, :], sel[:, e, :], ohT[:, :], start=True, stop=True).then_inc(sel_pe, 1)

                expert_in(0)
                for e in range(NE):
                    if e + 1 < NE:
                        expert_in(e + 1)
                    pe.wait_ge(fc_sq, NE * n + e + 1)
                    for b in range(GB):
                        i = pe.matmul(pa[:, b * D:(b + 1) * D], hq[e % 2][:, b * P:(b + 1) * P], wpj[:, e, :],
                                      start=(e == 0 and b % 2 == 0), stop=(e == NE - 1), skip_group_check=True)
                    i.then_inc(moe_pe, 1)

            for c in range(NC_):
                chunk_units(pe, c, layer1)

        @block.scalar
        def _(act):
            act.wait_ge(w_load, NLOAD)
            n = 0
            for l in range(2):
                for m in range(NH):
                    for j in range(2):
                        act.wait_ge(prep_pe, n + 1)
                        act.activation(KT[l][:, m, 8 * j:8 * j + 8, :].rearrange("p b k -> p (b k)"),
                                       (pb, pc)[n % 2][:, :], ACT.Identity,
                                       bias=biasK[l][:, m:m + 1]).then_inc(prep_ev, 1)
                        n += 1
            act.wait_ge(prep_done, 1)
            def layer0(c, g, n):
                turn_act(act, n, ln[0].turned, ln[0].landed, xT)
                for m in range(NH):
                    act.wait_ge(p_ready, 8 * n + 4 * m + 1)
                    if m:
                        act.wait_ge(u_ready, 2 * n + 1)
                    act.activation(tD[:, :], pa[:, 0:NT], ACT.Tanh, scale=0.5).then_inc(t_act, 1)
                    act.wait_ge(p_ready, 8 * n + 4 * m + 3)
                    act.activation(sA[:, GB * m:GB * m + GB, 1:P + 1], pb[:, :].rearrange("p (b t) -> p b t", b=GB),
                                   ACT.Tanh, bias=biasA[:, m:m + 1], scale=0.5).then_inc(t_act, 1)
                    act.wait_ge(p_ready, 8 * n + 4 * m + 4)
                    act.activation(tC[:, m, :], pc[:, :], ACT.Tanh, scale=0.5).then_inc(t_act, 1)
                turn_act(act, n, ln[1].turned, ln[1].landed, xT)
                attn_act(act, at[0], 0, n)
                turn_act(act, n, ln[2].turned, ln[2].landed, xT)
                turn_act(act, n, ln[3].turned, ln[3].landed, xT)
                act.wait_ge(xg_pe, n + 1)
                act.activation(R[0:96, bass.ds(GB * g, GB), c * P:(c + 1) * P],
                               pb[0:96, :].rearrange("p (b t) -> p b t", b=GB), ACT.Identity,
                               bias=biasG[:, 0:1]).then_inc(xg_ready, 1)

            for c in range(NC_):
                chunk_units(act, c, layer0)

            def lstm(n):
                for s in range(STEPS):
                    k = STEPS * n + s
                    act.wait_ge(l_pe, k + 1)
                    if positive(k):
                        act.wait_ge(l_h, k)
                    act.activation(gates[:, 0:80], pg[0:B, 0:80], ACT.Tanh).then_inc(l_tanh, 1)
                    act.wait_ge(l_c, k + 1)
                    act.activation(tcell[:, :], gates[:, 80:100], ACT.Tanh, scale=0.5).then_inc(l_tc, 1)

            lstm(0)
            with act.Fori(1, NC_ * NG) as n:
                lstm(n)

            def layer1(c, g, n):
                pos0 = sum(range(1, c + 1)) * NG
                act.wait_ge(z_pe, n + 1)
                act.activation(zrow[:, 4, :], pc[96:97, :], ACT.Exp, scale=-1.0).then_inc(z_exp, 1)
                for i_ in range(c + 1):
                    t = pos0 + (c + 1) * g + i_
                    act.wait_ge(pos_pe, t + 1)
                    if positive(t):
                        act.wait_ge(ctx_pe, t)
                    act.activation(wT[:, :], pb[:, :], ACT.Square).then_inc(pos_sq, 1)
                    act.wait_ge(pos_sq, t + 1)
                    act.activation(wT[:, :], wT[:, :], ACT.Exp, scale=-1.0).then_inc(pos_w, 1)
                turn_act(act, n, ln[4].turned, ln[4].landed, xT)
                attn_act(act, at[1], 1, n)
                turn_act(act, n, ln[5].turned, ln[5].landed, xT)
                act.wait_ge(r_small, 4 * n + 2)
                act.activation(lg[:, 1, :, :], lg[:, 0, :, :], ACT.Exp).then_inc(r_exp, 1)
                act.wait_ge(oh_pe, n + 1)
                act.activation(ohT[:, :], pb[0:NE, :], ACT.Identity).then_inc(oh_ev, 1)
                for e in range(NE):
                    k = NE * n + e
                    act.wait_ge(fc_pe, k + 1)
                    if positive(k):
                        act.wait_ge(fc_sum, k)
                    act.activation(hr, pb[:, :], ACT.Relu).then_inc(fc_relu, 1)
                    act.wait_ge(fc_mask, k + 1)
                    if e >= 2:
                        if positive(k - 1):
                            act.wait_ge(moe_pe, k - 1)
                    act.activation(hq[e % 2], hm2, ACT.Square).then_inc(fc_sq, 1)

            for c in range(NC_):
                chunk_units(act, c, layer1)

        @block.vector
        def _(dve):
            dve.memset(wcat[:, :], 0.0).then_inc(prep_in, 1)
            dve.memset(wms[:, :], 0.0)
            dve.memset(neghalf[:, :], -0.5)
            dve.memset(ones[:, :], 1.0)
            dve.memset(sA[:, :, 0:1], 0.0)
            dve.memset(carry[:, :, :], 0.0)
            dve.memset(mcarry[:, :], 0.0)
            dve.memset(mrow[:, 0, :], 0.0)
            dve.memset(urow[:, :], 0.0)
            dve.memset(hnew[:, :], 0.0)
            dve.memset(gates[:, :], 0.0)
            dve.memset(slots[:, :, :], 0.0)
            dve.memset(R[64:128, :, :], 0.0)
            dve.memset(vg[:, :, :], 0.0).then_inc(prep_in, 1)
            dve.wait_ge(prep_in, 2)
            for b in range(GB):
                vb = vg[:, b, :].rearrange("p (q w) -> p q w", w=VW)
                dve.memset(vb[0:64, :, 2 * HD:2 * HD + 1], 1.0)
                i = dve.memset(vb[64:128, :, 2 * HD + 1:VW], 1.0)
            i.then_inc(prep_in, 1)
            dve.wait_ge(w_load, NLOAD)
            for w in (wA, wB, wC, wD):
                for h in range(NH):
                    dve.tensor_scalar(w[:, h, :], w[:, h, :], normw[:, h:h + 1], None, ALU.mult)
            dve.tensor_scalar(wOut[:, :, :], wOut[:, :, :], 0.25, None, ALU.mult)
            dve.tensor_copy(sel[:, :, :], sel32[:, :, :])
            dve.tensor_scalar(biasA[:, :], biasA[:, :], 0.5, None, ALU.mult)
            dve.tensor_scalar(biasQ[0][:, :], biasQ[0][:, :], 0.25, None, ALU.mult)
            dve.tensor_scalar(biasQ[1][:, :], biasQ[1][:, :], 0.25, None, ALU.mult)
            dve.tensor_scalar(wcat[96:128, 0:60], wcat[96:128, 0:60], 0.25, None, ALU.mult)
            dve.tensor_scalar(wcat[96:128, 60:80], wcat[96:128, 60:80], 0.5, None, ALU.mult)
            dve.tensor_scalar(wms[96:128, :], wms[96:128, :], 0.5, None, ALU.mult)
            dve.tensor_scalar(wpj[:, :, :], wpj[:, :, :], 0.25, None, ALU.mult)
            dve.tensor_tensor(biasG[:, 0:1], biasG[:, 0:1], biasG[:, 1:2], ALU.add)
            dve.wait_ge(wf_pe, 1)
            dve.tensor_tensor(wF[:, :, :], pa[:, 0:NH * D].rearrange("p (h n) -> p h n", h=NH), wF[:, :, :],
                              ALU.add).then_inc(wf_ev, 1)
            for l in range(2):
                for b in range(B):
                    v = l * B + b
                    dve.wait_ge(prep_pe, 8 + v + 1)
                    if v >= GB:
                        if positive(16 * (v // GB)):
                            dve.wait_ge(v_store[v % GB], 16 * (v // GB))
                    vb = vg[:, v % GB, :].rearrange("p (q w) -> p q w", w=VW)
                    bank = (pb, pc)[v % 2]
                    for e in range(2):
                        r = slice(64 * e, 64 * e + 64)
                        dve.tensor_tensor(
                            vb[r, :, e * HD:(e + 1) * HD],
                            bank[r, 0:D].rearrange("p (q e w) -> p q e w", e=2, w=HD)[:, :, e, :],
                            onat[r, l, :].rearrange("p (q e w) -> p q e w", e=2, w=HD)[:, :, e, :],
                            ALU.add).then_inc(prep_v, 1)
            dve.wait_ge(prep_ev, 8)
            dve.wait_ge(prep_v, 4 * B)
            dve.wait_ge(wf_ev, 1)
            dve.memset(mx2[:, :], 0.0).then_inc(prep_done, 1)

            def layer0(c, g, n):
                s = ln[0]
                dve.wait_ge(x_load, 16 * n + 16)
                if positive(16 * n):
                    dve.wait_ge(xln_store, 16 * n)
                ln_dve(dve, s, n, xin, ln[3].turned, 2 * n, rms=True)
                dve.wait_ge(s.small, 9 * n + 9)
                if positive(16 * n):
                    dve.wait_ge(x3_store, 16 * n)
                for b in range(GB):
                    i = dve.tensor_scalar(xres[:, b, :], xin[:, b, :], s.tmp[:, 0, b:b + 1], s.tmp[:, 2, b:b + 1],
                                          ALU.mult, ALU.subtract)
                i.then_inc(base_ready, 1)
                if positive(n):
                    dve.wait_ge(s_scan, n)
                for m in range(NH):
                    i = dve.tensor_scalar(sU[:, GB * m:GB * m + GB, 0:1],
                                          carry[:, m, bass.ds(GB * g, GB)].rearrange("p (b o) -> p b o", o=1),
                                          1.0, None, ALU.mult)
                i.then_inc(s_carry, 1)
                for m in range(NH):
                    dve.wait_ge(p_ready, 8 * n + 4 * m + 2)
                    dve.wait_ge(t_act, 6 * n + 3 * m + 1)
                    dve.scalar_tensor_tensor(
                        sU[:, GB * m:GB * m + GB, 1:P + 1], tD[:, :].rearrange("p (b t) -> p b t", b=GB), 1.0,
                        pa[:, NT:2 * NT].rearrange("p (b t) -> p b t", b=GB), ALU.add, ALU.mult).then_inc(u_ready, 1)
                    dve.wait_ge(t_act, 6 * n + 3 * m + 2)
                    dve.tensor_scalar(sA[:, GB * m:GB * m + GB, 1:P + 1], sA[:, GB * m:GB * m + GB, 1:P + 1],
                                      0.5, 0.5, ALU.mult, ALU.add).then_inc(a_ready, 1)
                dve.wait_ge(a_ready, 2 * n + 2)
                dve.wait_ge(u_ready, 2 * n + 2)
                dve.wait_ge(s_carry, n + 1)
                dve.tensor_tensor_scan(sH[:, :, :].rearrange("p a t -> p (a t)"), sA[:, :, :].rearrange("p a t -> p (a t)"),
                                       sU[:, :, :].rearrange("p a t -> p (a t)"), 0.0, ALU.mult, ALU.add).then_inc(c_ready, 1)
                dve.wait_ge(c_ready, n + 1)
                for m in range(NH):
                    i = dve.tensor_scalar(carry[:, m, bass.ds(GB * g, GB)].rearrange("p (b o) -> p b o", o=1),
                                          sH[:, GB * m:GB * m + GB, P:P + 1], 1.0, None, ALU.mult)
                i.then_inc(s_scan, 1)
                dve.wait_ge(t_act, 6 * n + 6)
                for m in range(NH):
                    i = dve.scalar_tensor_tensor(
                        tC[:, m, :].rearrange("p (b t) -> p b t", b=GB), tC[:, m, :].rearrange("p (b t) -> p b t", b=GB),
                        1.0, sH[:, GB * m:GB * m + GB, 1:P + 1], ALU.add, ALU.mult)
                i.then_inc(g_ready, 1)
                dve.wait_ge(y_ready, n + 1)
                dve.wait_ge(f_base, 2 * n + 1)
                add_psum(dve, x1_ready)
                dve.wait_ge(x1_ready, n + 1)
                ln_dve(dve, ln[1], n, xres)
                attn_dve(dve, at[0], 0, n)
                dve.wait_ge(at[0].proj, n + 1)
                dve.wait_ge(at[0].base, n + 1)
                add_psum(dve, at[0].done)
                dve.wait_ge(at[0].done, n + 1)
                ln_dve(dve, ln[2], n, xres)
                dve.wait_ge(f_proj, n + 1)
                dve.wait_ge(f_base, 2 * n + 2)
                add_psum(dve, x3_ready)
                dve.wait_ge(x3_ready, n + 1)
                ln_dve(dve, ln[3], n, xres)

            for c in range(NC_):
                chunk_units(dve, c, layer0)

            dve.wait_ge(xg_ready, NC_ * NG)
            dve.transpose(slots[96:128, 0:2, :].rearrange("p s b -> p (s b)"), hnew[:, :]).then_inc(l_t, 1)
            def lstm(n):
                for s in range(STEPS):
                    k = STEPS * n + s
                    dve.wait_ge(l_tanh, k + 1)
                    dve.scalar_tensor_tensor(uprod[:, :], gates[:, 0:40], 1.0, gates[:, 60:100], ALU.add, ALU.mult).then_inc(l_u, 1)
                    dve.wait_ge(l_u, k + 1)
                    dve.scalar_tensor_tensor(gates[:, 80:100], uprod[:, 20:40], 0.5, uprod[:, 0:20], ALU.mult,
                                             ALU.add).then_inc(l_c, 1)
                    dve.wait_ge(l_tc, k + 1)
                    dve.scalar_tensor_tensor(hnew[0:B, 0:PE_], gates[:, 40:60], 1.0, tcell[:, :], ALU.add,
                                             ALU.mult).then_inc(l_h, 1)
                    dve.wait_ge(l_h, k + 1)
                    if s == STEPS - 1:
                        dve.transpose(slots[96:128, 0:2, :].rearrange("p s b -> p (s b)"), hnew[:, :])
                    if s in (0, 8, 16, 24):
                        if positive(4 * n + s // 8):
                            dve.wait_ge(l_out, 4 * n + s // 8)
                    dve.transpose(slots[96:128, s + 1:s + 3, :].rearrange("p s b -> p (s b)"), hnew[:, :]).then_inc(l_t, 1)

            lstm(0)
            with dve.Fori(1, NC_ * NG) as n:
                lstm(n)

            def layer1(c, g, n):
                pos0 = sum(range(1, c + 1)) * NG
                dve.wait_ge(z_pe, n + 1)
                m3 = lambda j: mrow[:, j, :].rearrange("p (b t) -> p b t", b=GB)
                z3 = lambda j: zrow[:, j, :].rearrange("p (b t) -> p b t", b=GB)
                J = jrow[:, 0:1, c * P:(c + 1) * P].broadcast_to([1, GB, P])
                RJ = jrow[:, 1:2, c * P:(c + 1) * P].broadcast_to([1, GB, P])
                dve.tensor_scalar(m3(0)[:, :, 1:P + 1], pc[0:1, :].rearrange("p (b t) -> p b t", b=GB), 0.0, None, ALU.max)
                dve.tensor_copy(m3(1)[:, :, 0:1], mcarry[:, bass.ds(GB * g, GB)].rearrange("p (b o) -> p b o", o=1))
                dve.tensor_scalar(zrow[:, 1, :], pc[32:33, :], 0.0, 1.0 / S, ALU.max, ALU.mult)
                dve.tensor_scalar(zrow[:, 2, :], pc[64:65, :], 0.0, None, ALU.max).then_inc(z_small, 1)
                dve.wait_ge(z_small, 5 * n + 1)
                dve.tensor_tensor(z3(3), z3(2), J, ALU.mult).then_inc(z_small, 1)
                dve.wait_ge(z_small, 5 * n + 2)
                dve.tensor_tensor(m3(1)[:, :, 1:P + 1], z3(1), z3(3), ALU.add).then_inc(z_small, 1)
                dve.wait_ge(z_small, 5 * n + 3)
                dve.tensor_tensor_scan(mrow[:, 2, :], mrow[:, 0, :], mrow[:, 1, :], 0.0, ALU.mult, ALU.add).then_inc(z_small, 1)
                dve.wait_ge(z_exp, n + 1)
                dve.tensor_scalar(zrow[:, 0, :], zrow[:, 4, :], 1.0, 0.5 ** 0.5, ALU.add, ALU.mult).then_inc(z_small, 1)
                dve.wait_ge(z_small, 5 * n + 4)
                dve.tensor_scalar(mcarry[:, bass.ds(GB * g, GB)].rearrange("p (b o) -> p b o", o=1), m3(2)[:, :, P:P + 1],
                                  1.0, None, ALU.mult)
                dve.wait_ge(z_small, 5 * n + 5)
                if positive(pos0 + (c + 1) * g):
                    dve.wait_ge(pos_pe, pos0 + (c + 1) * g)
                dve.tensor_tensor(urow[0:1, :].rearrange("p (b t) -> p b t", b=GB), z3(0), RJ, ALU.mult).then_inc(u_rows, 1)
                dve.scalar_tensor_tensor(urow[32:33, :].rearrange("p (b t) -> p b t", b=GB), m3(2)[:, :, 1:P + 1], -1.0,
                                         z3(0), ALU.mult, ALU.mult).then_inc(u_rows, 1)
                dve.wait_ge(ctx_pe, pos0 + (c + 1) * (g + 1))
                dve.tensor_scalar(nrm[:, 0, :], pc[:, 0:GB], 1e-24, None, ALU.max).then_inc(n_a, 1)
                dve.wait_ge(n_b, n + 1)
                dve.wait_ge(x3_load, 16 * n + 16)
                if positive(16 * n):
                    dve.wait_ge(o_store, 16 * n)
                for b in range(GB):
                    i = dve.scalar_tensor_tensor(xres[:, b, :], pa[:, b * D:(b + 1) * D], nrm[:, 1, b:b + 1], xin[:, b, :],
                                                 ALU.mult, ALU.add)
                i.then_inc(x4_ready, 1)
                dve.wait_ge(x4_ready, n + 1)
                ln_dve(dve, ln[4], n, xres, ln[5].turned, 2 * n)
                attn_dve(dve, at[1], 1, n)
                dve.wait_ge(at[1].proj, n + 1)
                dve.wait_ge(at[1].base, n + 1)
                add_psum(dve, at[1].done)
                dve.wait_ge(at[1].done, n + 1)
                ln_dve(dve, ln[5], n, xres)
                dve.wait_ge(r_pe, n + 1)
                l3 = pc[:, 0:GB * NE].rearrange("p (b e) -> p b e", b=GB)
                bc = lambda t: t.rearrange("p (b o) -> p b o", o=1).broadcast_to([P, GB, NE])
                dve.tensor_reduce(lmx[:, 0, :], l3, AX_X, ALU.max).then_inc(r_small, 1)
                dve.wait_ge(r_small, 4 * n + 1)
                dve.tensor_tensor(lg[:, 0, :, :], l3, bc(lmx[:, 0, :]), ALU.subtract).then_inc(r_small, 1)
                dve.wait_ge(r_exp, n + 1)
                dve.scalar_tensor_tensor(lg[:, 2, :, :], lg[:, 1, :, :], 1.0,
                                         rank[:, :].rearrange("p (o e) -> p o e", o=1).broadcast_to([P, GB, NE]),
                                         ALU.is_ge, ALU.mult).then_inc(r_small, 1)
                dve.wait_ge(r_small, 4 * n + 3)
                dve.tensor_reduce(lmx[:, 1, :], lg[:, 2, :, :], AX_X, ALU.max).then_inc(r_small, 1)
                dve.wait_ge(r_small, 4 * n + 4)
                dve.tensor_tensor(lg[:, 3, :, :], lg[:, 2, :, :], bc(lmx[:, 1, :]), ALU.is_equal).then_inc(r_oh, 1)
                for e in range(NE):
                    k = NE * n + e
                    dve.wait_ge(fc_relu, k + 1)
                    if positive(k):
                        dve.wait_ge(fc_mask, k)
                    dve.tensor_tensor(hm, pb[:, :], hr, ALU.add).then_inc(fc_sum, 1)
                    dve.wait_ge(fc_sum, k + 1)
                    dve.wait_ge(sel_pe, k + 1)
                    if positive(k):
                        dve.wait_ge(fc_sq, k)
                    dve.tensor_tensor(hm2, pc[:, :], hm, ALU.mult).then_inc(fc_mask, 1)
                dve.wait_ge(moe_pe, NE * n + NE)
                add_psum(dve, x6_ready)

            for c in range(NC_):
                chunk_units(dve, c, layer1)

        @block.gpsimd
        def _(pool):
            pool.wait_ge(prep_done, 1)
            def layer0(c, g, n):
                ln_pool(pool, ln[0], n, rms=True)
                pool.wait_ge(base_ready, n + 1)
                add_row(pool, rowOut, f_base)
                ln_pool(pool, ln[1], n)
                attn_pool(pool, at[0], 0, n, g, rowO[0])
                ln_pool(pool, ln[2], n)
                pool.wait_ge(ln[2].normed, n + 1)
                add_row(pool, rowF, f_base)
                ln_pool(pool, ln[3], n)

            for c in range(NC_):
                chunk_units(pool, c, layer0)

            def lstm(n):
                for k in range(4):
                    if k == 0:
                        if positive(STEPS * n):
                            pool.wait_ge(l_pe, STEPS * n)
                    pool.tensor_copy(slots[0:96, 8 * k:8 * k + 8, :],
                                     R[0:96, :, bass.ds(STEPS * n + 8 * k, 8)].rearrange("p b t -> p t b")
                                     ).then_inc(l_in, 1)
                for k in range(4):
                    pool.wait_ge(l_t, STEPS * n + 8 * k + 9)
                    pool.tensor_copy(R[96:128, :, bass.ds(STEPS * n + 8 * k, 8)].rearrange("p b t -> p t b"),
                                     slots[96:128, 8 * k + 1:8 * k + 9, :]).then_inc(l_out, 1)

            lstm(0)
            with pool.Fori(1, NC_ * NG) as n:
                lstm(n)

            def layer1(c, g, n):
                pos0 = sum(range(1, c + 1)) * NG
                for i_ in range(c + 1):
                    t = pos0 + (c + 1) * g + i_
                    pool.wait_ge(pos_w, t + 1)
                    if i_ == c:
                        pool.tensor_tensor(wT[:, :].rearrange("p (b t) -> p b t", b=GB),
                                           wT[:, :].rearrange("p (b t) -> p b t", b=GB),
                                           tri[:, :].rearrange("p (o t) -> p o t", o=1).broadcast_to([P, GB, P]),
                                           ALU.mult).then_inc(pos_m, 1)
                        pool.wait_ge(pos_m, n + 1)
                    pool.tensor_tensor(wsq[:, :], wT[:, :], wT[:, :], ALU.mult).then_inc(pos_w2, 1)
                pool.wait_ge(n_a, n + 1)
                pool.tensor_tensor(nrm[:, 1, :], nrm[:, 0, :], neghalf[:, :], ALU.pow).then_inc(n_b, 1)
                ln_pool(pool, ln[4], n)
                attn_pool(pool, at[1], 1, n, g, rowO[1])
                ln_pool(pool, ln[5], n)

            for c in range(NC_):
                chunk_units(pool, c, layer1)


def _constants():
    import numpy as np
    p = np.arange(P)
    gatesel = np.zeros((80, 80), np.float32)
    for j in range(PE_):
        gatesel[j, j] = gatesel[20 + j, 20 + j] = gatesel[60 + j, 40 + j] = 0.5
        gatesel[40 + j, 60 + j] = 1.0
    posl = np.zeros((64, NC_, P), np.float32)
    posl[0] = np.arange(S).reshape(NC_, P)
    posl[32] = 1.0
    j = np.arange(1, S + 1, dtype=np.float32)
    sel = np.repeat(np.eye(NE, dtype=np.float32)[:, :, None], P, axis=2)
    return {
        "c_ident": np.eye(P, dtype=np.float32), "c_tri": (p[:, None] <= p[None, :]).astype(np.float32),
        "c_headmask": (p[:, None] // HD == np.arange(NE)[None, :]).astype(np.float32),
        "c_rank": np.tile(np.arange(NE, 0, -1, dtype=np.float32), (P, 1)),
        "c_sel": sel, "c_posl": posl, "c_jrow": np.stack([j / np.float32(S), np.float32(1.0) / j])[None],
        "c_gatesel": gatesel,
    }


def kernel(**inputs):
    import numpy as _np
    import concourse.bacc as _bacc
    from concourse import mybir as _mybir
    from concourse.bass_utils import run_bass_kernel_spmd as _run

    i = {k: _np.asarray(v) for k, v in inputs.items()}
    columns = lambda v: v.reshape(NH, P).T
    w_ih = _np.zeros((D, 96), _np.float32)
    w_ih[:, 0:80] = i["L1_attn_W_ih"].T
    w_hh = i["L1_attn_W_hh"].T[:, [*range(0, 40), *range(60, 80), *range(40, 60)]]
    b_gates = _np.zeros((96, 2), _np.float32)
    b_gates[0:80, 0], b_gates[0:80, 1], b_gates[80, 0] = i["L1_attn_b_ih"], i["L1_attn_b_hh"], 1.0
    w_mu_sig, b_mu_sig = _np.zeros((PE_, P), _np.float32), _np.zeros((1, P), _np.float32)
    w_mu_sig[:, 0:96:32], w_mu_sig[:, 96:97] = i["L1_attn_W_mu"].T, i["L1_attn_W_sig"].T
    b_mu_sig[0, 0:96:32], b_mu_sig[0, 96:97] = i["L1_attn_b_mu"], i["L1_attn_b_sig"]
    data = {
        "x": i["x"], "ctx": i["ctx_1024"].transpose(2, 0, 1), "fside": i["fside_BxSxS2_0"],
        "mask0": i["mask_BxSxS2_bf1"].view(_np.uint8), "mask1": i["mask_BxSxS2_ik1"],
        "norm_w": columns(i["L0_attn_norm_w"]), "A_w": i["L0_attn_A_w"].T, "A_b": columns(i["L0_attn_A_b"]), "B_w": i["L0_attn_B_w"].T,
        "C_w": i["L0_attn_C_w"].T, "D_w": i["L0_attn_D_w"].T, "out_w": i["L0_attn_out_w"].T, "out_b": i["L0_attn_out_b"],
        "Wq": i["L0_xattn_Wq"].T, "bq": columns(i["L0_xattn_bq"]), "Wk": i["L0_xattn_Wk"].T, "bk": columns(i["L0_xattn_bk"]),
        "Wv": i["L0_xattn_Wv"].T, "bv": i["L0_xattn_bv"], "Wo": i["L0_xattn_Wo"].T, "bo": i["L0_xattn_bo"],
        "W": i["L0_ffn_W"].T, "b": i["L0_ffn_b"], "V_r": i["L0_ffn_V_r"].T, "C": i["L0_ffn_C"].T,
        "W_ih": w_ih, "W_hh": w_hh, "b_gates": b_gates, "W_mu_sig": w_mu_sig, "b_mu_sig": b_mu_sig,
        "wq_k": i["L1_xattn_wq_k"], "wq_b": columns(i["L1_xattn_wq_b"]), "wk_k": i["L1_xattn_wk_k"], "wk_b": columns(i["L1_xattn_wk_b"]),
        "wv_k": i["L1_xattn_wv_k"], "wv_b": i["L1_xattn_wv_b"], "wo_k": i["L1_xattn_wo_k"], "wo_b": i["L1_xattn_wo_b"],
        "w_router": i["L1_ffn_w_router"].T,
        "w_fc": i["L1_ffn_w_fc"].transpose(2, 0, 1).reshape(D, NE * P),
        "w_proj": i["L1_ffn_w_proj"].transpose(2, 0, 1),
    }
    data.update(_constants())
    nc = _bacc.Bacc("TRN2", target_bir_lowering=False, num_devices=1)
    arrays, args = {}, {}
    for name, v in data.items():
        v = _np.ascontiguousarray(v)
        arrays[f"in_{name}"] = v
        args[name] = nc.dram_tensor(f"in_{name}", v.shape, _mybir.dt.from_np(v.dtype), kind="ExternalInput").ap()
    out = nc.dram_tensor("out_0", (B, S, D), F32, kind="ExternalOutput").ap()
    decoder_program(nc, args, out)
    r = _run(nc, [arrays], core_ids=[0])
    return r.results[0]["out_0"]
```

```python
from contextlib import ExitStack

import concourse.bass as bass
from concourse import mybir

ALU = mybir.AluOpType
ACT = mybir.ActivationFunctionType
F32 = mybir.dt.float32
BF16 = mybir.dt.bfloat16
AX_X = mybir.AxisListType.X

P = 128
B, S, D = 16, 512, 256
SK, H = 64, 16
GB = 4
NC_, NG = S // P, B // GB
NT = GB * P
NH = D // P
NP = H // 2
HD = D // H
PE_ = 20
NE = 8
STEPS = P // NG
EPS = 1e-5
FMAX = 3.4028234663852886e38
VW = 2 * HD + 2


class LayerNorm:

    def __init__(self, name, sb, sem):
        self.stats, self.mv = sb(f"{name}_stats", [P, GB, 6]), sb(f"{name}_mv", [P, GB, 2])
        self.ve, self.rstd = sb(f"{name}_ve", [P, 2, GB]), sb(f"{name}_rstd", [P, 2, GB])
        self.tmp = sb(f"{name}_tmp", [P, 3, GB])
        self.small, self.inv, self.normed = sem(f"{name}_small"), sem(f"{name}_inv"), sem(f"{name}_normed")
        self.turned, self.landed = sem(f"{name}_turned"), sem(f"{name}_landed")


class Attention:

    def __init__(self, name, sem):
        self.q, self.q_ready, self.kbd = sem(f"{name}_q"), sem(f"{name}_q_ready"), sem(f"{name}_kbd")
        self.scores, self.masked, self.top = sem(f"{name}_scores"), sem(f"{name}_masked"), sem(f"{name}_top")
        self.shifted, self.exped, self.summed = sem(f"{name}_shifted"), sem(f"{name}_exped"), sem(f"{name}_summed")
        self.gated, self.turned, self.exT = sem(f"{name}_gated"), sem(f"{name}_turned"), sem(f"{name}_exT")
        self.pv, self.inv, self.o = sem(f"{name}_pv"), sem(f"{name}_inv"), sem(f"{name}_o")
        self.o_turned, self.oT, self.proj = sem(f"{name}_o_turned"), sem(f"{name}_oT"), sem(f"{name}_proj")
        self.base, self.done, self.v_load = sem(f"{name}_base"), sem(f"{name}_done"), sem(f"{name}_v_load")
        self.m_load, self.neg = sem(f"{name}_m_load"), sem(f"{name}_neg")


class Tiles:

    def __init__(self, name, sb):
        self.xres, self.xnat = sb(f"{name}_xres", [P, GB, D]), sb(f"{name}_xnat", [P, GB, D])
        self.xT, self.qT = sb(f"{name}_xT", [P, NH, NT]), sb(f"{name}_qT", [P, NH, NT])
        self.kg = sb(f"{name}_kg", [P, NH, GB, SK])
        self.kbd = [sb(f"{name}_kbd{i}", [P, NH, NE, SK]) for i in range(2)]
        self.vg = sb(f"{name}_vg", [P, GB, NP * VW])
        self.scratch = sb(f"{name}_scratch", [P, 3 * NH * GB * (P + 1)])
        self.ex = [self.scratch[:, i * H * SK:(i + 1) * H * SK].rearrange("p (a k) -> p a k", a=H) for i in range(2)]
        self.exT = self.scratch[:, 2 * H * SK:3 * H * SK].rearrange("p (j a t) -> p j a t", j=2, a=4)
        self.mx, self.sums, self.rs = sb(f"{name}_mx", [P, 4, NE]), sb(f"{name}_sums", [P, 4, NE]), sb(f"{name}_rs", [P, 4, NE])
        self.neg = sb(f"{name}_neg", [P, GB, SK])


def positive(value):
    return not (isinstance(value, int) and value <= 0)


def norm_steps(k, after, rms=False):
    steps = [("dve", "stat", 2 * k + h, 0.9, after[h:h + 1]) for h in range(2)]
    steps += [("pool", "root", k, 1.0, [("stat", 2 * k + 1)])]
    if rms:
        steps += [("dve", "rms", 0, 0.6, [("root", k)]), ("pool", "root", 9, 1.0, [("rms", 0)])]
    steps += [("dve", "norm", 2 * k + h, 0.65, [("root", 9 if rms else k)]) for h in range(2)]
    steps += [("pe", "turn", 2 * k + h, 0.45, [("norm", 2 * k + h)]) for h in range(2)]
    steps += [("act", "land", 2 * k + h, 0.5, [("turn", 2 * k + 1)]) for h in range(2)]
    return steps


def attention_steps(l, k):
    steps = [("pe", "query", h, 1.7, [("land", 2 * k + 1)]) for h in range(2)]
    steps += [("act", "qland", h, 0.6, [("query", h)]) for h in range(2)]
    steps += [("dve", "neg", 0, 0.2, [])]
    for u in range(2 * GB):
        steps += [
            ("pool", "keys", u, 1.0, [("score", u - 4)]),
            ("pe", "score", u, 0.85, [("qland", u % 2), ("keys", u), ("mask", u - 2)]),
            ("dve", "mask", u, 0.65, [("score", u), ("neg", 0), ("pturn", u - 4)]),
            ("dve", "max", u, 0.65, [("mask", u)]),
            ("pool", "shift", u, 0.95, [("max", u)]),
            ("act", "exp", u, 0.5, [("shift", u)])]
        if l == 1:
            steps += [("dve", "sums", u, 0.75, [("exp", u), ("o", u - 4)]), ("pool", "gate", u, 1.15, [("sums", u)])]
        steps += [
            ("pe", "pturn", u, 0.45, [("gate" if l else "exp", u), ("pland" if l else "o", u - 1)]),
            ("act", "pland", u, 0.5, [("pturn", u), ("pv", u - 2)]),
            ("pe", "pv", u, 0.3, [("pland", u), ("o", u - 1)]),
            ("dve", "o", u, 0.45 if l else 0.6, [("pv", u)] + ([("sums", u)] if l else []))]
    steps += [("pool", "orow", 0, 2.3, [("shift", 7)])]
    steps += [("pe", "oturn", h, 0.45, [("o", 4 * h + 3), ("mask", 7)]) for h in range(2)]
    steps += [("act", "oland", h, 0.5, [("oturn", 1)]) for h in range(2)]
    steps += [("pe", "proj", h, 1.75, [("oland", 1)]) for h in range(2)]
    steps += [("dve", "add", h, 0.65, [("proj", h), ("orow", 0)]) for h in range(2)]
    return steps


def layer0_steps():
    steps = norm_steps(0, [], rms=True)
    steps += [("dve", "base", 0, 1.4, [("rms", 0)]), ("pool", "brow", 0, 2.3, [("base", 0)]),
              ("sp", "loadx", 0, 0.1, [("base", 0), ("norm", 1)]), ("dve", "carryin", 0, 0.3, [])]
    before = [[], [], [], [("tanh", 0)], [("u", 0)], [("tanh", 1)], [("tanh", 2)], [("tanh", 3)]]
    for m in range(NH):
        for j in range(4):
            steps += [("pe", "gate", 4 * m + j, 1.7, [("land", 1)] + before[4 * m + j])]
            if j != 1:
                steps += [("act", "tanh", 3 * m + max(j - 1, 0), 0.5, [("gate", 4 * m + j)])]
        steps += [("dve", "u", m, 0.65, [("tanh", 3 * m), ("gate", 4 * m + 1)]), ("dve", "a", m, 0.4, [("tanh", 3 * m + 1)])]
    steps += [("dve", "scan", 0, 1.6, [("a", 1), ("u", 1), ("carryin", 0)]), ("dve", "gated", 0, 1.3, [("scan", 0), ("tanh", 5)])]
    steps += [("pe", "out", h, 1.75, [("gated", 0)]) for h in range(2)]
    steps += [("dve", "x1", h, 0.65, [("out", h), ("brow", 0)]) for h in range(2)]
    steps += norm_steps(1, [("x1", 0), ("x1", 1)]) + attention_steps(0, 1)
    steps += [("sp", "loadc", 0, 0.1, [("pv", 7)])]
    steps += norm_steps(2, [("add", 0), ("add", 1)])
    steps += [("pool", "frow", 0, 2.3, [("norm", 5)])]
    steps += [("pe", "ffn", h, 1.75, [("land", 5)]) for h in range(2)]
    steps += [("dve", "x3", h, 0.65, [("ffn", h), ("frow", 0)]) for h in range(2)]
    steps += norm_steps(3, [("x3", 0), ("x3", 1)])
    steps += [("sp", "store", 0, 0.1, [("norm", 7)]),
              ("pe", "gatein", 0, 1.7, [("land", 7)]), ("act", "gatein", 1, 0.6, [("gatein", 0)])]
    return steps


def layer1_steps(c):
    steps = [("sp", "loadx3", 0, 0.1, []), ("pe", "rows", 0, 0.85, []), ("act", "rows", 1, 0.5, [("rows", 0)]),
             ("dve", "rows", 2, 2.8, [("rows", 0)]), ("dve", "rows", 3, 2.8, [("rows", 2), ("rows", 1)])]
    for i in range(c + 1):
        steps += [
            ("pe", "pos", i, 0.85, [("rows", 3), ("square", i - 1)]),
            ("act", "square", i, 0.5, [("pos", i), ("ctx", i - 2)]),
            ("act", "weight", i, 0.55, [("square", i)]),
            ("pool", "weight2", i, 1.25 if i < c else 2.6, [("weight", i)]),
            ("pe", "ctx", i, 2.2, [("weight2", i)])]
        if i >= 2:
            steps += [("sp", "history", i, 0.1, [("ctx", i - 2)])]
    steps += [("dve", "size", 0, 0.1, [("ctx", c)]), ("pool", "root", 8, 1.0, [("size", 0)])]
    steps += [("dve", "x4", h, 0.85, [("root", 8)]) for h in range(2)]
    steps += [("sp", "history", 9, 0.1, [("ctx", c)])]
    steps += norm_steps(4, [("x4", 0), ("x4", 1)]) + attention_steps(1, 4)
    steps += [("sp", "loadc", 0, 0.1, [("gate", 7), ("pv", 7)])]
    steps += norm_steps(5, [("add", 0), ("add", 1)])
    steps += [("pe", "router", 0, 0.8, [("land", 11)]), ("dve", "router", 1, 0.4, [("router", 0)]),
              ("act", "router", 2, 0.15, [("router", 1)]), ("dve", "router", 3, 0.5, [("router", 2)]),
              ("pe", "router", 4, 0.5, [("router", 3)]), ("act", "router", 5, 0.5, [("router", 4)])]
    for e in range(NE):
        steps += [
            ("pe", "hidden", e, 1.7, [("router", 5), ("kept", e - 2)]),
            ("act", "relu", e, 0.5, [("hidden", e), ("squared", e - 2)]),
            ("dve", "leaky", e, 0.65, [("relu", e)]),
            ("pe", "select", e, 0.25, [("leaky", e)]),
            ("dve", "kept", e, 0.65, [("select", e)]),
            ("act", "squared", e, 0.55, [("kept", e), ("expert", e - 2)]),
            ("pe", "expert", e, 3.4, [("squared", e)])]
    steps += [("dve", "x6", h, 0.65, [("expert", NE - 1)]) for h in range(2)]
    steps += [("sp", "store", 0, 0.1, [("x6", 1)])]
    return steps


def lstm_steps():
    steps = [("pool", "slots", k, 0.6, [("gates", 8 * k - 13)]) for k in range(4)]
    for s in range(STEPS):
        steps += [("pe", "gates", s, 0.3, [("state", s - 1), ("slots", s // 8)]), ("act", "tanh", s, 0.15, [("gates", s)]),
                  ("dve", "cell", s, 0.35, [("tanh", s)]), ("act", "tcell", s, 0.15, [("cell", s)]),
                  ("dve", "state", s, 0.45 if s % 8 < 7 else 0.8, [("tcell", s)])]
    return steps


HOP = 0.2
BODY = {0: 95.0, 1: 100.0, 2: 120.0, 3: 125.0, 4: 125.0, 5: 125.0}


def planned(stage):
    streams = {0: layer0_steps() if stage < NC_ else [], 1: layer1_steps(stage - 2) if stage >= 2 else [],
               2: lstm_steps() if 1 <= stage <= NC_ else []}
    steps, after, last = {}, {}, {}
    for stream, found in streams.items():
        for engine, family, index, takes, needs in found:
            key = (stream, family, index)
            needs = [(stream, *x) for x in needs if x[1] >= 0]
            if (stream, engine, family) in last:
                needs.append(last[stream, engine, family])
            last[stream, engine, family] = key
            steps[key] = (engine, takes, [x for x in needs if x in steps or x[0] == stream])
    for key, (_, _, needs) in steps.items():
        for x in needs:
            after.setdefault(x, []).append(key)
    rest = {}

    def remaining(key):
        if key not in rest:
            rest[key] = steps[key][1] + HOP + max([remaining(x) for x in after.get(key, [])], default=0.0)
        return rest[key]

    start, end, free, order = {}, {}, {}, []
    waiting = set(steps)
    while waiting:
        best = None
        for key in waiting:
            engine, takes, needs = steps[key]
            if any(x in waiting for x in needs):
                continue
            ready = max([end[x] + (HOP if steps[x][0] != engine else 0.1) for x in needs], default=0.0)
            rank = remaining(key)
            if key[0] == 2:
                ready = max(ready, BODY[stage] * key[2] / STEPS) if key[1] == "gates" else ready
                rank += 1000.0
            begin = max(ready, free.get(engine, 0.0))
            offer = (round(begin / 0.3), -rank, begin, key)
            if best is None or offer < best:
                best = offer
        key = best[3]
        engine, takes, _ = steps[key]
        start[key], end[key] = best[2], best[2] + takes
        free[engine] = end[key]
        waiting.remove(key)
        order.append((engine, *key))
    return order


PLANS = {stage: planned(stage) for stage in range(6)}


def positions(c, g):
    return sum(range(1, c + 1)) * NG + (c + 1) * g


def run_stages(engine, name, step):
    def body(stage, g):
        for who, stream, family, index in PLANS[stage]:
            if who == name:
                c = stage - (0, 2, 1)[stream]
                step(stream, family, index, c, g, NG * c + g)

    for stage in range(NC_ + 2):
        if stage <= 2:
            body(stage, 0)
        with engine.Fori(1 if stage <= 2 else 0, NG) as g:
            body(stage, g)


def decoder_program(nc, a, out):
    ctx = ExitStack()
    with ctx:
        def sb(name, shape, dt=F32):
            return ctx.enter_context(nc.sbuf_tensor(name, shape, dt))

        def ps(name, shape, dt=F32):
            return ctx.enter_context(nc.psum_tensor(name, shape, dt))

        def sem(name):
            return ctx.enter_context(nc.semaphore(name))

        x3_dram = nc.dram_tensor("x3_dram", [B, S, D], F32, kind="Internal").ap()
        xln_dram = nc.dram_tensor("xln_dram", [B, S, D], F32, kind="Internal").ap()
        k_dram = nc.dram_tensor("k_dram", [2, P, NH, B, SK], F32, kind="Internal").ap()
        v_dram = nc.dram_tensor("v_dram", [2, B, P, NP * VW], F32, kind="Internal").ap()

        ident = sb("ident", [P, P])
        tri = sb("tri", [P, P])
        headmask = sb("headmask", [P, NE])
        rank = sb("rank", [P, NE])
        neghalf = sb("neghalf", [P, GB])
        sel = sb("sel", [NE, NE, P], BF16)

        posl = sb("posl", [64, NC_, P])
        jrow = sb("jrow", [1, 2, S])
        wA = sb("wA", [P, NH, D])
        wB = sb("wB", [P, NH, D])
        wC = sb("wC", [P, NH, D])
        wD = sb("wD", [P, NH, D])
        wOut = sb("wOut", [P, NH, D])
        wQ = [sb(f"wQ{l}", [P, NH, D]) for l in range(2)]
        wO = [sb(f"wO{l}", [P, NH, D]) for l in range(2)]
        wF = sb("wF", [P, NH, D])
        wih = sb("wih", [P, NH, 96])
        wcat = sb("wcat", [P, 80])
        wms = sb("wms", [P, P])
        wR = sb("wR", [P, NH, NE])
        wfc = sb("wfc", [P, NH, NE * P])
        wpj = sb("wpj", [P, NE, D])
        normw = sb("normw", [P, NH])
        biasA = sb("biasA", [P, NH])
        biasQ = [sb(f"biasQ{l}", [P, NH]) for l in range(2)]
        biasK = [sb(f"biasK{l}", [P, NH]) for l in range(2)]
        biasG = sb("biasG", [96, 2])
        rowOut = sb("rowOut", [P, D])
        rowO = [sb(f"rowO{l}", [P, D]) for l in range(2)]
        rowF = sb("rowF", [P, D])
        ones = sb("ones", [P, 1])

        R = sb("R", [P, B, 3 * P])
        slots = sb("slots", [P, STEPS + 2, B])
        gates = sb("gates", [B, 5 * PE_])
        uprod = sb("uprod", [B, 2 * PE_])
        tcell = sb("tcell", [B, PE_])
        hnew = sb("hnew", [32, 32])
        carry = sb("carry", [P, NH, B])
        mcarry = sb("mcarry", [1, B])

        tiles = [Tiles(f"l{l}", sb) for l in range(2)]
        xin = sb("xin", [P, GB, D])
        mask8 = sb("mask8", [P, GB, SK], mybir.dt.uint8)
        sA, sU, sH = (tiles[0].scratch[:, j * NH * GB * (P + 1):(j + 1) * NH * GB * (P + 1)].rearrange(
            "p (a t) -> p a t", t=P + 1) for j in range(3))
        tD = sb("tD", [P, NT])
        tC = tiles[0].qT
        gp = sb("gp", [P, GB, SK])
        mask32 = sb("mask32", [P, GB, SK], mybir.dt.int32)
        xln = sb("xln", [P, 2, GB, D])
        wT = [sb(f"wT{i}", [P, NT]) for i in range(2)]
        wsq = [sb(f"wsq{i}", [P, NT]) for i in range(2)]
        zrow = tiles[1].scratch[0:1, 0:3 * NT].rearrange("p (j n) -> p j n", j=3)
        mrow = tiles[1].scratch[0:1, 3 * NT:3 * NT + 3 * GB * (P + 1)].rearrange("p (j n) -> p j n", j=3)
        urow = sb("urow", [64, NT])
        nrm = sb("nrm", [P, 2, GB])
        lg = sb("lg", [P, 4, GB, NE])
        lmx = sb("lmx", [P, 2, GB])
        ohT = sb("ohT", [NE, NT], BF16)
        hr = [sb(f"hr{i}", [P, NT]) for i in range(2)]
        hq = [sb(f"hq{i}", [P, NT]) for i in range(2)]
        ctxA = xln[:, :, :, :].rearrange("p i b d -> p (i b d)").rearrange("p (h b k) -> p h b k", h=NH, b=B)
        kv_w = [(tiles[l].xres[:, 0:NH, :], tiles[l].xres[:, NH:2 * NH, :]) for l in range(2)]
        once = tiles[0].xnat
        sel32 = tiles[1].xnat[0:NE, :, :].rearrange("p b d -> p (b d)").rearrange("p (e m) -> p e m", e=NE)
        KT = [tiles[l].scratch[:, 0:NH * B * SK].rearrange("p (h b k) -> p h b k", h=NH, b=B) for l in range(2)]

        p0 = ps("p0", [P, 3 * NT])
        p1 = ps("p1", [P, 4 * NT])
        pg = ps("pg", [P, NT])
        pairs = [p0[:, 0:2 * NT], p1[:, 0:2 * NT]]
        pb = p0[:, 2 * NT:3 * NT]
        qb, qc = p1[:, 2 * NT:3 * NT], p1[:, 3 * NT:4 * NT]
        banks = [[p0[:, j * NT:(j + 1) * NT] for j in range(3)], [p1[:, j * NT:(j + 1) * NT] for j in range(4)]]
        t_bank, o_bank = [pb, qb], [pb, qc]

        ln = [LayerNorm(f"ln{i}", sb, sem) for i in range(6)]
        at = [Attention(f"at{i}", sem) for i in range(2)]
        w_load, prep_in, prep_pe, prep_ev, prep_v, prep_done = (
            sem(n) for n in ("w_load", "prep_in", "prep_pe", "prep_ev", "prep_v", "prep_done"))
        k_store = sem("k_store")
        v_store = [sem(f"v_store{i}") for i in range(GB)]
        wf_pe, wf_ev = sem("wf_pe"), sem("wf_ev")
        x_load, base_ready, p_ready, t_act, u_ready, a_ready, s_carry, s_scan, g_ready, y_ready, x1_ready = (
            sem(n) for n in ("x_load", "base_ready", "p_ready", "t_act", "u_ready", "a_ready", "s_carry",
                             "s_scan", "g_ready", "y_ready", "x1_ready"))
        c_ready, f_proj, f_base, x3_ready, xg_pe, xg_ready, x3_store, xln_store = (
            sem(n) for n in ("c_ready", "f_proj", "f_base", "x3_ready", "xg_pe", "xg_ready", "x3_store", "xln_store"))
        xln_load = [sem(f"xln_load{i}") for i in range(2)]
        l_in, l_pe, l_tanh, l_u, l_c, l_tc, l_h, l_t, l_out = (
            sem(n) for n in ("l_in", "l_pe", "l_tanh", "l_u", "l_c", "l_tc", "l_h", "l_t", "l_out"))
        x3_load, z_pe, z_small, z_exp, u_rows, pos_pe, pos_sq, pos_w, pos_m, pos_w2, ctx_pe, n_a, n_b, x4_ready = (
            sem(n) for n in ("x3_load", "z_pe", "z_small", "z_exp", "u_rows",
                             "pos_pe", "pos_sq", "pos_w", "pos_m", "pos_w2", "ctx_pe", "n_a", "n_b", "x4_ready"))
        r_pe, r_small, r_exp, r_oh, oh_pe, oh_ev, fc_pe, sel_pe, fc_relu, fc_sum, fc_mask, fc_sq, moe_pe, x6_ready, o_store = (
            sem(n) for n in ("r_pe", "r_small", "r_exp", "r_oh", "oh_pe", "oh_ev", "fc_pe", "sel_pe",
                             "fc_relu", "fc_sum", "fc_mask", "fc_sq", "moe_pe", "x6_ready", "o_store"))

        halves = lambda w: w.rearrange("(h p) n -> p h n", p=P)
        unit = lambda t, c, g: t[bass.ds(GB * g, GB), c * P:(c + 1) * P, :].rearrange("b t d -> t b d")
        NLOAD = 0
        loads = [
            (ident[:, :], a["c_ident"]), (tri[:, :], a["c_tri"]), (headmask[:, :], a["c_headmask"]),
            (rank[:, :], a["c_rank"]), (sel32, a["c_sel"]), (posl[:, :, :], a["c_posl"]),
            (jrow[:, :, :], a["c_jrow"]),
            (wA[:, :, :], halves(a["A_w"])), (wB[:, :, :], halves(a["B_w"])), (wC[:, :, :], halves(a["C_w"])),
            (wD[:, :, :], halves(a["D_w"])), (wOut[:, :, :], halves(a["out_w"])),
            (wQ[0][:, :, :], halves(a["Wq"])), (wQ[1][:, :, :], halves(a["wq_k"])),
            (wO[0][:, :, :], halves(a["Wo"])), (wO[1][:, :, :], halves(a["wo_k"])),
            (wF[:, :, :], halves(a["W"])), (wR[:, :, :], halves(a["w_router"])), (wih[:, :, :], halves(a["W_ih"])), (biasG[:, :], a["b_gates"]),
            (wfc[:, :, :], halves(a["w_fc"])), (wpj[:, :, :], a["w_proj"]),
            (normw[:, :], a["norm_w"]),
            (biasA[:, :], a["A_b"]),
            (biasQ[0][:, :], a["bq"]),
            (biasQ[1][:, :], a["wq_b"]),
            (biasK[0][:, :], a["bk"]),
            (biasK[1][:, :], a["wk_b"]),
            (rowOut[:, :], a["out_b"].rearrange("(o n) -> o n", o=1).broadcast_to([P, D])),
            (rowO[0][:, :], a["bo"].rearrange("(o n) -> o n", o=1).broadcast_to([P, D])),
            (rowO[1][:, :], a["wo_b"].rearrange("(o n) -> o n", o=1).broadcast_to([P, D])),
            (rowF[:, :], a["b"].rearrange("(o n) -> o n", o=1).broadcast_to([P, D])),
            (ctxA, a["ctx"].rearrange("(h p) b k -> p h b k", p=P)),
            (kv_w[0][0], halves(a["Wk"])), (kv_w[0][1], halves(a["Wv"])),
            (kv_w[1][0], halves(a["wk_k"])), (kv_w[1][1], halves(a["wv_k"])),
            (once[:, 0, :], a["bv"].rearrange("(o n) -> o n", o=1).broadcast_to([P, D])),
            (once[:, 1, :], a["wv_b"].rearrange("(o n) -> o n", o=1).broadcast_to([P, D])),
            (once[0:32, 2, :], a["C"]), (once[0:32, 3, :], a["V_r"]),
        ]
        late_loads = [
            (wcat[0:80, :], a["c_gatesel"]), (wcat[96:116, :], a["W_hh"]),
            (wms[80:81, :], a["b_mu_sig"]), (wms[96:116, :], a["W_mu_sig"]),
        ]
        NLOAD = 16 * (len(loads) + len(late_loads))
        block = ctx.enter_context(nc.Block())


        @block.sync
        def _(sp):
            for dst, src in loads:
                sp.dma_start(dst, src).then_inc(w_load, 16)
            sp.wait_ge(prep_in, 3)
            for dst, src in late_loads:
                sp.dma_start(dst, src).then_inc(w_load, 16)
            sp.wait_ge(prep_ev, 8)
            for l in range(2):
                sp.dma_start(k_dram[l], KT[l]).then_inc(k_store, 16)
            for l in range(2):
                for b in range(B):
                    n = l * B + b
                    sp.wait_ge(prep_v, 2 * n + 2)
                    sp.dma_start(v_dram[l, b, :, :], tiles[0].vg[:, n % GB, :]).then_inc(v_store[n % GB], 16)
            sp.wait_ge(k_store, 32)
            for i in range(GB):
                sp.wait_ge(v_store[i], 16 * (2 * B // GB))
            sp.wait_ge(prep_done, 1)

            def load_x(c, g, n):
                if positive(n):
                    sp.wait_ge(base_ready, n)
                    sp.wait_ge(ln[0].normed, 2 * n)
                sp.dma_start(xin[:, :, :], unit(a["x"], c, g)).then_inc(x_load, 16)

            def load_context(l, c, g, n):
                t, w = at[l], tiles[l]
                if positive(n):
                    sp.wait_ge(t.kbd, 2 * GB * n)
                    sp.wait_ge(t.pv, 2 * GB * n)
                    sp.wait_ge(t.neg, n)
                    if l == 1:
                        sp.wait_ge(t.gated, 2 * GB * n)
                sp.dma_start(w.vg[:, :, :], v_dram[l, bass.ds(GB * g, GB), :, :].rearrange("b p n -> p b n")
                             ).then_inc(t.v_load, 16)
                sp.dma_start(w.kg[:, :, :, :], k_dram[l, :, :, bass.ds(GB * g, GB), :]).then_inc(t.m_load, 16)
                if l == 0:
                    sp.dma_start(mask8[:, :, :], unit(a["mask0"], c, g)).then_inc(t.m_load, 16)
                else:
                    sp.dma_start(mask32[:, :, :], unit(a["mask1"], c, g)).then_inc(t.m_load, 16)
                    sp.dma_start(gp[:, :, :], unit(a["fside"], c, g)).then_inc(t.m_load, 16)

            def load_history(i, c, g, n):
                used = positions(c, g) + (i - 1 if i >= 2 else 0)
                sp.wait_ge(xln_store, 16 * NG * (c + 1))
                if positive(used):
                    sp.wait_ge(ctx_pe, used)
                sp.dma_start(xln[:, i % 2, :, :], unit(xln_dram, i, g)).then_inc(xln_load[i % 2], 16)

            def sp_step(stream, family, index, c, g, n):
                c2, g2 = (n + 1) // NG, (n + 1) % NG
                last = n + 1 == NC_ * NG
                if (stream, family) == (0, "store"):
                    sp.wait_ge(ln[3].normed, 2 * n + 2)
                    sp.dma_start(unit(xln_dram, c, g), tiles[0].xnat[:, :, :]).then_inc(xln_store, 16)
                    sp.dma_start(unit(x3_dram, c, g), tiles[0].xres[:, :, :]).then_inc(x3_store, 16)
                elif (stream, family) == (1, "store"):
                    sp.wait_ge(x6_ready, 2 * n + 2)
                    sp.dma_start(unit(out, c, g), tiles[1].xres[:, :, :]).then_inc(o_store, 16)
                elif family == "loadx3":
                    if positive(n):
                        sp.wait_ge(o_store, 16 * n)
                    sp.wait_ge(x3_store, 16 * NG * (c + 1))
                    sp.dma_start(tiles[1].xres[:, :, :], unit(x3_dram, c, g)).then_inc(x3_load, 16)
                elif family == "history" and index < NC_:
                    load_history(index, c, g, n)
                elif last:
                    return
                elif family == "loadx":
                    load_x(c2, g2, n + 1)
                elif family == "loadc":
                    load_context(stream, c2, g2, n + 1)
                elif family == "history":
                    for i in range(min(2, c2 + 1)):
                        load_history(i, c2, g2, n + 1)

            for stage in range(NC_ + 2):
                for g in range(NG):
                    if (stage, g) == (0, 0):
                        load_x(0, 0, 0)
                        load_context(0, 0, 0, 0)
                    if (stage, g) == (2, 0):
                        load_history(0, 0, 0, 0)
                        load_context(1, 0, 0, 0)
                    for who, stream, family, index in PLANS[stage]:
                        if who == "sp":
                            c = stage - (0, 2, 1)[stream]
                            sp_step(stream, family, index, c, g, NG * c + g)
            sp.wait_ge(o_store, 16 * NC_ * NG)

        @block.tensor
        def _(pe):
            pe.wait_ge(w_load, NLOAD)
            for h in range(NH):
                i = pe.matmul(banks[0][0][:, h * D:(h + 1) * D], once[0:32, 3, h * P:(h + 1) * P], once[0:32, 2, :],
                              start=True, stop=True)
            i.then_inc(wf_pe, 1)
            n = 0
            for l in range(2):
                for m in range(NH):
                    for j in range(2):
                        if n >= 2:
                            pe.wait_ge(prep_ev, n - 1)
                        for k in range(NH):
                            i = pe.matmul(banks[1][n % 2], kv_w[l][0][:, k, m * P:(m + 1) * P],
                                          ctxA[:, k, 8 * j:8 * j + 8, :].rearrange("p b k -> p (b k)"),
                                          start=(k == 0), stop=(k == NH - 1))
                        i.then_inc(prep_pe, 1)
                        n += 1
            pe.wait_ge(prep_ev, n)
            for l in range(2):
                for b in range(B):
                    v = l * B + b
                    if v >= 2:
                        pe.wait_ge(prep_v, 2 * v - 2)
                    for e in range(2):
                        for k in range(NH):
                            i = pe.matmul(banks[1][v % 2][64 * e:64 * e + 64, 0:D], ctxA[:, k, b, :], kv_w[l][1][:, k, :],
                                          start=(k == 0), stop=(k == NH - 1))
                    i.then_inc(prep_pe, 1)
            pe.wait_ge(prep_done, 1)

            def turn(l, h, src, done):
                for m in range(NH):
                    for b in (2 * h, 2 * h + 1):
                        i = pe.transpose(banks[l][m][:, b * P:(b + 1) * P], src[:, b, m * P:(m + 1) * P], ident[:, :])
                i.then_inc(done, 1)

            def project(l, h, x, w, done):
                for b in (2 * h, 2 * h + 1):
                    for k in range(NH):
                        i = pe.matmul(pairs[l][:, b * D:(b + 1) * D], x[:, k, b * P:(b + 1) * P], w[:, k, :],
                                      start=(k == 0), stop=(k == NH - 1))
                i.then_inc(done, 1)

            def attention_step(l, family, i_, n):
                t, w = at[l], tiles[l]
                if family == "query":
                    if i_ == 0:
                        pe.wait_ge(ln[(1, 4)[l]].landed, 2 * n + 2)
                    for k in range(NH):
                        i = pe.matmul(banks[l][2 - i_], wQ[l][:, k, i_ * P:(i_ + 1) * P], w.xT[:, k, :],
                                      start=(k == 0), stop=(k == NH - 1))
                    i.then_inc(t.q, 1)
                    return
                if family == "oturn":
                    pe.wait_ge(t.o, 2 * GB * n + GB * i_ + GB)
                    if i_ == 0:
                        pe.wait_ge(t.masked, 2 * GB * n + 2 * GB)
                    turn(l, i_, w.xnat, t.o_turned)
                    return
                if family == "proj":
                    pe.wait_ge(t.oT, 2 * n + 2)
                    project(l, i_, w.xT, wO[l], t.proj)
                    return
                u, (b, j), N = i_, divmod(i_, 2), 2 * GB * n + i_
                if family == "score":
                    if u < 2:
                        pe.wait_ge(t.q_ready, 2 * n + u + 1)
                    else:
                        pe.wait_ge(t.masked, N - 1)
                    pe.wait_ge(t.kbd, N + 1)
                    pe.matmul(banks[l][j], w.qT[:, j, b * P:(b + 1) * P],
                              w.kbd[b % 2][:, j, :, :].rearrange("p a k -> p (a k)"), start=True, stop=True
                              ).then_inc(t.scores, 1)
                elif family == "pturn":
                    if l == 0:
                        pe.wait_ge(t.exped, N + 1)
                        if u:
                            pe.wait_ge(t.o, N)
                    else:
                        pe.wait_ge(t.gated, N + 1)
                        if u:
                            pe.wait_ge(t.exT, N)
                    for p in range(4):
                        src = w.ex[b % 2][:, 8 * j + 2 * p:8 * j + 2 * p + 2, :].rearrange("p a k -> p (a k)")
                        i = pe.transpose(t_bank[l][:, p * P:(p + 1) * P], src, ident[:, :])
                    i.then_inc(t.turned, 1)
                elif family == "pv":
                    if u == 0:
                        pe.wait_ge(t.v_load, 16 * n + 16)
                    elif l == 1:
                        pe.wait_ge(t.o, N)
                    pe.wait_ge(t.exT, N + 1)
                    for p in range(4):
                        q = 4 * j + p
                        i = pe.matmul(o_bank[l][:, q * VW:(q + 1) * VW], w.exT[:, j, p, :], w.vg[:, b, q * VW:(q + 1) * VW],
                                      start=True, stop=True)
                    i.then_inc(t.pv, 1)

            def pe_step(stream, family, i_, c, g, n):
                if stream == 2:
                    if i_ % 8 == 0:
                        pe.wait_ge(l_in, 4 * n + i_ // 8 + 1)
                    pe.wait_ge(l_t, STEPS * n + i_ + 1)
                    pe.matmul(pg[0:B, 0:80], slots[:, i_, :], wcat[:, :], start=True, stop=True).then_inc(l_pe, 1)
                elif family in ("query", "score", "pturn", "pv", "oturn", "proj"):
                    attention_step(stream, family, i_, n)
                elif family == "turn":
                    k, h = divmod(i_, 2)
                    pe.wait_ge(ln[k].normed, 2 * n + h + 1)
                    turn(stream, h, tiles[stream].xnat, ln[k].turned)
                elif family == "gate":
                    m, j = divmod(i_, 4)
                    if i_ == 0:
                        pe.wait_ge(ln[0].landed, 2 * n + 2)
                        if positive(n):
                            pe.wait_ge(xg_ready, n)
                    elif i_ == 4:
                        pe.wait_ge(u_ready, 2 * n + 1)
                    elif i_ >= 3:
                        pe.wait_ge(t_act, 6 * n + max(i_ - 3, 1))
                    w = (wD, wB, wA, wC)[j]
                    bank = banks[0][(0, 1, 2, 0, 1, 2, 0, 1)[i_]]
                    for k in range(NH):
                        i = pe.matmul(bank, w[:, k, m * P:(m + 1) * P], tiles[0].xT[:, k, :],
                                      start=(k == 0), stop=(k == NH - 1))
                    i.then_inc(p_ready, 1)
                elif family == "out":
                    pe.wait_ge(g_ready, n + 1)
                    project(0, i_, tC, wOut, y_ready)
                elif family == "ffn":
                    pe.wait_ge(ln[2].landed, 2 * n + 2)
                    project(0, i_, tiles[0].xT, wF, f_proj)
                elif family == "gatein":
                    pe.wait_ge(ln[3].landed, 2 * n + 2)
                    for k in range(NH):
                        i = pe.matmul(pb[0:96, :], wih[:, k, :], tiles[0].xT[:, k, :], start=(k == 0), stop=(k == NH - 1))
                    i.then_inc(xg_pe, 1)
                elif family == "rows":
                    pe.wait_ge(l_out, 4 * NG * (c + 1))
                    pe.matmul(qc, wms[:, :], R[:, bass.ds(GB * g, GB), (c % 3) * P:(c % 3 + 1) * P],
                              start=True, stop=True).then_inc(z_pe, 1)
                elif family == "pos":
                    if i_ == 0:
                        pe.wait_ge(u_rows, 2 * n + 2)
                    else:
                        pe.wait_ge(pos_sq, positions(c, g) + i_)
                    pe.matmul(qb, posl[:, i_, :], urow[:, :], start=True, stop=True).then_inc(pos_pe, 1)
                elif family == "ctx":
                    pe.wait_ge(pos_w2, positions(c, g) + i_ + 1)
                    even, odd = c // 2 + 1, (c + 1) // 2
                    loaded = [sum(k // 2 + 1 for k in range(c)) * NG + even * g,
                              sum((k + 1) // 2 for k in range(c)) * NG + odd * g][i_ % 2] + i_ // 2 + 1
                    pe.wait_ge(xln_load[i_ % 2], 16 * loaded)
                    for b in range(GB):
                        pe.matmul(pairs[1][:, b * D:(b + 1) * D], wT[i_ % 2][:, b * P:(b + 1) * P], xln[:, i_ % 2, b, :],
                                  start=(i_ == 0 and b % 2 == 0), stop=(i_ == c), skip_group_check=True)
                    for b in range(GB):
                        i = pe.matmul(qc[:, b:b + 1], wsq[i_ % 2][:, b * P:(b + 1) * P], ones[:, :],
                                      start=(i_ == 0 and b == 0), stop=(i_ == c), skip_group_check=True)
                    i.then_inc(ctx_pe, 1)
                elif family == "router" and i_ == 0:
                    pe.wait_ge(ln[5].landed, 2 * n + 2)
                    for b in range(GB):
                        for k in range(NH):
                            i = pe.matmul(qc[:, b * NE:(b + 1) * NE], tiles[1].xT[:, k, b * P:(b + 1) * P], wR[:, k, :],
                                          start=(k == 0), stop=(k == NH - 1))
                    i.then_inc(r_pe, 1)
                elif family == "router":
                    pe.wait_ge(r_oh, n + 1)
                    for b in range(GB):
                        i = pe.transpose(qb[0:NE, b * P:(b + 1) * P], lg[:, 3, b, :], ident[:, :])
                    i.then_inc(oh_pe, 1)
                elif family == "hidden":
                    if i_ == 0:
                        pe.wait_ge(oh_ev, n + 1)
                    elif i_ >= 2:
                        pe.wait_ge(fc_mask, NE * n + i_ - 1)
                    for k in range(NH):
                        i = pe.matmul(banks[1][2 + i_ % 2], wfc[:, k, i_ * P:(i_ + 1) * P], tiles[1].xT[:, k, :],
                                      start=(k == 0), stop=(k == NH - 1))
                    i.then_inc(fc_pe, 1)
                elif family == "select":
                    pe.wait_ge(fc_sum, NE * n + i_ + 1)
                    pe.matmul(banks[1][2 + i_ % 2], sel[:, i_, :], ohT[:, :], start=True, stop=True).then_inc(sel_pe, 1)
                elif family == "expert":
                    pe.wait_ge(fc_sq, NE * n + i_ + 1)
                    for b in range(GB):
                        i = pe.matmul(pairs[1][:, b * D:(b + 1) * D], hq[i_ % 2][:, b * P:(b + 1) * P], wpj[:, i_, :],
                                      start=(i_ == 0 and b % 2 == 0), stop=(i_ == NE - 1), skip_group_check=True)
                    i.then_inc(moe_pe, 1)

            run_stages(pe, "pe", pe_step)

        @block.scalar
        def _(act):
            act.wait_ge(w_load, NLOAD)
            n = 0
            for l in range(2):
                for m in range(NH):
                    for j in range(2):
                        act.wait_ge(prep_pe, n + 1)
                        act.activation(KT[l][:, m, 8 * j:8 * j + 8, :].rearrange("p b k -> p (b k)"),
                                       banks[1][n % 2], ACT.Identity,
                                       bias=biasK[l][:, m:m + 1]).then_inc(prep_ev, 1)
                        n += 1
            act.wait_ge(prep_done, 1)

            def act_step(stream, family, i_, c, g, n):
                if stream == 2:
                    k = STEPS * n + i_
                    if family == "tanh":
                        act.wait_ge(l_pe, k + 1)
                        act.activation(gates[:, 0:80], pg[0:B, 0:80], ACT.Tanh).then_inc(l_tanh, 1)
                    else:
                        act.wait_ge(l_c, k + 1)
                        act.activation(tcell[:, :], gates[:, 80:100], ACT.Tanh, scale=0.5).then_inc(l_tc, 1)
                    return
                t, w = at[stream], tiles[stream]
                if family == "land":
                    k, h = divmod(i_, 2)
                    if h == 0:
                        act.wait_ge(ln[k].turned, 2 * n + 2)
                    act.activation(w.xT[:, h, :], banks[stream][h], ACT.Identity).then_inc(ln[k].landed, 1)
                elif family == "oland":
                    if i_ == 0:
                        act.wait_ge(t.o_turned, 2 * n + 2)
                    act.activation(w.xT[:, i_, :], banks[stream][i_], ACT.Identity).then_inc(t.oT, 1)
                elif family == "qland":
                    act.wait_ge(t.q, 2 * n + i_ + 1)
                    act.activation(w.qT[:, i_, :], banks[stream][2 - i_], ACT.Identity,
                                   bias=biasQ[stream][:, i_:i_ + 1], scale=0.25).then_inc(t.q_ready, 1)
                elif family == "exp":
                    b, j = divmod(i_, 2)
                    act.wait_ge(t.shifted, 2 * GB * n + i_ + 1)
                    ex = w.ex[b % 2][:, NE * j:NE * j + NE, :]
                    act.activation(ex, ex, ACT.Exp).then_inc(t.exped, 1)
                elif family == "pland":
                    act.wait_ge(t.turned, 2 * GB * n + i_ + 1)
                    if i_ >= 2:
                        act.wait_ge(t.pv, 2 * GB * n + i_ - 1)
                    act.activation(w.exT[:, i_ % 2, :, :], t_bank[stream].rearrange("p (a t) -> p a t", a=4),
                                   ACT.Identity).then_inc(t.exT, 1)
                elif family == "tanh":
                    m, j = divmod(i_, 3)
                    bank = banks[0][(0, 2, 0, 1, 0, 1)[i_]]
                    act.wait_ge(p_ready, 8 * n + 4 * m + (1, 3, 4)[j])
                    if j == 0:
                        act.activation(tD[:, :], bank, ACT.Tanh, scale=0.5).then_inc(t_act, 1)
                    elif j == 1:
                        act.activation(sA[:, GB * m:GB * m + GB, 1:P + 1], bank.rearrange("p (b t) -> p b t", b=GB),
                                       ACT.Tanh, bias=biasA[:, m:m + 1], scale=0.5).then_inc(t_act, 1)
                    else:
                        act.activation(tC[:, m, :], bank, ACT.Tanh, scale=0.5).then_inc(t_act, 1)
                elif family == "gatein":
                    act.wait_ge(xg_pe, n + 1)
                    if c == 3:
                        act.wait_ge(z_pe, NG)
                    act.activation(R[0:96, bass.ds(GB * g, GB), (c % 3) * P:(c % 3 + 1) * P],
                                   pb[0:96, :].rearrange("p (b t) -> p b t", b=GB), ACT.Identity,
                                   bias=biasG[:, 0:1]).then_inc(xg_ready, 1)
                elif family == "rows":
                    act.wait_ge(z_pe, n + 1)
                    act.activation(zrow[:, 0, :], qc[96:97, :], ACT.Exp, scale=-1.0).then_inc(z_exp, 1)
                elif family == "square":
                    act.wait_ge(pos_pe, positions(c, g) + i_ + 1)
                    if i_ >= 2:
                        act.wait_ge(ctx_pe, positions(c, g) + i_ - 1)
                    act.activation(wT[i_ % 2][:, :], qb, ACT.Square).then_inc(pos_sq, 1)
                elif family == "weight":
                    act.wait_ge(pos_sq, positions(c, g) + i_ + 1)
                    act.activation(wT[i_ % 2][:, :], wT[i_ % 2][:, :], ACT.Exp, scale=-1.0).then_inc(pos_w, 1)
                elif family == "router" and i_ == 2:
                    act.wait_ge(r_small, 4 * n + 2)
                    act.activation(lg[:, 1, :, :], lg[:, 0, :, :], ACT.Exp).then_inc(r_exp, 1)
                elif family == "router":
                    act.wait_ge(oh_pe, n + 1)
                    act.activation(ohT[:, :], qb[0:NE, :], ACT.Identity).then_inc(oh_ev, 1)
                elif family == "relu":
                    act.wait_ge(fc_pe, NE * n + i_ + 1)
                    if i_ >= 2:
                        act.wait_ge(fc_sq, NE * n + i_ - 1)
                    act.activation(hr[i_ % 2][:, :], banks[1][2 + i_ % 2], ACT.Relu).then_inc(fc_relu, 1)
                elif family == "squared":
                    act.wait_ge(fc_mask, NE * n + i_ + 1)
                    if i_ >= 2:
                        act.wait_ge(moe_pe, NE * n + i_ - 1)
                    act.activation(hq[i_ % 2][:, :], hr[i_ % 2][:, :], ACT.Square).then_inc(fc_sq, 1)

            run_stages(act, "act", act_step)

        @block.vector
        def _(dve):
            vg = tiles[0].vg
            dve.memset(wcat[:, :], 0.0).then_inc(prep_in, 1)
            dve.memset(wms[:, :], 0.0)
            dve.memset(neghalf[:, :], -0.5)
            dve.memset(ones[:, :], 1.0)
            dve.memset(carry[:, :, :], 0.0)
            dve.memset(mcarry[:, :], 0.0)
            dve.memset(urow[:, :], 0.0)
            dve.memset(hnew[:, :], 0.0)
            dve.memset(gates[:, :], 0.0)
            dve.memset(slots[:, :, :], 0.0)
            dve.memset(R[64:128, :, :], 0.0)
            dve.memset(vg[:, :, :], 0.0).then_inc(prep_in, 1)
            dve.wait_ge(prep_in, 2)
            for b in range(GB):
                vb = vg[:, b, :].rearrange("p (q w) -> p q w", w=VW)
                dve.memset(vb[0:64, :, 2 * HD:2 * HD + 1], 1.0)
                i = dve.memset(vb[64:128, :, 2 * HD + 1:VW], 1.0)
            i.then_inc(prep_in, 1)
            dve.wait_ge(w_load, NLOAD)
            for w in (wA, wB, wC, wD):
                for h in range(NH):
                    dve.tensor_scalar(w[:, h, :], w[:, h, :], normw[:, h:h + 1], None, ALU.mult)
            dve.tensor_scalar(wOut[:, :, :], wOut[:, :, :], 0.25, None, ALU.mult)
            dve.tensor_copy(sel[:, :, :], sel32)
            dve.tensor_scalar(biasA[:, :], biasA[:, :], 0.5, None, ALU.mult)
            dve.tensor_scalar(biasQ[0][:, :], biasQ[0][:, :], 0.25, None, ALU.mult)
            dve.tensor_scalar(biasQ[1][:, :], biasQ[1][:, :], 0.25, None, ALU.mult)
            dve.tensor_scalar(wcat[96:128, 0:60], wcat[96:128, 0:60], 0.25, None, ALU.mult)
            dve.tensor_scalar(wcat[96:128, 60:80], wcat[96:128, 60:80], 0.5, None, ALU.mult)
            dve.tensor_scalar(wms[96:128, :], wms[96:128, :], 0.5, None, ALU.mult)
            dve.tensor_scalar(wpj[:, :, :], wpj[:, :, :], 0.25, None, ALU.mult)
            dve.tensor_tensor(biasG[:, 0:1], biasG[:, 0:1], biasG[:, 1:2], ALU.add)
            dve.wait_ge(wf_pe, 1)
            dve.tensor_tensor(wF[:, :, :], banks[0][0][:, 0:NH * D].rearrange("p (h n) -> p h n", h=NH), wF[:, :, :],
                              ALU.add).then_inc(wf_ev, 1)
            for l in range(2):
                for b in range(B):
                    v = l * B + b
                    dve.wait_ge(prep_pe, 8 + v + 1)
                    if v >= GB:
                        dve.wait_ge(v_store[v % GB], 16 * (v // GB))
                    vb = vg[:, v % GB, :].rearrange("p (q w) -> p q w", w=VW)
                    bank = banks[1][v % 2]
                    for e in range(2):
                        r = slice(64 * e, 64 * e + 64)
                        dve.tensor_tensor(
                            vb[r, :, e * HD:(e + 1) * HD],
                            bank[r, 0:D].rearrange("p (q e w) -> p q e w", e=2, w=HD)[:, :, e, :],
                            once[r, l, :].rearrange("p (q e w) -> p q e w", e=2, w=HD)[:, :, e, :],
                            ALU.add).then_inc(prep_v, 1)
            dve.wait_ge(prep_ev, 8)
            dve.wait_ge(k_store, 32)
            dve.wait_ge(prep_v, 4 * B)
            dve.wait_ge(wf_ev, 1)
            dve.transpose(slots[96:128, 0:2, :].rearrange("p s b -> p (s b)"), hnew[:, :]).then_inc(l_t, 1)
            dve.memset(tiles[0].sums[:, 0, :], 0.0).then_inc(prep_done, 1)

            def statistics(s, h, n, src, small):
                for b in (2 * h, 2 * h + 1):
                    i = dve.bn_stats(s.stats[:, b, :], src[:, b, :])
                i.then_inc(s.small, 1)
                dve.wait_ge(s.small, small * n + 2 * h + 1)
                dve.memset(s.tmp[:, 0, h:h + 1], 0.0)
                for b in (2 * h, 2 * h + 1):
                    i = dve.bn_aggr(s.mv[:, b, :], s.stats[:, b, :])
                i.then_inc(s.small, 1)
                if h:
                    dve.wait_ge(s.small, small * n + 4)
                    dve.tensor_scalar(s.ve[:, 0, :], s.mv[:, :, 1], EPS, None, ALU.add).then_inc(s.small, 1)

            def rms(s, n):
                dve.wait_ge(s.inv, 2 * n + 1)
                dve.tensor_tensor(s.tmp[:, 0, :], s.rstd[:, 0, :], s.rstd[:, 0, :], ALU.mult).then_inc(s.small, 1)
                dve.wait_ge(s.small, 11 * n + 6)
                dve.tensor_tensor(s.tmp[:, 1, :], s.tmp[:, 0, :], s.mv[:, :, 1], ALU.mult).then_inc(s.small, 1)
                dve.wait_ge(s.small, 11 * n + 7)
                dve.tensor_scalar(s.ve[:, 1, :], s.tmp[:, 1, :], EPS, None, ALU.add).then_inc(s.small, 1)
                dve.tensor_tensor(s.tmp[:, 2, :], s.mv[:, :, 0], s.rstd[:, 0, :], ALU.mult).then_inc(s.small, 1)
                dve.tensor_scalar(s.tmp[:, 0, :], s.rstd[:, 0, :], 1.0, None, ALU.add).then_inc(s.small, 1)

            def normalise(s, h, scale, src, dst):
                for b in (2 * h, 2 * h + 1):
                    i = dve.tensor_scalar(dst[:, b, :], src[:, b, :], s.mv[:, b, 0:1], scale[:, b:b + 1],
                                          ALU.subtract, ALU.mult)
                i.then_inc(s.normed, 1)

            def add_product(l, h, done):
                x = tiles[l].xres[:, 2 * h:2 * h + 2, :]
                dve.tensor_tensor(x, banks[l][h].rearrange("p (b d) -> p b d", b=2), x, ALU.add).then_inc(done, 1)

            def attention_step(l, family, i_, n):
                t, w = at[l], tiles[l]
                u, (b, j), N = i_, divmod(i_, 2), 2 * GB * n + i_
                heads = slice(NE * j, NE * j + NE)
                if family == "neg":
                    if l == 0:
                        dve.wait_ge(t.m_load, 32 * n + 32)
                        dve.tensor_scalar(w.neg[:, :, :], mask8[:, :, :], 1.0, FMAX, ALU.subtract, ALU.mult).then_inc(t.neg, 1)
                    else:
                        dve.wait_ge(t.m_load, 48 * n + 48)
                        dve.tensor_scalar(w.neg[:, :, :], mask32[:, :, :], 1.0, 1e9, ALU.subtract, ALU.mult).then_inc(t.neg, 1)
                elif family == "mask":
                    if u == 0:
                        dve.wait_ge(t.neg, n + 1)
                    if u >= 4:
                        dve.wait_ge(t.turned, N - 3)
                    dve.wait_ge(t.scores, N + 1)
                    dve.tensor_tensor(w.ex[b % 2][:, heads, :], banks[l][j].rearrange("p (a k) -> p a k", a=NE),
                                      w.neg[:, b:b + 1, :].broadcast_to([P, NE, SK]), ALU.add).then_inc(t.masked, 1)
                elif family == "max":
                    dve.wait_ge(t.masked, N + 1)
                    dve.tensor_reduce(w.mx[:, u % 4, :], w.ex[b % 2][:, heads, :], AX_X, ALU.max).then_inc(t.top, 1)
                elif family == "sums":
                    dve.wait_ge(t.exped, N + 1)
                    dve.tensor_reduce(w.sums[:, u % 4, :], w.ex[b % 2][:, heads, :], AX_X, ALU.add).then_inc(t.summed, 1)
                    dve.wait_ge(t.summed, N + 1)
                    dve.reciprocal(w.rs[:, u % 4, :], w.sums[:, u % 4, :]).then_inc(t.inv, 1)
                elif family == "o":
                    o = o_bank[l][:, 4 * j * VW:4 * (j + 1) * VW].rearrange("p (q w) -> p q w", w=VW)
                    rs = w.rs[:, u % 4, :].rearrange("p (q e) -> p q e", e=2)
                    dve.wait_ge(t.pv, N + 1)
                    if l == 0:
                        dve.reciprocal(rs, o[:, :, 2 * HD:VW]).then_inc(t.inv, 1)
                    dve.wait_ge(t.inv, N + 1)
                    dve.tensor_tensor(
                        w.xnat[:, b, j * P:(j + 1) * P].rearrange("p (q e w) -> p q e w", e=2, w=HD),
                        o[:, :, 0:2 * HD].rearrange("p q (e w) -> p q e w", e=2),
                        w.rs[:, u % 4, :].rearrange("p (q e o) -> p q e o", e=2, o=1).broadcast_to([P, 4, 2, HD]),
                        ALU.mult).then_inc(t.o, 1)
                elif family == "add":
                    dve.wait_ge(t.proj, 2 * n + i_ + 1)
                    if i_ == 0:
                        dve.wait_ge(t.base, n + 1)
                    add_product(l, i_, t.done)

            def dve_step(stream, family, i_, c, g, n):
                if stream == 2:
                    lstm_step(family, i_, c, g, n)
                elif family in ("neg", "mask", "max", "sums", "o", "add"):
                    attention_step(stream, family, i_, n)
                elif family == "stat":
                    k, h = divmod(i_, 2)
                    if k == 0:
                        if h == 0:
                            dve.wait_ge(x_load, 16 * n + 16)
                        statistics(ln[0], h, n, xin, 11)
                    else:
                        ready = (None, x1_ready, at[0].done, x3_ready, x4_ready, at[1].done)[k]
                        dve.wait_ge(ready, 2 * n + h + 1)
                        statistics(ln[k], h, n, tiles[stream].xres, 5)
                elif family == "rms":
                    rms(ln[0], n)
                elif family == "norm":
                    k, h = divmod(i_, 2)
                    s = ln[k]
                    if k:
                        if h == 0:
                            dve.wait_ge(s.inv, n + 1)
                        normalise(s, h, s.rstd[:, 0, :], tiles[stream].xres, tiles[stream].xnat)
                        return
                    if h == 0:
                        dve.wait_ge(s.inv, 2 * n + 2)
                        dve.tensor_tensor(s.tmp[:, 1, :], s.rstd[:, 0, :], s.rstd[:, 1, :], ALU.mult).then_inc(s.small, 1)
                        if positive(n):
                            dve.wait_ge(xln_store, 16 * n)
                            dve.wait_ge(ln[3].turned, 2 * n)
                        dve.wait_ge(s.small, 11 * n + 11)
                    normalise(s, h, s.tmp[:, 1, :], xin, tiles[0].xnat)
                elif family == "base":
                    s = ln[0]
                    if positive(n):
                        dve.wait_ge(x3_store, 16 * n)
                    dve.wait_ge(s.small, 11 * n + 10)
                    for b in range(GB):
                        i = dve.tensor_scalar(tiles[0].xres[:, b, :], xin[:, b, :], s.tmp[:, 0, b:b + 1], s.tmp[:, 2, b:b + 1],
                                              ALU.mult, ALU.subtract)
                    i.then_inc(base_ready, 1)
                elif family == "carryin":
                    dve.memset(sA[:, :, 0:1], 0.0)
                    for m in range(NH):
                        i = dve.tensor_scalar(sU[:, GB * m:GB * m + GB, 0:1],
                                              carry[:, m, bass.ds(GB * g, GB)].rearrange("p (b o) -> p b o", o=1),
                                              1.0, None, ALU.mult)
                    i.then_inc(s_carry, 1)
                elif family == "u":
                    dve.wait_ge(p_ready, 8 * n + 4 * i_ + 2)
                    dve.wait_ge(t_act, 6 * n + 3 * i_ + 1)
                    dve.scalar_tensor_tensor(
                        sU[:, GB * i_:GB * i_ + GB, 1:P + 1], tD[:, :].rearrange("p (b t) -> p b t", b=GB), 1.0,
                        banks[0][1 + i_].rearrange("p (b t) -> p b t", b=GB), ALU.add, ALU.mult).then_inc(u_ready, 1)
                elif family == "a":
                    decay = sA[:, GB * i_:GB * i_ + GB, 1:P + 1]
                    dve.wait_ge(t_act, 6 * n + 3 * i_ + 2)
                    dve.tensor_scalar(decay, decay, 0.5, 0.5, ALU.mult, ALU.add).then_inc(a_ready, 1)
                elif family == "scan":
                    dve.wait_ge(a_ready, 2 * n + 2)
                    dve.wait_ge(u_ready, 2 * n + 2)
                    dve.wait_ge(s_carry, n + 1)
                    flat = lambda v: v.rearrange("p a t -> p (a t)")
                    dve.tensor_tensor_scan(flat(sH), flat(sA), flat(sU), 0.0, ALU.mult, ALU.add).then_inc(c_ready, 1)
                elif family == "gated":
                    dve.wait_ge(c_ready, n + 1)
                    for m in range(NH):
                        i = dve.tensor_scalar(carry[:, m, bass.ds(GB * g, GB)].rearrange("p (b o) -> p b o", o=1),
                                              sH[:, GB * m:GB * m + GB, P:P + 1], 1.0, None, ALU.mult)
                    i.then_inc(s_scan, 1)
                    dve.wait_ge(t_act, 6 * n + 6)
                    for m in range(NH):
                        i = dve.scalar_tensor_tensor(
                            tC[:, m, :].rearrange("p (b t) -> p b t", b=GB), tC[:, m, :].rearrange("p (b t) -> p b t", b=GB),
                            1.0, sH[:, GB * m:GB * m + GB, 1:P + 1], ALU.add, ALU.mult)
                    i.then_inc(g_ready, 1)
                elif family == "x1":
                    dve.wait_ge(y_ready, 2 * n + i_ + 1)
                    if i_ == 0:
                        dve.wait_ge(f_base, 2 * n + 1)
                    add_product(0, i_, x1_ready)
                elif family == "x3":
                    dve.wait_ge(f_proj, 2 * n + i_ + 1)
                    if i_ == 0:
                        dve.wait_ge(f_base, 2 * n + 2)
                    add_product(0, i_, x3_ready)
                elif family == "rows":
                    position_rows(i_, c, g, n)
                elif family == "size":
                    dve.wait_ge(ctx_pe, positions(c, g) + c + 1)
                    dve.tensor_scalar(nrm[:, 0, :], qc[:, 0:GB], 1e-24, None, ALU.max).then_inc(n_a, 1)
                elif family == "x4":
                    if i_ == 0:
                        dve.wait_ge(n_b, n + 1)
                        dve.wait_ge(x3_load, 16 * n + 16)
                    x = tiles[1].xres
                    for b in (2 * i_, 2 * i_ + 1):
                        i = dve.scalar_tensor_tensor(x[:, b, :], pairs[1][:, b * D:(b + 1) * D], nrm[:, 1, b:b + 1],
                                                     x[:, b, :], ALU.mult, ALU.add)
                    i.then_inc(x4_ready, 1)
                elif family == "router":
                    l3 = qc[:, 0:GB * NE].rearrange("p (b e) -> p b e", b=GB)
                    bc = lambda v: v.rearrange("p (b o) -> p b o", o=1).broadcast_to([P, GB, NE])
                    if i_ == 1:
                        dve.wait_ge(r_pe, n + 1)
                        dve.tensor_reduce(lmx[:, 0, :], l3, AX_X, ALU.max).then_inc(r_small, 1)
                        dve.wait_ge(r_small, 4 * n + 1)
                        dve.tensor_tensor(lg[:, 0, :, :], l3, bc(lmx[:, 0, :]), ALU.subtract).then_inc(r_small, 1)
                        return
                    dve.wait_ge(r_exp, n + 1)
                    dve.scalar_tensor_tensor(lg[:, 2, :, :], lg[:, 1, :, :], 1.0,
                                             rank[:, :].rearrange("p (o e) -> p o e", o=1).broadcast_to([P, GB, NE]),
                                             ALU.is_ge, ALU.mult).then_inc(r_small, 1)
                    dve.wait_ge(r_small, 4 * n + 3)
                    dve.tensor_reduce(lmx[:, 1, :], lg[:, 2, :, :], AX_X, ALU.max).then_inc(r_small, 1)
                    dve.wait_ge(r_small, 4 * n + 4)
                    dve.tensor_tensor(lg[:, 3, :, :], lg[:, 2, :, :], bc(lmx[:, 1, :]), ALU.is_equal).then_inc(r_oh, 1)
                elif family == "leaky":
                    h_ = hr[i_ % 2]
                    dve.wait_ge(fc_relu, NE * n + i_ + 1)
                    dve.tensor_tensor(h_[:, :], banks[1][2 + i_ % 2], h_[:, :], ALU.add).then_inc(fc_sum, 1)
                elif family == "kept":
                    h_ = hr[i_ % 2]
                    dve.wait_ge(fc_sum, NE * n + i_ + 1)
                    dve.wait_ge(sel_pe, NE * n + i_ + 1)
                    dve.tensor_tensor(h_[:, :], banks[1][2 + i_ % 2], h_[:, :], ALU.mult).then_inc(fc_mask, 1)
                elif family == "x6":
                    if i_ == 0:
                        dve.wait_ge(moe_pe, NE * n + NE)
                    add_product(1, i_, x6_ready)

            def position_rows(part, c, g, n):
                m3 = lambda j: mrow[:, j, :].rearrange("p (b t) -> p b t", b=GB)
                z3 = lambda j: zrow[:, j, :].rearrange("p (b t) -> p b t", b=GB)
                J = jrow[:, 0:1, c * P:(c + 1) * P].broadcast_to([1, GB, P])
                RJ = jrow[:, 1:2, c * P:(c + 1) * P].broadcast_to([1, GB, P])
                if part == 2:
                    dve.wait_ge(z_pe, n + 1)
                    dve.tensor_scalar(m3(0)[:, :, 1:P + 1], qc[0:1, :].rearrange("p (b t) -> p b t", b=GB), 0.0, None, ALU.max)
                    dve.memset(m3(0)[:, :, 0:1], 0.0)
                    dve.tensor_copy(m3(1)[:, :, 0:1], mcarry[:, bass.ds(GB * g, GB)].rearrange("p (b o) -> p b o", o=1))
                    dve.tensor_scalar(zrow[:, 1, :], qc[32:33, :], 0.0, 1.0 / S, ALU.max, ALU.mult)
                    dve.tensor_scalar(zrow[:, 2, :], qc[64:65, :], 0.0, None, ALU.max).then_inc(z_small, 1)
                    dve.wait_ge(z_small, 5 * n + 1)
                    dve.tensor_tensor(z3(2), z3(2), J, ALU.mult).then_inc(z_small, 1)
                    dve.wait_ge(z_small, 5 * n + 2)
                    dve.tensor_tensor(m3(1)[:, :, 1:P + 1], z3(1), z3(2), ALU.add).then_inc(z_small, 1)
                    return
                dve.wait_ge(z_small, 5 * n + 3)
                dve.tensor_tensor_scan(mrow[:, 2, :], mrow[:, 0, :], mrow[:, 1, :], 0.0, ALU.mult, ALU.add).then_inc(z_small, 1)
                dve.wait_ge(z_exp, n + 1)
                dve.tensor_scalar(zrow[:, 0, :], zrow[:, 0, :], 1.0, 0.5 ** 0.5, ALU.add, ALU.mult).then_inc(z_small, 1)
                dve.wait_ge(z_small, 5 * n + 4)
                dve.tensor_scalar(mcarry[:, bass.ds(GB * g, GB)].rearrange("p (b o) -> p b o", o=1), m3(2)[:, :, P:P + 1],
                                  1.0, None, ALU.mult)
                dve.wait_ge(z_small, 5 * n + 5)
                dve.tensor_tensor(urow[0:1, :].rearrange("p (b t) -> p b t", b=GB), z3(0), RJ, ALU.mult).then_inc(u_rows, 1)
                dve.scalar_tensor_tensor(urow[32:33, :].rearrange("p (b t) -> p b t", b=GB), m3(2)[:, :, 1:P + 1], -1.0,
                                         z3(0), ALU.mult, ALU.mult).then_inc(u_rows, 1)

            def lstm_step(family, s, c, g, n):
                k = STEPS * n + s
                if family == "cell":
                    dve.wait_ge(l_tanh, k + 1)
                    dve.scalar_tensor_tensor(uprod[:, :], gates[:, 0:40], 1.0, gates[:, 60:100], ALU.add, ALU.mult).then_inc(l_u, 1)
                    dve.wait_ge(l_u, k + 1)
                    dve.scalar_tensor_tensor(gates[:, 80:100], uprod[:, 20:40], 0.5, uprod[:, 0:20], ALU.mult,
                                             ALU.add).then_inc(l_c, 1)
                    return
                dve.wait_ge(l_tc, k + 1)
                dve.scalar_tensor_tensor(hnew[0:B, 0:PE_], gates[:, 40:60], 1.0, tcell[:, :], ALU.add,
                                         ALU.mult).then_inc(l_h, 1)
                dve.wait_ge(l_h, k + 1)
                if s == STEPS - 1:
                    dve.transpose(slots[96:128, 0:2, :].rearrange("p s b -> p (s b)"), hnew[:, :])
                dve.transpose(slots[96:128, s + 1:s + 3, :].rearrange("p s b -> p (s b)"), hnew[:, :]).then_inc(l_t, 1)
                if s % 8 == 7:
                    dve.wait_ge(l_t, k + 2)
                    dve.tensor_scalar(R[96:128, :, bass.ds((c % 3) * P + STEPS * g + s - 7, 8)].rearrange("p b t -> p t b"),
                                      slots[96:128, s - 6:s + 2, :], 1.0, None, ALU.mult).then_inc(l_out, 1)

            run_stages(dve, "dve", dve_step)

        @block.gpsimd
        def _(pool):
            pool.wait_ge(prep_done, 1)

            def add_row(l, row, done):
                w = tiles[l]
                pool.tensor_tensor(w.xres[:, :, :], w.xres[:, :, :],
                                   row[:, :].rearrange("p (o d) -> p o d", o=1).broadcast_to([P, GB, D]),
                                   ALU.add).then_inc(done, 1)

            def pool_step(stream, family, i_, c, g, n):
                if stream == 2:
                    if i_ == 0:
                        pool.wait_ge(xg_ready, NG * (c + 1))
                    if positive(n):
                        pool.wait_ge(l_pe, STEPS * n - 24 + 8 * i_)
                    pool.tensor_copy(slots[0:96, 8 * i_:8 * i_ + 8, :],
                                     R[0:96, :, bass.ds((c % 3) * P + STEPS * g + 8 * i_, 8)].rearrange("p b t -> p t b")
                                     ).then_inc(l_in, 1)
                    return
                t, w = at[stream], tiles[stream]
                b, j = divmod(i_, 2)
                N = 2 * GB * n + i_
                if family == "root":
                    if i_ == 8:
                        pool.wait_ge(n_a, n + 1)
                        pool.tensor_tensor(nrm[:, 1, :], nrm[:, 0, :], neghalf[:, :], ALU.pow).then_inc(n_b, 1)
                    elif i_ == 9:
                        pool.wait_ge(ln[0].small, 11 * n + 8)
                        pool.tensor_tensor(ln[0].rstd[:, 1, :], ln[0].ve[:, 1, :], neghalf[:, :], ALU.pow).then_inc(ln[0].inv, 1)
                    else:
                        s = ln[i_]
                        pool.wait_ge(s.small, (5 if i_ else 11) * n + 5)
                        pool.tensor_tensor(s.rstd[:, 0, :], s.ve[:, 0, :], neghalf[:, :], ALU.pow).then_inc(s.inv, 1)
                elif family == "brow":
                    pool.wait_ge(base_ready, n + 1)
                    add_row(0, rowOut, f_base)
                elif family == "frow":
                    pool.wait_ge(ln[2].normed, 2 * n + 2)
                    add_row(0, rowF, f_base)
                elif family == "orow":
                    add_row(stream, rowO[stream], t.base)
                elif family == "keys":
                    if i_ == 0:
                        pool.wait_ge(t.m_load, (32 if stream == 0 else 48) * (n + 1))
                    if positive(N - 3):
                        pool.wait_ge(t.scores, N - 3)
                    pool.tensor_tensor(
                        w.kbd[b % 2][:, j, :, :], w.kg[:, j, b:b + 1, :].broadcast_to([P, NE, SK]),
                        headmask[:, :].rearrange("p (a o) -> p a o", o=1).broadcast_to([P, NE, SK]), ALU.mult
                    ).then_inc(t.kbd, 1)
                elif family == "shift":
                    ex = w.ex[b % 2][:, NE * j:NE * j + NE, :]
                    pool.wait_ge(t.top, N + 1)
                    pool.tensor_tensor(ex, ex, w.mx[:, i_ % 4, :].rearrange("p (a o) -> p a o", o=1).broadcast_to([P, NE, SK]),
                                       ALU.subtract).then_inc(t.shifted, 1)
                elif family == "gate":
                    ex = w.ex[b % 2][:, NE * j:NE * j + NE, :]
                    pool.wait_ge(t.summed, N + 1)
                    pool.tensor_tensor(ex, ex, gp[:, b:b + 1, :].broadcast_to([P, NE, SK]), ALU.mult).then_inc(t.gated, 1)
                elif family == "weight2":
                    k = positions(c, g) + i_
                    wt, sq = wT[i_ % 2], wsq[i_ % 2]
                    pool.wait_ge(pos_w, k + 1)
                    if i_ == c:
                        w3 = wt[:, :].rearrange("p (b t) -> p b t", b=GB)
                        pool.tensor_tensor(w3, w3, tri[:, :].rearrange("p (o t) -> p o t", o=1).broadcast_to([P, GB, P]),
                                           ALU.mult).then_inc(pos_m, 1)
                        pool.wait_ge(pos_m, n + 1)
                    pool.tensor_tensor(sq[:, :], wt[:, :], wt[:, :], ALU.mult).then_inc(pos_w2, 1)

            run_stages(pool, "pool", pool_step)


def _constants():
    import numpy as np
    p = np.arange(P)
    gatesel = np.zeros((80, 80), np.float32)
    for j in range(PE_):
        gatesel[j, j] = gatesel[20 + j, 20 + j] = gatesel[60 + j, 40 + j] = 0.5
        gatesel[40 + j, 60 + j] = 1.0
    posl = np.zeros((64, NC_, P), np.float32)
    posl[0] = np.arange(S).reshape(NC_, P)
    posl[32] = 1.0
    j = np.arange(1, S + 1, dtype=np.float32)
    sel = np.repeat(np.eye(NE, dtype=np.float32)[:, :, None], P, axis=2)
    return {
        "c_ident": np.eye(P, dtype=np.float32), "c_tri": (p[:, None] <= p[None, :]).astype(np.float32),
        "c_headmask": (p[:, None] // HD == np.arange(NE)[None, :]).astype(np.float32),
        "c_rank": np.tile(np.arange(NE, 0, -1, dtype=np.float32), (P, 1)),
        "c_sel": sel, "c_posl": posl, "c_jrow": np.stack([j / np.float32(S), np.float32(1.0) / j])[None],
        "c_gatesel": gatesel,
    }


def kernel(**inputs):
    import numpy as _np
    import concourse.bacc as _bacc
    from concourse import mybir as _mybir
    from concourse.bass_utils import run_bass_kernel_spmd as _run

    i = {k: _np.asarray(v) for k, v in inputs.items()}
    columns = lambda v: v.reshape(NH, P).T
    w_ih = _np.zeros((D, 96), _np.float32)
    w_ih[:, 0:80] = i["L1_attn_W_ih"].T
    w_hh = i["L1_attn_W_hh"].T[:, [*range(0, 40), *range(60, 80), *range(40, 60)]]
    b_gates = _np.zeros((96, 2), _np.float32)
    b_gates[0:80, 0], b_gates[0:80, 1], b_gates[80, 0] = i["L1_attn_b_ih"], i["L1_attn_b_hh"], 1.0
    w_mu_sig, b_mu_sig = _np.zeros((PE_, P), _np.float32), _np.zeros((1, P), _np.float32)
    w_mu_sig[:, 0:96:32], w_mu_sig[:, 96:97] = i["L1_attn_W_mu"].T, i["L1_attn_W_sig"].T
    b_mu_sig[0, 0:96:32], b_mu_sig[0, 96:97] = i["L1_attn_b_mu"], i["L1_attn_b_sig"]
    data = {
        "x": i["x"], "ctx": i["ctx_1024"].transpose(2, 0, 1), "fside": i["fside_BxSxS2_0"],
        "mask0": i["mask_BxSxS2_bf1"].view(_np.uint8), "mask1": i["mask_BxSxS2_ik1"],
        "norm_w": columns(i["L0_attn_norm_w"]), "A_w": i["L0_attn_A_w"].T, "A_b": columns(i["L0_attn_A_b"]), "B_w": i["L0_attn_B_w"].T,
        "C_w": i["L0_attn_C_w"].T, "D_w": i["L0_attn_D_w"].T, "out_w": i["L0_attn_out_w"].T, "out_b": i["L0_attn_out_b"],
        "Wq": i["L0_xattn_Wq"].T, "bq": columns(i["L0_xattn_bq"]), "Wk": i["L0_xattn_Wk"].T, "bk": columns(i["L0_xattn_bk"]),
        "Wv": i["L0_xattn_Wv"].T, "bv": i["L0_xattn_bv"], "Wo": i["L0_xattn_Wo"].T, "bo": i["L0_xattn_bo"],
        "W": i["L0_ffn_W"].T, "b": i["L0_ffn_b"], "V_r": i["L0_ffn_V_r"].T, "C": i["L0_ffn_C"].T,
        "W_ih": w_ih, "W_hh": w_hh, "b_gates": b_gates, "W_mu_sig": w_mu_sig, "b_mu_sig": b_mu_sig,
        "wq_k": i["L1_xattn_wq_k"], "wq_b": columns(i["L1_xattn_wq_b"]), "wk_k": i["L1_xattn_wk_k"], "wk_b": columns(i["L1_xattn_wk_b"]),
        "wv_k": i["L1_xattn_wv_k"], "wv_b": i["L1_xattn_wv_b"], "wo_k": i["L1_xattn_wo_k"], "wo_b": i["L1_xattn_wo_b"],
        "w_router": i["L1_ffn_w_router"].T,
        "w_fc": i["L1_ffn_w_fc"].transpose(2, 0, 1).reshape(D, NE * P),
        "w_proj": i["L1_ffn_w_proj"].transpose(2, 0, 1),
    }
    data.update(_constants())
    nc = _bacc.Bacc("TRN2", target_bir_lowering=False, num_devices=1)
    arrays, args = {}, {}
    for name, v in data.items():
        v = _np.ascontiguousarray(v)
        arrays[f"in_{name}"] = v
        args[name] = nc.dram_tensor(f"in_{name}", v.shape, _mybir.dt.from_np(v.dtype), kind="ExternalInput").ap()
    out = nc.dram_tensor("out_0", (B, S, D), F32, kind="ExternalOutput").ap()
    decoder_program(nc, args, out)
    r = _run(nc, [arrays], core_ids=[0])
    return r.results[0]["out_0"]
```

```python
from contextlib import ExitStack

import concourse.bass as bass
from concourse import mybir

ALU = mybir.AluOpType
ACT = mybir.ActivationFunctionType
F32 = mybir.dt.float32
BF16 = mybir.dt.bfloat16
AX_X = mybir.AxisListType.X

P = 128
B, S, D = 16, 512, 256
SK, H = 64, 16
GB = 4
NC_, NG = S // P, B // GB
NT = GB * P
NH = D // P
NP = H // 2
HD = D // H
PE_ = 20
NE = 8
STEPS = P // NG
EPS = 1e-5
FMAX = 3.4028234663852886e38
VW = 2 * HD + 2


LAYER0_UNITS = (12, 4)


def bodies(stage):
    return NG // 2 if stage < 2 else NG


def lane_unit(lane, stage, r):
    if stage < 2:
        return 0, stage, 2 * r + lane, 2 * stage + r, 2 * stage + r
    if lane == 0:
        return 0, stage, r, NG * (stage - 1) + r, NG * (stage - 1) + r
    return 1, stage - 2, r, NG * (stage - 2) + r, NG * (stage - 2) + LAYER0_UNITS[1] + r


def chunks_done(lane, c):
    return 2 * min(c + 1, 2) + (NG * max(c - 1, 0) if lane == 0 else 0)


LANES = [[lane_unit(lane, stage, r) for stage in range(NC_ + 2) if lane or stage < NC_ for r in range(bodies(stage))]
         for lane in range(2)]


class LayerNorm:

    def __init__(self, lane, sb, sem):
        name, self.first = f"ln{lane}", LAYER0_UNITS[lane]
        self.stats, self.mv = sb(f"{name}_stats", [P, GB, 6]), sb(f"{name}_mv", [P, GB, 2])
        self.ve, self.rstd = sb(f"{name}_ve", [P, 2, GB]), sb(f"{name}_rstd", [P, 2, GB])
        self.tmp = sb(f"{name}_tmp", [P, 4, GB])
        self.small, self.inv, self.normed = sem(f"{name}_small"), sem(f"{name}_inv"), sem(f"{name}_normed")
        self.turned, self.landed = sem(f"{name}_turned"), sem(f"{name}_landed")

    def before(self, layer, n, k):
        return 4 * n + k if layer == 0 else 4 * self.first + 2 * n + k - 4

    def before_small(self, layer, n, k):
        return 26 * n + (0, 11, 16, 21)[k] if layer == 0 else 26 * self.first + 10 * n + 5 * (k - 4)

    def before_roots(self, layer, n, k):
        return 5 * n + (0, 2, 3, 4)[k] if layer == 0 else 5 * self.first + 2 * n + k - 4


class Scan:

    def __init__(self, lane, sem):
        self.x_load, self.base_ready, self.p_ready = sem(f"x_load{lane}"), sem(f"base_ready{lane}"), sem(f"p_ready{lane}")
        self.t_act, self.u_ready, self.a_ready = sem(f"t_act{lane}"), sem(f"u_ready{lane}"), sem(f"a_ready{lane}")
        self.s_carry, self.c_ready, self.s_scan = sem(f"s_carry{lane}"), sem(f"c_ready{lane}"), sem(f"s_scan{lane}")
        self.g_ready, self.y_ready, self.x1_ready = sem(f"g_ready{lane}"), sem(f"y_ready{lane}"), sem(f"x1_ready{lane}")
        self.f_proj, self.f_base, self.x3_ready = sem(f"f_proj{lane}"), sem(f"f_base{lane}"), sem(f"x3_ready{lane}")
        self.xg_pe, self.xg_ready = sem(f"xg_pe{lane}"), sem(f"xg_ready{lane}")
        self.x3_store, self.xln_store = sem(f"x3_store{lane}"), sem(f"xln_store{lane}")


class Attention:

    def __init__(self, name, sem):
        self.q, self.q_ready, self.kbd = sem(f"{name}_q"), sem(f"{name}_q_ready"), sem(f"{name}_kbd")
        self.scores, self.masked, self.top = sem(f"{name}_scores"), sem(f"{name}_masked"), sem(f"{name}_top")
        self.shifted, self.exped, self.summed = sem(f"{name}_shifted"), sem(f"{name}_exped"), sem(f"{name}_summed")
        self.gated, self.turned, self.exT = sem(f"{name}_gated"), sem(f"{name}_turned"), sem(f"{name}_exT")
        self.pv, self.inv, self.o = sem(f"{name}_pv"), sem(f"{name}_inv"), sem(f"{name}_o")
        self.o_turned, self.oT, self.proj = sem(f"{name}_o_turned"), sem(f"{name}_oT"), sem(f"{name}_proj")
        self.base, self.done, self.v_load = sem(f"{name}_base"), sem(f"{name}_done"), sem(f"{name}_v_load")
        self.m_load, self.neg = sem(f"{name}_m_load"), sem(f"{name}_neg")


class Tiles:

    def __init__(self, name, sb):
        self.xres, self.xnat = sb(f"{name}_xres", [P, GB, D]), sb(f"{name}_xnat", [P, GB, D])
        self.xT, self.qT = sb(f"{name}_xT", [P, NH, NT]), sb(f"{name}_qT", [P, NH, NT])
        self.kg = sb(f"{name}_kg", [P, NH, GB, SK])
        self.kbd = [sb(f"{name}_kbd{i}", [P, NH, NE, SK]) for i in range(2)]
        self.vg = sb(f"{name}_vg", [P, GB, NP * VW])
        self.scratch = sb(f"{name}_scratch", [P, 3 * NH * GB * (P + 1)])
        self.ex = [self.scratch[:, i * H * SK:(i + 1) * H * SK].rearrange("p (a k) -> p a k", a=H) for i in range(2)]
        self.exT = self.scratch[:, 2 * H * SK:3 * H * SK].rearrange("p (j a t) -> p j a t", j=2, a=4)
        self.mx, self.sums, self.rs = sb(f"{name}_mx", [P, 4, NE]), sb(f"{name}_sums", [P, 4, NE]), sb(f"{name}_rs", [P, 4, NE])
        self.neg = sb(f"{name}_neg", [P, GB, SK])


def positive(value):
    return not (isinstance(value, int) and value <= 0)


def norm_steps(k, after, rms=False):
    steps = [("dve", "stat", 2 * k + h, 0.9, after[h:h + 1]) for h in range(2)]
    steps += [("pool", "root", k, 1.0, [("stat", 2 * k + 1)])]
    if rms:
        steps += [("dve", "rms", 0, 0.6, [("root", k)]), ("pool", "root", 9, 1.0, [("rms", 0)])]
    steps += [("dve", "norm", 2 * k + h, 0.65, [("root", 9 if rms else k)]) for h in range(2)]
    steps += [("pe", "turn", 2 * k + h, 0.45, [("norm", 2 * k + h)]) for h in range(2)]
    steps += [("act", "land", 2 * k + h, 0.5, [("turn", 2 * k + 1)]) for h in range(2)]
    return steps


def attention_steps(l, k, ahead=False):
    steps = [("pe", "query", h, 1.7, [("land", 2 * k + 1)]) for h in range(2)]
    steps += [("act", "qland", h, 0.6, [("query", h)]) for h in range(2)]
    steps += [("dve", "neg", 0, 0.2, [])]
    for u in range(2 * GB):
        steps += [
            ("pool", "keys", u, 1.0, [("score", u - 4)]),
            ("pe", "score", u, 0.85, [("qland", u % 2), ("keys", u), ("mask", u - 2)]),
            ("dve", "mask", u, 0.6, [("score", u), ("neg", 0), ("pturn", u - 4)] + ([("rows", 3)] if u == 0 and ahead else [])),
            ("dve", "max", u, 0.6, [("mask", u)]),
            ("pool", "shift", u, 1.0, [("max", u)]),
            ("act", "exp", u, 0.5, [("shift", u)])]
        if l == 1:
            steps += [("dve", "sums", u, 0.85, [("exp", u), ("o", u - 4)]), ("pool", "gate", u, 1.22, [("sums", u)])]
        steps += [
            ("pe", "pturn", u, 0.45, [("gate" if l else "exp", u), ("pland" if l else "o", u - 1)]),
            ("act", "pland", u, 0.5, [("pturn", u), ("pv", u - 2)]),
            ("pe", "pv", u, 0.8, [("pland", u), ("o", u - 1)]),
            ("dve", "o", u, 0.2 if l else 0.45, [("pv", u)] + ([("sums", u)] if l else []))]
    steps += [("pool", "orow", 0, 2.3, [("shift", 7)])]
    steps += [("pe", "oturn", h, 0.45, [("o", 4 * h + 3), ("mask", 7)]) for h in range(2)]
    steps += [("act", "oland", h, 0.5, [("oturn", 1)]) for h in range(2)]
    steps += [("pe", "proj", h, 1.75, [("oland", 1)]) for h in range(2)]
    steps += [("dve", "add", h, 0.65, [("proj", h), ("orow", 0)]) for h in range(2)]
    return steps


def layer0_steps():
    steps = norm_steps(0, [], rms=True)
    steps += [("dve", "base", 0, 1.4, [("rms", 0)]), ("pool", "brow", 0, 2.3, [("base", 0)]),
              ("sp", "loadx", 0, 0.1, [("base", 0), ("norm", 1)]), ("dve", "carryin", 0, 0.3, [])]
    before = [[], [], [], [("tanh", 0)], [("u", 0)], [("tanh", 1)], [("tanh", 2)], [("tanh", 3)]]
    for m in range(NH):
        for j in range(4):
            steps += [("pe", "product", 4 * m + j, 1.7, [("land", 1)] + before[4 * m + j])]
            if j != 1:
                steps += [("act", "tanh", 3 * m + max(j - 1, 0), 0.5, [("product", 4 * m + j)])]
        steps += [("dve", "u", m, 0.65, [("tanh", 3 * m), ("product", 4 * m + 1)]), ("dve", "a", m, 0.4, [("tanh", 3 * m + 1)])]
    steps += [("dve", "scan", 0, 1.15, [("a", 1), ("u", 1), ("carryin", 0)]), ("dve", "gated", 0, 1.3, [("scan", 0), ("tanh", 5)])]
    steps += [("pe", "out", h, 1.75, [("gated", 0)]) for h in range(2)]
    steps += [("dve", "x1", h, 0.65, [("out", h), ("brow", 0)]) for h in range(2)]
    steps += norm_steps(1, [("x1", 0), ("x1", 1)]) + attention_steps(0, 1)
    steps += [("sp", "loadc", 0, 0.1, [("pv", 7)])]
    steps += norm_steps(2, [("add", 0), ("add", 1)])
    steps += [("pool", "frow", 0, 2.3, [("norm", 5)])]
    steps += [("pe", "ffn", h, 1.75, [("land", 5)]) for h in range(2)]
    steps += [("dve", "x3", h, 0.65, [("ffn", h), ("frow", 0)]) for h in range(2)]
    steps += norm_steps(3, [("x3", 0), ("x3", 1)])
    steps += [("sp", "store", 0, 0.1, [("norm", 7)]),
              ("pe", "gatein", 0, 1.7, [("land", 7)]), ("act", "gatein", 1, 0.6, [("gatein", 0)])]
    return steps


def layer1_steps(c, ahead):
    steps = [("sp", "loadx3", 0, 0.1, [])]
    for i in range(c + 1):
        steps += [
            ("pe", "pos", i, 0.85, [("square", i - 1)]),
            ("act", "square", i, 0.5, [("pos", i), ("ctx", i - 2)]),
            ("act", "weight", i, 0.55, [("square", i)]),
            ("pool", "weight2", i, 1.25 if i < c else 2.6, [("weight", i)]),
            ("pe", "ctx", i, 2.6, [("weight2", i)])]
        if i >= 2:
            steps += [("sp", "history", i, 0.1, [("ctx", i - 2)])]
    steps += [("dve", "size", 0, 0.1, [("ctx", c)]), ("pool", "root", 8, 1.0, [("size", 0)])]
    steps += [("dve", "x4", h, 0.85, [("root", 8)]) for h in range(2)]
    steps += [("sp", "history", 9, 0.1, [("ctx", c)])]
    if ahead:
        steps += [("pe", "rows", 0, 0.85, [("size", 0)]), ("act", "rows", 1, 0.5, [("rows", 0)]),
                  ("dve", "rows", 2, 3.3, [("rows", 0)]), ("dve", "rows", 3, 2.3, [("rows", 2), ("rows", 1)])]
    steps += norm_steps(4, [("x4", 0), ("x4", 1)]) + attention_steps(1, 4, ahead)
    steps += [("sp", "loadc", 0, 0.1, [("gate", 7), ("pv", 7)])]
    steps += norm_steps(5, [("add", 0), ("add", 1)])
    steps += [("pe", "router", 0, 2.4, [("land", 11)]), ("dve", "router", 1, 0.4, [("router", 0)]),
              ("act", "router", 2, 0.15, [("router", 1)]), ("dve", "router", 3, 0.5, [("router", 2)]),
              ("pe", "router", 4, 0.5, [("router", 3)]), ("act", "router", 5, 0.5, [("router", 4)])]
    for e in range(NE):
        steps += [
            ("pe", "hidden", e, 1.7, [("router", 5), ("kept", e - 2)]),
            ("act", "relu", e, 0.5, [("hidden", e), ("squared", e - 2)]),
            ("dve", "leaky", e, 0.65, [("relu", e)]),
            ("pe", "select", e, 0.25, [("leaky", e)]),
            ("dve", "kept", e, 0.65, [("select", e)]),
            ("act", "squared", e, 0.55, [("kept", e), ("expert", e - 2)]),
            ("pe", "expert", e, 1.75, [("squared", e)])]
    steps += [("dve", "x6", h, 0.65, [("expert", NE - 1)]) for h in range(2)]
    steps += [("sp", "store", 0, 0.1, [("x6", 1)])]
    return steps


def lstm_steps(count):
    steps = [("pool", "slots", k, 0.55, [("gates", 8 * k - 13)]) for k in range(count // 8)]
    for s in range(count):
        steps += [("pe", "gates", s, 0.15, [("state", s - 1), ("slots", s // 8)]), ("act", "tanh", s, 0.15, [("gates", s)]),
                  ("dve", "cell", s, 0.35, [("tanh", s)]), ("act", "tcell", s, 0.15, [("cell", s)]),
                  ("dve", "state", s, 0.35 if s % 8 < 7 else 0.75, [("tcell", s)])]
    return steps


HOPS = {"pe": 0.22, "act": 0.2, "dve": 0.18, "pool": 0.1, "sp": 0.2}
PACE = {0: (0.0, 4.0, 0.4), 1: (96.0, 16.0, 0.6), 2: (128.0, 4.0, 0.3), 3: (140.0, 0.0, 0.4), 4: (112.0, -18.0, 0.35),
        5: (0.0, 22.0, 0.4)}
HALVED = ("product", "query", "out", "proj", "ffn", "hidden", "expert", "gated", "base")


IDLE, FILL, WARM = 0.3, 0.9, (0, 4, 5)


def planned(stage, ahead):
    recurrence, (spread, lead, window) = P // bodies(stage), PACE[stage]
    streams = {0: layer0_steps() if stage < NC_ else [], 1: layer1_steps(stage - 2, ahead) if stage >= 2 else layer0_steps(),
               2: lstm_steps(recurrence) if 1 <= stage <= NC_ else []}
    steps, after, last = {}, {}, {}
    for stream, found in streams.items():
        for engine, family, index, takes, needs in found:
            needs = [(stream, x[0], 2 * x[1] + 1 if x[0] in HALVED else x[1]) for x in needs if x[1] >= 0]
            halves = 2 if family in HALVED else 1
            for index in range(halves * index, halves * index + halves):
                key = (stream, family, index)
                if (stream, engine, family) in last:
                    needs = needs + [last[stream, engine, family]]
                last[stream, engine, family] = key
                steps[key] = (engine, takes / halves, needs)
    for key, (_, _, needs) in steps.items():
        for x in needs:
            after.setdefault(x, []).append(key)
    rest = {}

    def remaining(key):
        if key not in rest:
            rest[key] = steps[key][1] + HOPS[steps[key][0]] + max([remaining(x) for x in after.get(key, [])], default=0.0)
        return rest[key]

    start, end, free, order = {}, {}, {}, []
    waiting = set(steps)
    while waiting:
        best = None
        for key in waiting:
            engine, takes, needs = steps[key]
            if any(x in waiting for x in needs):
                continue
            ready = max([end[x] + (HOPS[steps[x][0]] if steps[x][0] != engine else 0.1) for x in needs], default=0.0)
            rank = remaining(key) + lead * key[0]
            if key[0] == 2:
                ready = max(ready, spread * key[2] / recurrence) if key[1] == "gates" else ready
                rank += 1000.0
            begin = max(ready, free.get(engine, 0.0))
            offer = (round(begin / window), -rank, begin, key)
            if best is None or offer < best:
                best = offer
        key = best[3]
        engine, takes, _ = steps[key]
        start[key], end[key] = best[2], best[2] + takes
        free[engine] = end[key]
        waiting.remove(key)
        order.append((engine, *key))
    kept, last = [], 0.0
    for who, *key in order:
        key = tuple(key)
        if who == "pe":
            gap = start[key] - last
            if gap > IDLE and stage in WARM:
                kept += [("pe", 3, "warm", i) for i in range(int(gap * FILL / 0.22))]
            last = end[key]
        kept.append((who, *key))
    return kept


PLANS = {(stage, ahead): planned(stage, ahead) for stage in range(NC_ + 2) for ahead in (False, True)
         if stage >= 2 or not ahead}


def positions(c, g):
    return sum(range(1, c + 1)) * NG + (c + 1) * g


def run_stages(engine, name, step, lstm_step):
    def body(stage, r, ahead=False):
        for who, stream, family, index in PLANS[stage, ahead]:
            if who == name and stream == 2:
                c, per_body = stage - 1, P // bodies(stage)
                lstm_step(family, index, c, per_body * r, P * c + per_body * r, P * c // 8 + per_body // 8 * r)
            elif who == name and family == "warm":
                step(0, stage, family, index, 0, 0, 0, 0)
            elif who == name:
                layer, c, g, n, m = lane_unit(stream, stage, r)
                if family == "rows":
                    g, n, m = g + 1, n + 1, m + 1
                step(stream, layer, family, index, c, g, n, m)

    for stage in range(2):
        body(stage, 0)
        with engine.Fori(1, bodies(stage)) as r:
            body(stage, r)
    for stage in range(2, NC_ + 2):
        for who, index in (("pe", 0), ("act", 1), ("dve", 2), ("dve", 3)):
            if who == name:
                layer, c, g, n, m = lane_unit(1, stage, 0)
                step(1, layer, "rows", index, c, g, n, m)
        if stage == 2:
            body(stage, 0, ahead=True)
        with engine.Fori(1 if stage == 2 else 0, NG - 1) as r:
            body(stage, r, ahead=True)
        body(stage, NG - 1)


def decoder_program(nc, a, out):
    ctx = ExitStack()
    with ctx:
        def sb(name, shape, dt=F32):
            return ctx.enter_context(nc.sbuf_tensor(name, shape, dt))

        def ps(name, shape, dt=F32):
            return ctx.enter_context(nc.psum_tensor(name, shape, dt))

        def sem(name):
            return ctx.enter_context(nc.semaphore(name))

        x3_dram = nc.dram_tensor("x3_dram", [B, S, D], F32, kind="Internal").ap()
        xln_dram = nc.dram_tensor("xln_dram", [B, S, D], F32, kind="Internal").ap()
        k_dram = nc.dram_tensor("k_dram", [2, P, NH, B, SK], F32, kind="Internal").ap()
        v_dram = nc.dram_tensor("v_dram", [2, B, P, NP * VW], F32, kind="Internal").ap()

        ident = sb("ident", [P, P])
        tri = sb("tri", [P, P])
        headmask = sb("headmask", [P, NE])
        rank = sb("rank", [P, NE])
        neghalf = sb("neghalf", [P, GB])
        sel = sb("sel", [NE, NE, P], BF16)

        posl = sb("posl", [64, NC_, P])
        jrow = sb("jrow", [1, 2, S])
        wA = sb("wA", [P, NH, D])
        wB = sb("wB", [P, NH, D])
        wC = sb("wC", [P, NH, D])
        wD = sb("wD", [P, NH, D])
        wOut = sb("wOut", [P, NH, D])
        wQ = [sb(f"wQ{l}", [P, NH, D]) for l in range(2)]
        wO = [sb(f"wO{l}", [P, NH, D]) for l in range(2)]
        wF = sb("wF", [P, NH, D])
        wih = sb("wih", [P, NH, 96])
        wcat = sb("wcat", [P, 80])
        wms = sb("wms", [P, P])
        wR = sb("wR", [P, NH, NE])
        wfc = sb("wfc", [P, NH, NE * P])
        wpj = sb("wpj", [P, NE, D])
        normw = sb("normw", [P, NH])
        biasA = sb("biasA", [P, NH])
        biasQ = [sb(f"biasQ{l}", [P, NH]) for l in range(2)]
        biasK = [sb(f"biasK{l}", [P, NH]) for l in range(2)]
        biasG = sb("biasG", [96, 2])
        rowOut = sb("rowOut", [P, D])
        rowO = [sb(f"rowO{l}", [P, D]) for l in range(2)]
        rowF = sb("rowF", [P, D])
        ones = sb("ones", [P, 1])
        warm = sb("warm", [P, NT], BF16)

        R = sb("R", [P, B, 3 * P])
        slots = sb("slots", [P, STEPS + 2, B])
        gates = sb("gates", [B, 5 * PE_])
        uprod = sb("uprod", [B, 2 * PE_])
        tcell = sb("tcell", [B, PE_])
        hnew = sb("hnew", [32, 32])
        carry = sb("carry", [P, NH, B])
        mcarry = sb("mcarry", [1, B])

        tiles = [Tiles(f"l{l}", sb) for l in range(2)]
        mask8 = [sb(f"mask8_{lane}", [P, GB, SK], mybir.dt.uint8) for lane in range(2)]
        sA, sU, sH = ([t.scratch[:, j * NH * GB * (P + 1):(j + 1) * NH * GB * (P + 1)].rearrange(
            "p (a t) -> p a t", t=P + 1) for t in tiles] for j in range(3))
        gp = sb("gp", [P, GB, SK])
        mask32 = sb("mask32", [P, GB, SK], mybir.dt.int32)
        xln = sb("xln", [P, 2, GB, D])
        wT = [sb(f"wT{i}", [P, NT]) for i in range(2)]
        wsq = [sb(f"wsq{i}", [P, NT]) for i in range(2)]
        xin = [sb("xin", [P, GB, D])[:, :, :], xln[:, 0, :, :]]
        tD = [sb("tD", [P, NT])[:, :], wT[0][:, :]]
        zrow = tiles[1].scratch[0:1, 0:3 * NT].rearrange("p (j n) -> p j n", j=3)
        mrow = tiles[1].scratch[0:1, 3 * NT:3 * NT + 3 * GB * (P + 1)].rearrange("p (j n) -> p j n", j=3)
        urow = sb("urow", [64, NT])
        nrm = sb("nrm", [P, 2, GB])
        lg = sb("lg", [P, 4, GB, NE])
        lmx = sb("lmx", [P, 2, GB])
        ohT = sb("ohT", [NE, NT], BF16)
        hr = [sb(f"hr{i}", [P, NT]) for i in range(2)]
        hq = [sb(f"hq{i}", [P, NT]) for i in range(2)]
        ctxA = xln[:, :, :, :].rearrange("p i b d -> p (i b d)").rearrange("p (h b k) -> p h b k", h=NH, b=B)
        kv_w = [(tiles[l].xres[:, 0:NH, :], tiles[l].xres[:, NH:2 * NH, :]) for l in range(2)]
        once = tiles[0].xnat
        sel32 = tiles[1].xnat[0:NE, :, :].rearrange("p b d -> p (b d)").rearrange("p (e m) -> p e m", e=NE)
        KT = [tiles[l].scratch[:, 0:NH * B * SK].rearrange("p (h b k) -> p h b k", h=NH, b=B) for l in range(2)]

        p0 = ps("p0", [P, 3 * NT])
        p1 = ps("p1", [P, 4 * NT])
        pg = ps("pg", [P, NT])
        pairs = [p0[:, 0:2 * NT], p1[:, 0:2 * NT]]
        pb = p0[:, 2 * NT:3 * NT]
        qb, qc = p1[:, 2 * NT:3 * NT], p1[:, 3 * NT:4 * NT]
        banks = [[p0[:, j * NT:(j + 1) * NT] for j in range(3)], [p1[:, j * NT:(j + 1) * NT] for j in range(4)]]
        t_bank, o_bank = [pb, qb], [pb, qc]

        ln = [LayerNorm(lane, sb, sem) for lane in range(2)]
        at = [Attention(f"at{i}", sem) for i in range(2)]
        w_load, prep_in, prep_pe, prep_ev, prep_v, prep_done = (
            sem(n) for n in ("w_load", "prep_in", "prep_pe", "prep_ev", "prep_v", "prep_done"))
        k_store = sem("k_store")
        v_store = [sem(f"v_store{i}") for i in range(GB)]
        wf_pe, wf_ev = sem("wf_pe"), sem("wf_ev")
        scans = [Scan(lane, sem) for lane in range(2)]
        xln_load = [sem(f"xln_load{i}") for i in range(2)]
        l_in, l_pe, l_tanh, l_u, l_c, l_tc, l_h, l_t, l_out = (
            sem(n) for n in ("l_in", "l_pe", "l_tanh", "l_u", "l_c", "l_tc", "l_h", "l_t", "l_out"))
        x3_load, z_pe, z_small, z_exp, u_rows, pos_pe, pos_sq, pos_w, pos_m, pos_w2, ctx_pe, n_a, n_b, x4_ready = (
            sem(n) for n in ("x3_load", "z_pe", "z_small", "z_exp", "u_rows",
                             "pos_pe", "pos_sq", "pos_w", "pos_m", "pos_w2", "ctx_pe", "n_a", "n_b", "x4_ready"))
        r_pe, r_small, r_exp, r_oh, oh_pe, oh_ev, fc_pe, sel_pe, fc_relu, fc_sum, fc_mask, fc_sq, moe_pe, x6_ready, o_store = (
            sem(n) for n in ("r_pe", "r_small", "r_exp", "r_oh", "oh_pe", "oh_ev", "fc_pe", "sel_pe",
                             "fc_relu", "fc_sum", "fc_mask", "fc_sq", "moe_pe", "x6_ready", "o_store"))

        halves = lambda w: w.rearrange("(h p) n -> p h n", p=P)
        unit = lambda t, c, g: t[bass.ds(GB * g, GB), c * P:(c + 1) * P, :].rearrange("b t d -> t b d")
        NLOAD = 0
        loads = [
            (ident[:, :], a["c_ident"]), (tri[:, :], a["c_tri"]), (headmask[:, :], a["c_headmask"]),
            (rank[:, :], a["c_rank"]), (sel32, a["c_sel"]), (posl[:, :, :], a["c_posl"]),
            (jrow[:, :, :], a["c_jrow"]),
            (wA[:, :, :], halves(a["A_w"])), (wB[:, :, :], halves(a["B_w"])), (wC[:, :, :], halves(a["C_w"])),
            (wD[:, :, :], halves(a["D_w"])), (wOut[:, :, :], halves(a["out_w"])),
            (wQ[0][:, :, :], halves(a["Wq"])), (wQ[1][:, :, :], halves(a["wq_k"])),
            (wO[0][:, :, :], halves(a["Wo"])), (wO[1][:, :, :], halves(a["wo_k"])),
            (wF[:, :, :], halves(a["W"])), (wR[:, :, :], halves(a["w_router"])), (wih[:, :, :], halves(a["W_ih"])), (biasG[:, :], a["b_gates"]),
            (wfc[:, :, :], halves(a["w_fc"])), (wpj[:, :, :], a["w_proj"]),
            (normw[:, :], a["norm_w"]),
            (biasA[:, :], a["A_b"]),
            (biasQ[0][:, :], a["bq"]),
            (biasQ[1][:, :], a["wq_b"]),
            (biasK[0][:, :], a["bk"]),
            (biasK[1][:, :], a["wk_b"]),
            (rowOut[:, :], a["out_b"].rearrange("(o n) -> o n", o=1).broadcast_to([P, D])),
            (rowO[0][:, :], a["bo"].rearrange("(o n) -> o n", o=1).broadcast_to([P, D])),
            (rowO[1][:, :], a["wo_b"].rearrange("(o n) -> o n", o=1).broadcast_to([P, D])),
            (rowF[:, :], a["b"].rearrange("(o n) -> o n", o=1).broadcast_to([P, D])),
            (ctxA, a["ctx"].rearrange("(h p) b k -> p h b k", p=P)),
            (kv_w[0][0], halves(a["Wk"])), (kv_w[0][1], halves(a["Wv"])),
            (kv_w[1][0], halves(a["wk_k"])), (kv_w[1][1], halves(a["wv_k"])),
            (once[:, 0, :], a["bv"].rearrange("(o n) -> o n", o=1).broadcast_to([P, D])),
            (once[:, 1, :], a["wv_b"].rearrange("(o n) -> o n", o=1).broadcast_to([P, D])),
            (once[0:32, 2, :], a["C"]), (once[0:32, 3, :], a["V_r"]),
        ]
        late_loads = [
            (wcat[0:80, :], a["c_gatesel"]), (wcat[96:116, :], a["W_hh"]),
            (wms[80:81, :], a["b_mu_sig"]), (wms[96:116, :], a["W_mu_sig"]),
        ]
        NLOAD = 16 * (len(loads) + len(late_loads))
        block = ctx.enter_context(nc.Block())


        @block.sync
        def _(sp):
            for dst, src in loads:
                sp.dma_start(dst, src).then_inc(w_load, 16)
            sp.wait_ge(prep_in, 3)
            for dst, src in late_loads:
                sp.dma_start(dst, src).then_inc(w_load, 16)
            sp.wait_ge(prep_ev, 8)
            for l in range(2):
                sp.dma_start(k_dram[l], KT[l]).then_inc(k_store, 16)
            for l in range(2):
                for b in range(B):
                    n = l * B + b
                    sp.wait_ge(prep_v, 2 * n + 2)
                    sp.dma_start(v_dram[l, b, :, :], tiles[0].vg[:, n % GB, :]).then_inc(v_store[n % GB], 16)
            sp.wait_ge(k_store, 32)
            for i in range(GB):
                sp.wait_ge(v_store[i], 16 * (2 * B // GB))
            sp.wait_ge(prep_done, 1)

            def load_x(lane, c, g, n):
                l0 = scans[lane]
                if n:
                    sp.wait_ge(l0.base_ready, n)
                    sp.wait_ge(ln[lane].normed, 2 * ln[lane].before(0, n, 0) - 6)
                sp.dma_start(xin[lane], unit(a["x"], c, g)).then_inc(l0.x_load, 16)

            def load_context(lane, layer, c, g, m):
                t, w = at[lane], tiles[lane]
                if m:
                    sp.wait_ge(t.kbd, 2 * GB * m)
                    sp.wait_ge(t.pv, 2 * GB * m)
                    sp.wait_ge(t.neg, m)
                    if layer == 1 and m > LAYER0_UNITS[lane]:
                        sp.wait_ge(t.gated, 2 * GB * (m - LAYER0_UNITS[lane]))
                sp.dma_start(w.vg[:, :, :], v_dram[layer, bass.ds(GB * g, GB), :, :].rearrange("b p n -> p b n")
                             ).then_inc(t.v_load, 16)
                sp.dma_start(w.kg[:, :, :, :], k_dram[layer, :, :, bass.ds(GB * g, GB), :]).then_inc(t.m_load, 16)
                if layer == 0:
                    sp.dma_start(mask8[lane][:, :, :], unit(a["mask0"], c, g)).then_inc(t.m_load, 16)
                else:
                    sp.dma_start(mask32[:, :, :], unit(a["mask1"], c, g)).then_inc(t.m_load, 16)
                    sp.dma_start(gp[:, :, :], unit(a["fside"], c, g)).then_inc(t.m_load, 16)

            def load_history(i, c, g, n):
                used = positions(c, g) + (i - 1 if i >= 2 else 0)
                for lane in range(2):
                    sp.wait_ge(scans[lane].xln_store, 16 * chunks_done(lane, c))
                if n == 0:
                    sp.wait_ge(scans[1].base_ready, LAYER0_UNITS[1])
                    sp.wait_ge(ln[1].normed, 2 * ln[1].before(1, 0, 4))
                if positive(used):
                    sp.wait_ge(ctx_pe, used)
                sp.dma_start(xln[:, i % 2, :, :], unit(xln_dram, i, g)).then_inc(xln_load[i % 2], 16)

            def sp_step(lane, layer, family, index, c, g, n, m):
                l0 = scans[lane]
                later = LANES[lane][m + 1] if m + 1 < len(LANES[lane]) else None
                if family == "store" and layer == 0:
                    sp.wait_ge(ln[lane].normed, 2 * ln[lane].before(0, n, 4))
                    sp.dma_start(unit(xln_dram, c, g), tiles[lane].xnat[:, :, :]).then_inc(l0.xln_store, 16)
                    sp.dma_start(unit(x3_dram, c, g), tiles[lane].xres[:, :, :]).then_inc(l0.x3_store, 16)
                elif family == "store":
                    sp.wait_ge(x6_ready, 2 * n + 2)
                    sp.dma_start(unit(out, c, g), tiles[1].xres[:, :, :]).then_inc(o_store, 16)
                elif family == "loadx3":
                    if positive(n):
                        sp.wait_ge(o_store, 16 * n)
                    for k in range(2):
                        sp.wait_ge(scans[k].x3_store, 16 * (LAYER0_UNITS[k] if k else chunks_done(k, c)))
                    sp.dma_start(tiles[1].xres[:, :, :], unit(x3_dram, c, g)).then_inc(x3_load, 16)
                elif family == "history" and index < NC_:
                    load_history(index, c, g, n)
                elif later is None:
                    return
                elif family == "loadx" and later[0] == 0:
                    load_x(lane, *later[1:4])
                elif family == "loadc":
                    load_context(lane, later[0], later[1], later[2], m + 1)
                else:
                    for i in range(min(2, later[1] + 1)):
                        load_history(i, *later[1:4])

            for lane in range(2):
                load_x(lane, 0, lane, 0)
                load_context(lane, 0, 0, lane, 0)
            for stage in range(NC_ + 2):
                for r in range(bodies(stage)):
                    for who, lane, family, index in PLANS[stage, stage >= 2 and r < NG - 1]:
                        if who == "sp":
                            layer, c, g, n, m = lane_unit(lane, stage, r)
                            sp_step(lane, layer, family, index, c, g, n, m)
            sp.wait_ge(o_store, 16 * NC_ * NG)

        @block.tensor
        def _(pe):
            pe.wait_ge(w_load, NLOAD)
            for h in range(NH):
                i = pe.matmul(banks[0][0][:, h * D:(h + 1) * D], once[0:32, 3, h * P:(h + 1) * P], once[0:32, 2, :],
                              start=True, stop=True)
            i.then_inc(wf_pe, 1)
            n = 0
            for l in range(2):
                for m in range(NH):
                    for j in range(2):
                        if n >= 2:
                            pe.wait_ge(prep_ev, n - 1)
                        for k in range(NH):
                            i = pe.matmul(banks[1][n % 2], kv_w[l][0][:, k, m * P:(m + 1) * P],
                                          ctxA[:, k, 8 * j:8 * j + 8, :].rearrange("p b k -> p (b k)"),
                                          start=(k == 0), stop=(k == NH - 1))
                        i.then_inc(prep_pe, 1)
                        n += 1
            pe.wait_ge(prep_ev, n)
            for l in range(2):
                for b in range(B):
                    v = l * B + b
                    if v >= 2:
                        pe.wait_ge(prep_v, 2 * v - 2)
                    for e in range(2):
                        for k in range(NH):
                            i = pe.matmul(banks[1][v % 2][64 * e:64 * e + 64, 0:D], ctxA[:, k, b, :], kv_w[l][1][:, k, :],
                                          start=(k == 0), stop=(k == NH - 1))
                    i.then_inc(prep_pe, 1)
            pe.wait_ge(prep_done, 1)

            def turn(l, h, src, done):
                for m in range(NH):
                    for b in (2 * h, 2 * h + 1):
                        i = pe.transpose(banks[l][m][:, b * P:(b + 1) * P], src[:, b, m * P:(m + 1) * P], ident[:, :])
                i.then_inc(done, 1)

            def project(l, b, x, w, done):
                for k in range(NH):
                    i = pe.matmul(pairs[l][:, b * D:(b + 1) * D], x[:, k, b * P:(b + 1) * P], w[:, k, :],
                                  start=(k == 0), stop=(k == NH - 1))
                if b % 2:
                    i.then_inc(done, 1)

            def attention_step(l, layer, family, i_, n, m):
                t, w = at[l], tiles[l]
                if family == "query":
                    half, k = divmod(i_, 2)
                    if i_ == 0:
                        pe.wait_ge(ln[l].landed, 2 * ln[l].before(layer, n, (1, 4)[layer]) + 2)
                    i = pe.matmul(banks[l][2 - half], wQ[layer][:, k, half * P:(half + 1) * P], w.xT[:, k, :],
                                  start=(k == 0), stop=(k == NH - 1))
                    if k:
                        i.then_inc(t.q, 1)
                    return
                if family == "oturn":
                    pe.wait_ge(t.o, 2 * GB * m + GB * i_ + GB)
                    if i_ == 0:
                        pe.wait_ge(t.masked, 2 * GB * m + 2 * GB)
                    turn(l, i_, w.xnat, t.o_turned)
                    return
                if family == "proj":
                    pe.wait_ge(t.oT, 2 * m + 2)
                    project(l, i_, w.xT, wO[layer], t.proj)
                    return
                u, (b, j), N = i_, divmod(i_, 2), 2 * GB * m + i_
                if family == "score":
                    if u < 2:
                        pe.wait_ge(t.q_ready, 2 * m + u + 1)
                    else:
                        pe.wait_ge(t.masked, N - 1)
                    pe.wait_ge(t.kbd, N + 1)
                    pe.matmul(banks[l][j], w.qT[:, j, b * P:(b + 1) * P],
                              w.kbd[b % 2][:, j, :, :].rearrange("p a k -> p (a k)"), start=True, stop=True
                              ).then_inc(t.scores, 1)
                elif family == "pturn":
                    if layer == 0:
                        pe.wait_ge(t.exped, N + 1)
                    else:
                        pe.wait_ge(t.gated, 2 * GB * n + i_ + 1)
                    if u and l == 0:
                        pe.wait_ge(t.o, N)
                    elif u:
                        pe.wait_ge(t.exT, N)
                    for p in range(4):
                        src = w.ex[b % 2][:, 8 * j + 2 * p:8 * j + 2 * p + 2, :].rearrange("p a k -> p (a k)")
                        i = pe.transpose(t_bank[l][:, p * P:(p + 1) * P], src, ident[:, :])
                    i.then_inc(t.turned, 1)
                elif family == "pv":
                    if u == 0:
                        pe.wait_ge(t.v_load, 16 * m + 16)
                    elif l == 1:
                        pe.wait_ge(t.o, N)
                    pe.wait_ge(t.exT, N + 1)
                    for p in range(4):
                        q = 4 * j + p
                        i = pe.matmul(o_bank[l][:, q * VW:(q + 1) * VW], w.exT[:, j, p, :], w.vg[:, b, q * VW:(q + 1) * VW],
                                      start=True, stop=True)
                    i.then_inc(t.pv, 1)

            def pe_lstm(family, s, c, time, k, pieces):
                if s % 8 == 0:
                    pe.wait_ge(l_in, pieces + s // 8 + 1)
                pe.wait_ge(l_t, k + s + 1)
                pe.matmul(pg[0:B, 0:80], slots[:, s % STEPS, :], wcat[:, :], start=True, stop=True).then_inc(l_pe, 1)

            def pe_step(lane, layer, family, i_, c, g, n, m):
                l0 = scans[lane]
                if family in ("query", "score", "pturn", "pv", "oturn", "proj"):
                    attention_step(lane, layer, family, i_, n, m)
                elif family == "warm":
                    pe.matmul(pg[:, :] if layer == 0 else banks[0][0], warm[:, 0:P], warm[:, :], start=True, stop=True)
                elif family == "turn":
                    k, h = divmod(i_, 2)
                    pe.wait_ge(ln[lane].normed, 2 * ln[lane].before(layer, n, k) + h + 1)
                    turn(lane, h, tiles[lane].xnat, ln[lane].turned)
                elif family == "product":
                    i_, k = divmod(i_, 2)
                    half, j = divmod(i_, 4)
                    if k:
                        pass
                    elif i_ == 0:
                        pe.wait_ge(ln[lane].landed, 2 * ln[lane].before(0, n, 0) + 2)
                        if positive(n):
                            pe.wait_ge(l0.xg_ready, n)
                    elif i_ == 4:
                        pe.wait_ge(l0.u_ready, 2 * n + 1)
                    elif i_ >= 3:
                        pe.wait_ge(l0.t_act, 6 * n + max(i_ - 3, 1))
                    w = (wD, wB, wA, wC)[j]
                    bank = banks[lane][(0, 1, 2, 0, 1, 2, 0, 1)[i_]]
                    i = pe.matmul(bank, w[:, k, half * P:(half + 1) * P], tiles[lane].xT[:, k, :],
                                  start=(k == 0), stop=(k == NH - 1))
                    if k:
                        i.then_inc(l0.p_ready, 1)
                elif family == "out":
                    pe.wait_ge(l0.g_ready, n + 1)
                    project(lane, i_, tiles[lane].qT, wOut, l0.y_ready)
                elif family == "ffn":
                    pe.wait_ge(ln[lane].landed, 2 * ln[lane].before(0, n, 2) + 2)
                    project(lane, i_, tiles[lane].xT, wF, l0.f_proj)
                elif family == "gatein":
                    pe.wait_ge(ln[lane].landed, 2 * ln[lane].before(0, n, 3) + 2)
                    for k in range(NH):
                        i = pe.matmul(banks[lane][2][0:96, :], wih[:, k, :], tiles[lane].xT[:, k, :], start=(k == 0), stop=(k == NH - 1))
                    i.then_inc(l0.xg_pe, 1)
                elif family == "rows":
                    pe.wait_ge(l_out, 4 * NG * (c + 1))
                    if positive(n):
                        pe.wait_ge(n_a, n)
                    pe.matmul(qc, wms[:, :], R[:, bass.ds(GB * g, GB), (c % 3) * P:(c % 3 + 1) * P],
                              start=True, stop=True).then_inc(z_pe, 1)
                elif family == "pos":
                    if i_ == 0:
                        pe.wait_ge(u_rows, 2 * n + 2)
                    else:
                        pe.wait_ge(pos_sq, positions(c, g) + i_)
                    pe.matmul(qb, posl[:, i_, :], urow[:, :], start=True, stop=True).then_inc(pos_pe, 1)
                elif family == "ctx":
                    if i_ == 0 and positive(n):
                        pe.wait_ge(x6_ready, 2 * n)
                    pe.wait_ge(pos_w2, positions(c, g) + i_ + 1)
                    even, odd = c // 2 + 1, (c + 1) // 2
                    loaded = [sum(k // 2 + 1 for k in range(c)) * NG + even * g,
                              sum((k + 1) // 2 for k in range(c)) * NG + odd * g][i_ % 2] + i_ // 2 + 1
                    pe.wait_ge(xln_load[i_ % 2], 16 * loaded)
                    for b in range(GB):
                        pe.matmul(pairs[1][:, b * D:(b + 1) * D], wT[i_ % 2][:, b * P:(b + 1) * P], xln[:, i_ % 2, b, :],
                                  start=(i_ == 0 and b % 2 == 0), stop=(i_ == c), skip_group_check=True)
                    for b in range(GB):
                        i = pe.matmul(qc[:, b:b + 1], wsq[i_ % 2][:, b * P:(b + 1) * P], ones[:, :],
                                      start=(i_ == 0 and b == 0), stop=(i_ == c), skip_group_check=True)
                    i.then_inc(ctx_pe, 1)
                elif family == "router" and i_ == 0:
                    pe.wait_ge(ln[lane].landed, 2 * ln[lane].before(1, n, 5) + 2)
                    for b in range(GB):
                        for k in range(NH):
                            i = pe.matmul(qc[:, b * NE:(b + 1) * NE], tiles[1].xT[:, k, b * P:(b + 1) * P], wR[:, k, :],
                                          start=(k == 0), stop=(k == NH - 1))
                    i.then_inc(r_pe, 1)
                elif family == "router":
                    pe.wait_ge(r_oh, n + 1)
                    for b in range(GB):
                        i = pe.transpose(qb[0:NE, b * P:(b + 1) * P], lg[:, 3, b, :], ident[:, :])
                    i.then_inc(oh_pe, 1)
                elif family == "hidden":
                    i_, k = divmod(i_, 2)
                    if k == 0 and i_ == 0:
                        pe.wait_ge(oh_ev, n + 1)
                    elif k == 0 and i_ >= 2:
                        pe.wait_ge(fc_mask, NE * n + i_ - 1)
                    i = pe.matmul(banks[1][2 + i_ % 2], wfc[:, k, i_ * P:(i_ + 1) * P], tiles[1].xT[:, k, :],
                                  start=(k == 0), stop=(k == NH - 1))
                    if k:
                        i.then_inc(fc_pe, 1)
                elif family == "select":
                    pe.wait_ge(fc_sum, NE * n + i_ + 1)
                    pe.matmul(banks[1][2 + i_ % 2], sel[:, i_, :], ohT[:, :], start=True, stop=True).then_inc(sel_pe, 1)
                elif family == "expert":
                    i_, half = divmod(i_, 2)
                    if half == 0:
                        pe.wait_ge(fc_sq, NE * n + i_ + 1)
                    for b in (2 * half, 2 * half + 1):
                        i = pe.matmul(pairs[1][:, b * D:(b + 1) * D], hq[i_ % 2][:, b * P:(b + 1) * P], wpj[:, i_, :],
                                      start=(i_ == 0 and b % 2 == 0), stop=(i_ == NE - 1), skip_group_check=True)
                    if half:
                        i.then_inc(moe_pe, 1)

            run_stages(pe, "pe", pe_step, pe_lstm)

        @block.scalar
        def _(act):
            act.wait_ge(w_load, NLOAD)
            n = 0
            for l in range(2):
                for m in range(NH):
                    for j in range(2):
                        act.wait_ge(prep_pe, n + 1)
                        act.activation(KT[l][:, m, 8 * j:8 * j + 8, :].rearrange("p b k -> p (b k)"),
                                       banks[1][n % 2], ACT.Identity,
                                       bias=biasK[l][:, m:m + 1]).then_inc(prep_ev, 1)
                        n += 1
            act.wait_ge(prep_done, 1)

            def act_lstm(family, s, c, time, k, pieces):
                if family == "tanh":
                    act.wait_ge(l_pe, k + s + 1)
                    act.activation(gates[:, 0:80], pg[0:B, 0:80], ACT.Tanh).then_inc(l_tanh, 1)
                else:
                    act.wait_ge(l_c, k + s + 1)
                    act.activation(tcell[:, :], gates[:, 80:100], ACT.Tanh, scale=0.5).then_inc(l_tc, 1)

            def act_step(lane, layer, family, i_, c, g, n, m):
                t, w, l0 = at[lane], tiles[lane], scans[lane]
                if family == "land":
                    k, h = divmod(i_, 2)
                    if h == 0:
                        act.wait_ge(ln[lane].turned, 2 * ln[lane].before(layer, n, k) + 2)
                    act.activation(w.xT[:, h, :], banks[lane][h], ACT.Identity).then_inc(ln[lane].landed, 1)
                elif family == "oland":
                    if i_ == 0:
                        act.wait_ge(t.o_turned, 2 * m + 2)
                    act.activation(w.xT[:, i_, :], banks[lane][i_], ACT.Identity).then_inc(t.oT, 1)
                elif family == "qland":
                    act.wait_ge(t.q, 2 * m + i_ + 1)
                    act.activation(w.qT[:, i_, :], banks[lane][2 - i_], ACT.Identity,
                                   bias=biasQ[layer][:, i_:i_ + 1], scale=0.25).then_inc(t.q_ready, 1)
                elif family == "exp":
                    b, j = divmod(i_, 2)
                    act.wait_ge(t.shifted, 2 * GB * m + i_ + 1)
                    ex = w.ex[b % 2][:, NE * j:NE * j + NE, :]
                    act.activation(ex, ex, ACT.Exp).then_inc(t.exped, 1)
                elif family == "pland":
                    act.wait_ge(t.turned, 2 * GB * m + i_ + 1)
                    if i_ >= 2:
                        act.wait_ge(t.pv, 2 * GB * m + i_ - 1)
                    act.activation(w.exT[:, i_ % 2, :, :], t_bank[lane].rearrange("p (a t) -> p a t", a=4),
                                   ACT.Identity).then_inc(t.exT, 1)
                elif family == "tanh":
                    half, j = divmod(i_, 3)
                    bank = banks[lane][(0, 2, 0, 1, 0, 1)[i_]]
                    act.wait_ge(l0.p_ready, 8 * n + 4 * half + (1, 3, 4)[j])
                    if j == 0:
                        act.activation(tD[lane], bank, ACT.Tanh, scale=0.5).then_inc(l0.t_act, 1)
                    elif j == 1:
                        act.activation(sA[lane][:, GB * half:GB * half + GB, 1:P + 1], bank.rearrange("p (b t) -> p b t", b=GB),
                                       ACT.Tanh, bias=biasA[:, half:half + 1], scale=0.5).then_inc(l0.t_act, 1)
                    else:
                        act.activation(w.qT[:, half, :], bank, ACT.Tanh, scale=0.5).then_inc(l0.t_act, 1)
                elif family == "gatein":
                    act.wait_ge(l0.xg_pe, n + 1)
                    if c == 3:
                        act.wait_ge(z_pe, NG)
                    act.activation(R[0:96, bass.ds(GB * g, GB), (c % 3) * P:(c % 3 + 1) * P],
                                   banks[lane][2][0:96, :].rearrange("p (b t) -> p b t", b=GB), ACT.Identity,
                                   bias=biasG[:, 0:1]).then_inc(l0.xg_ready, 1)
                elif family == "rows":
                    act.wait_ge(z_pe, n + 1)
                    act.activation(zrow[:, 0, :], qc[96:97, :], ACT.Exp, scale=-1.0).then_inc(z_exp, 1)
                elif family == "square":
                    act.wait_ge(pos_pe, positions(c, g) + i_ + 1)
                    if i_ >= 2:
                        act.wait_ge(ctx_pe, positions(c, g) + i_ - 1)
                    act.activation(wT[i_ % 2][:, :], qb, ACT.Square).then_inc(pos_sq, 1)
                elif family == "weight":
                    act.wait_ge(pos_sq, positions(c, g) + i_ + 1)
                    act.activation(wT[i_ % 2][:, :], wT[i_ % 2][:, :], ACT.Exp, scale=-1.0).then_inc(pos_w, 1)
                elif family == "router" and i_ == 2:
                    act.wait_ge(r_small, 4 * n + 2)
                    act.activation(lg[:, 1, :, :], lg[:, 0, :, :], ACT.Exp).then_inc(r_exp, 1)
                elif family == "router":
                    act.wait_ge(oh_pe, n + 1)
                    act.activation(ohT[:, :], qb[0:NE, :], ACT.Identity).then_inc(oh_ev, 1)
                elif family == "relu":
                    act.wait_ge(fc_pe, NE * n + i_ + 1)
                    if i_ >= 2:
                        act.wait_ge(fc_sq, NE * n + i_ - 1)
                    act.activation(hr[i_ % 2][:, :], banks[1][2 + i_ % 2], ACT.Relu).then_inc(fc_relu, 1)
                elif family == "squared":
                    act.wait_ge(fc_mask, NE * n + i_ + 1)
                    if i_ >= 2:
                        act.wait_ge(moe_pe, NE * n + i_ - 1)
                    act.activation(hq[i_ % 2][:, :], hr[i_ % 2][:, :], ACT.Square).then_inc(fc_sq, 1)

            run_stages(act, "act", act_step, act_lstm)

        @block.vector
        def _(dve):
            vg = tiles[0].vg
            dve.memset(wcat[:, :], 0.0).then_inc(prep_in, 1)
            dve.memset(wms[:, :], 0.0)
            dve.memset(neghalf[:, :], -0.5)
            dve.memset(ones[:, :], 1.0)
            dve.memset(warm[:, :], 1.0)
            dve.memset(carry[:, :, :], 0.0)
            dve.memset(mcarry[:, :], 0.0)
            dve.memset(urow[:, :], 0.0)
            dve.memset(hnew[:, :], 0.0)
            dve.memset(gates[:, :], 0.0)
            dve.memset(slots[:, :, :], 0.0)
            dve.memset(R[64:128, :, :], 0.0)
            dve.memset(vg[:, :, :], 0.0).then_inc(prep_in, 1)
            dve.wait_ge(prep_in, 2)
            for b in range(GB):
                vb = vg[:, b, :].rearrange("p (q w) -> p q w", w=VW)
                dve.memset(vb[0:64, :, 2 * HD:2 * HD + 1], 1.0)
                i = dve.memset(vb[64:128, :, 2 * HD + 1:VW], 1.0)
            i.then_inc(prep_in, 1)
            dve.wait_ge(w_load, NLOAD)
            for w in (wA, wB, wC, wD):
                for h in range(NH):
                    dve.tensor_scalar(w[:, h, :], w[:, h, :], normw[:, h:h + 1], None, ALU.mult)
            dve.tensor_scalar(wOut[:, :, :], wOut[:, :, :], 0.25, None, ALU.mult)
            dve.tensor_copy(sel[:, :, :], sel32)
            dve.tensor_scalar(biasA[:, :], biasA[:, :], 0.5, None, ALU.mult)
            dve.tensor_scalar(biasQ[0][:, :], biasQ[0][:, :], 0.25, None, ALU.mult)
            dve.tensor_scalar(biasQ[1][:, :], biasQ[1][:, :], 0.25, None, ALU.mult)
            dve.tensor_scalar(wcat[96:128, 0:60], wcat[96:128, 0:60], 0.25, None, ALU.mult)
            dve.tensor_scalar(wcat[96:128, 60:80], wcat[96:128, 60:80], 0.5, None, ALU.mult)
            dve.tensor_scalar(wms[96:128, :], wms[96:128, :], 0.5, None, ALU.mult)
            dve.tensor_scalar(wpj[:, :, :], wpj[:, :, :], 0.25, None, ALU.mult)
            dve.tensor_tensor(biasG[:, 0:1], biasG[:, 0:1], biasG[:, 1:2], ALU.add)
            dve.wait_ge(wf_pe, 1)
            dve.tensor_tensor(wF[:, :, :], banks[0][0][:, 0:NH * D].rearrange("p (h n) -> p h n", h=NH), wF[:, :, :],
                              ALU.add).then_inc(wf_ev, 1)
            for l in range(2):
                for b in range(B):
                    v = l * B + b
                    dve.wait_ge(prep_pe, 8 + v + 1)
                    if v >= GB:
                        dve.wait_ge(v_store[v % GB], 16 * (v // GB))
                    vb = vg[:, v % GB, :].rearrange("p (q w) -> p q w", w=VW)
                    bank = banks[1][v % 2]
                    for e in range(2):
                        r = slice(64 * e, 64 * e + 64)
                        dve.tensor_tensor(
                            vb[r, :, e * HD:(e + 1) * HD],
                            bank[r, 0:D].rearrange("p (q e w) -> p q e w", e=2, w=HD)[:, :, e, :],
                            once[r, l, :].rearrange("p (q e w) -> p q e w", e=2, w=HD)[:, :, e, :],
                            ALU.add).then_inc(prep_v, 1)
            dve.wait_ge(prep_ev, 8)
            dve.wait_ge(k_store, 32)
            dve.wait_ge(prep_v, 4 * B)
            dve.wait_ge(wf_ev, 1)
            dve.transpose(slots[96:128, 0:2, :].rearrange("p s b -> p (s b)"), hnew[:, :]).then_inc(l_t, 1)
            dve.memset(tiles[0].sums[:, 0, :], 0.0).then_inc(prep_done, 1)

            def statistics(s, h, small, src):
                for b in (2 * h, 2 * h + 1):
                    i = dve.bn_stats(s.stats[:, b, :], src[:, b, :])
                i.then_inc(s.small, 1)
                dve.wait_ge(s.small, small + 2 * h + 1)
                dve.memset(s.tmp[:, 0, h:h + 1], 0.0)
                for b in (2 * h, 2 * h + 1):
                    i = dve.bn_aggr(s.mv[:, b, :], s.stats[:, b, :])
                i.then_inc(s.small, 1)
                if h:
                    dve.wait_ge(s.small, small + 4)
                    dve.tensor_scalar(s.ve[:, 0, :], s.mv[:, :, 1], EPS, None, ALU.add).then_inc(s.small, 1)

            def rms(s, small, roots):
                dve.wait_ge(s.inv, roots + 1)
                dve.tensor_tensor(s.tmp[:, 0, :], s.rstd[:, 0, :], s.rstd[:, 0, :], ALU.mult).then_inc(s.small, 1)
                dve.wait_ge(s.small, small + 6)
                dve.tensor_tensor(s.tmp[:, 1, :], s.tmp[:, 0, :], s.mv[:, :, 1], ALU.mult).then_inc(s.small, 1)
                dve.wait_ge(s.small, small + 7)
                dve.tensor_scalar(s.ve[:, 1, :], s.tmp[:, 1, :], EPS, None, ALU.add).then_inc(s.small, 1)
                dve.tensor_tensor(s.tmp[:, 2, :], s.mv[:, :, 0], s.rstd[:, 0, :], ALU.mult).then_inc(s.small, 1)
                dve.tensor_scalar(s.tmp[:, 0, :], s.rstd[:, 0, :], 1.0, None, ALU.add).then_inc(s.small, 1)

            def normalise(s, h, scale, src, dst):
                for b in (2 * h, 2 * h + 1):
                    i = dve.tensor_scalar(dst[:, b, :], src[:, b, :], s.mv[:, b, 0:1], scale[:, b:b + 1],
                                          ALU.subtract, ALU.mult)
                i.then_inc(s.normed, 1)

            def add_product(l, h, done):
                x = tiles[l].xres[:, 2 * h:2 * h + 2, :]
                dve.tensor_tensor(x, banks[l][h].rearrange("p (b d) -> p b d", b=2), x, ALU.add).then_inc(done, 1)

            def attention_step(l, layer, family, i_, n, m):
                t, w = at[l], tiles[l]
                u, (b, j), N = i_, divmod(i_, 2), 2 * GB * m + i_
                heads = slice(NE * j, NE * j + NE)
                if family == "neg":
                    if layer == 0:
                        dve.wait_ge(t.m_load, 32 * n + 32)
                        dve.tensor_scalar(w.neg[:, :, :], mask8[l][:, :, :], 1.0, FMAX, ALU.subtract, ALU.mult).then_inc(t.neg, 1)
                    else:
                        dve.wait_ge(t.m_load, 32 * LAYER0_UNITS[l] + 48 * n + 48)
                        dve.tensor_scalar(w.neg[:, :, :], mask32[:, :, :], 1.0, 1e9, ALU.subtract, ALU.mult).then_inc(t.neg, 1)
                elif family == "mask":
                    if u == 0:
                        dve.wait_ge(t.neg, m + 1)
                    if u >= 4:
                        dve.wait_ge(t.turned, N - 3)
                    dve.wait_ge(t.scores, N + 1)
                    dve.tensor_tensor(w.ex[b % 2][:, heads, :], banks[l][j].rearrange("p (a k) -> p a k", a=NE),
                                      w.neg[:, b:b + 1, :].broadcast_to([P, NE, SK]), ALU.add).then_inc(t.masked, 1)
                elif family == "max":
                    dve.wait_ge(t.masked, N + 1)
                    dve.tensor_reduce(w.mx[:, u % 4, :], w.ex[b % 2][:, heads, :], AX_X, ALU.max).then_inc(t.top, 1)
                elif family == "sums":
                    dve.wait_ge(t.exped, N + 1)
                    dve.tensor_reduce(w.sums[:, u % 4, :], w.ex[b % 2][:, heads, :], AX_X, ALU.add).then_inc(t.summed, 1)
                    dve.wait_ge(t.summed, 2 * GB * n + i_ + 1)
                    dve.reciprocal(w.rs[:, u % 4, :], w.sums[:, u % 4, :]).then_inc(t.inv, 1)
                elif family == "o":
                    o = o_bank[l][:, 4 * j * VW:4 * (j + 1) * VW].rearrange("p (q w) -> p q w", w=VW)
                    rs = w.rs[:, u % 4, :].rearrange("p (q e) -> p q e", e=2)
                    dve.wait_ge(t.pv, N + 1)
                    if layer == 0:
                        dve.reciprocal(rs, o[:, :, 2 * HD:VW]).then_inc(t.inv, 1)
                    dve.wait_ge(t.inv, N + 1)
                    dve.tensor_tensor(
                        w.xnat[:, b, j * P:(j + 1) * P].rearrange("p (q e w) -> p q e w", e=2, w=HD),
                        o[:, :, 0:2 * HD].rearrange("p q (e w) -> p q e w", e=2),
                        w.rs[:, u % 4, :].rearrange("p (q e o) -> p q e o", e=2, o=1).broadcast_to([P, 4, 2, HD]),
                        ALU.mult).then_inc(t.o, 1)
                elif family == "add":
                    dve.wait_ge(t.proj, 2 * m + i_ + 1)
                    if i_ == 0:
                        dve.wait_ge(t.base, m + 1)
                    add_product(l, i_, t.done)

            def dve_step(lane, layer, family, i_, c, g, n, m):
                s, l0, w = ln[lane], scans[lane], tiles[lane]
                if family in ("neg", "mask", "max", "sums", "o", "add"):
                    attention_step(lane, layer, family, i_, n, m)
                elif family == "stat":
                    k, h = divmod(i_, 2)
                    small = s.before_small(layer, n, k)
                    if k == 0:
                        if h == 0:
                            dve.wait_ge(l0.x_load, 16 * n + 16)
                        statistics(s, h, small, xin[lane])
                    else:
                        ready = (None, l0.x1_ready, at[lane].done, l0.x3_ready, x4_ready, at[lane].done)[k]
                        dve.wait_ge(ready, 2 * (m if k in (2, 5) else n) + h + 1)
                        statistics(s, h, small, w.xres)
                elif family == "rms":
                    rms(s, s.before_small(0, n, 0), s.before_roots(0, n, 0))
                elif family == "norm":
                    k, h = divmod(i_, 2)
                    if k:
                        if h == 0:
                            dve.wait_ge(s.inv, s.before_roots(layer, n, k) + 1)
                        normalise(s, h, s.rstd[:, 0, :], w.xres, w.xnat)
                        return
                    if h == 0:
                        dve.wait_ge(s.inv, s.before_roots(0, n, 0) + 2)
                        dve.tensor_tensor(s.tmp[:, 1, :], s.rstd[:, 0, :], s.rstd[:, 1, :], ALU.mult).then_inc(s.small, 1)
                        if positive(n):
                            dve.wait_ge(l0.xln_store, 16 * n)
                            dve.wait_ge(s.turned, 2 * s.before(0, n, 0))
                        dve.wait_ge(s.small, s.before_small(0, n, 0) + 11)
                    normalise(s, h, s.tmp[:, 1, :], xin[lane], w.xnat)
                elif family == "base":
                    if i_ == 0:
                        if positive(n):
                            dve.wait_ge(l0.x3_store, 16 * n)
                        dve.wait_ge(s.small, s.before_small(0, n, 0) + 10)
                    for b in (2 * i_, 2 * i_ + 1):
                        i = dve.tensor_scalar(w.xres[:, b, :], xin[lane][:, b, :], s.tmp[:, 0, b:b + 1], s.tmp[:, 2, b:b + 1],
                                              ALU.mult, ALU.subtract)
                    if i_:
                        i.then_inc(l0.base_ready, 1)
                elif family == "carryin":
                    dve.memset(sA[lane][:, :, 0:1], 0.0)
                    for half in range(NH):
                        i = dve.tensor_scalar(sU[lane][:, GB * half:GB * half + GB, 0:1],
                                              carry[:, half, bass.ds(GB * g, GB)].rearrange("p (b o) -> p b o", o=1),
                                              1.0, None, ALU.mult)
                    i.then_inc(l0.s_carry, 1)
                elif family == "u":
                    dve.wait_ge(l0.p_ready, 8 * n + 4 * i_ + 2)
                    dve.wait_ge(l0.t_act, 6 * n + 3 * i_ + 1)
                    dve.scalar_tensor_tensor(
                        sU[lane][:, GB * i_:GB * i_ + GB, 1:P + 1], tD[lane].rearrange("p (b t) -> p b t", b=GB), 1.0,
                        banks[lane][1 + i_].rearrange("p (b t) -> p b t", b=GB), ALU.add, ALU.mult).then_inc(l0.u_ready, 1)
                elif family == "a":
                    decay = sA[lane][:, GB * i_:GB * i_ + GB, 1:P + 1]
                    dve.wait_ge(l0.t_act, 6 * n + 3 * i_ + 2)
                    dve.tensor_scalar(decay, decay, 0.5, 0.5, ALU.mult, ALU.add).then_inc(l0.a_ready, 1)
                elif family == "scan":
                    dve.wait_ge(l0.a_ready, 2 * n + 2)
                    dve.wait_ge(l0.u_ready, 2 * n + 2)
                    dve.wait_ge(l0.s_carry, n + 1)
                    flat = lambda v: v.rearrange("p a t -> p (a t)")
                    dve.tensor_tensor_scan(flat(sH[lane]), flat(sA[lane]), flat(sU[lane]), 0.0, ALU.mult, ALU.add).then_inc(l0.c_ready, 1)
                elif family == "gated":
                    if i_ == 0:
                        dve.wait_ge(l0.c_ready, n + 1)
                        for half in range(NH):
                            i = dve.tensor_scalar(carry[:, half, bass.ds(GB * g, GB)].rearrange("p (b o) -> p b o", o=1),
                                                  sH[lane][:, GB * half:GB * half + GB, P:P + 1], 1.0, None, ALU.mult)
                        i.then_inc(l0.s_scan, 1)
                        dve.wait_ge(l0.t_act, 6 * n + 6)
                    tC = w.qT[:, i_, :].rearrange("p (b t) -> p b t", b=GB)
                    i = dve.scalar_tensor_tensor(tC, tC, 1.0, sH[lane][:, GB * i_:GB * i_ + GB, 1:P + 1], ALU.add, ALU.mult)
                    if i_:
                        i.then_inc(l0.g_ready, 1)
                elif family == "x1":
                    dve.wait_ge(l0.y_ready, 2 * n + i_ + 1)
                    if i_ == 0:
                        dve.wait_ge(l0.f_base, 2 * n + 1)
                    add_product(lane, i_, l0.x1_ready)
                elif family == "x3":
                    dve.wait_ge(l0.f_proj, 2 * n + i_ + 1)
                    if i_ == 0:
                        dve.wait_ge(l0.f_base, 2 * n + 2)
                    add_product(lane, i_, l0.x3_ready)
                elif family == "rows":
                    position_rows(i_, c, g, n)
                elif family == "size":
                    dve.wait_ge(ctx_pe, positions(c, g) + c + 1)
                    dve.tensor_scalar(nrm[:, 0, :], qc[:, 0:GB], 1e-24, None, ALU.max).then_inc(n_a, 1)
                elif family == "x4":
                    if i_ == 0:
                        dve.wait_ge(n_b, n + 1)
                        dve.wait_ge(x3_load, 16 * n + 16)
                    x = tiles[1].xres
                    for b in (2 * i_, 2 * i_ + 1):
                        i = dve.scalar_tensor_tensor(x[:, b, :], pairs[1][:, b * D:(b + 1) * D], nrm[:, 1, b:b + 1],
                                                     x[:, b, :], ALU.mult, ALU.add)
                    i.then_inc(x4_ready, 1)
                elif family == "router":
                    l3 = qc[:, 0:GB * NE].rearrange("p (b e) -> p b e", b=GB)
                    bc = lambda v: v.rearrange("p (b o) -> p b o", o=1).broadcast_to([P, GB, NE])
                    if i_ == 1:
                        dve.wait_ge(r_pe, n + 1)
                        dve.tensor_reduce(lmx[:, 0, :], l3, AX_X, ALU.max).then_inc(r_small, 1)
                        dve.wait_ge(r_small, 4 * n + 1)
                        dve.tensor_tensor(lg[:, 0, :, :], l3, bc(lmx[:, 0, :]), ALU.subtract).then_inc(r_small, 1)
                        return
                    dve.wait_ge(r_exp, n + 1)
                    dve.scalar_tensor_tensor(lg[:, 2, :, :], lg[:, 1, :, :], 1.0,
                                             rank[:, :].rearrange("p (o e) -> p o e", o=1).broadcast_to([P, GB, NE]),
                                             ALU.is_ge, ALU.mult).then_inc(r_small, 1)
                    dve.wait_ge(r_small, 4 * n + 3)
                    dve.tensor_reduce(lmx[:, 1, :], lg[:, 2, :, :], AX_X, ALU.max).then_inc(r_small, 1)
                    dve.wait_ge(r_small, 4 * n + 4)
                    dve.tensor_tensor(lg[:, 3, :, :], lg[:, 2, :, :], bc(lmx[:, 1, :]), ALU.is_equal).then_inc(r_oh, 1)
                elif family == "leaky":
                    h_ = hr[i_ % 2]
                    dve.wait_ge(fc_relu, NE * n + i_ + 1)
                    dve.tensor_tensor(h_[:, :], banks[1][2 + i_ % 2], h_[:, :], ALU.add).then_inc(fc_sum, 1)
                elif family == "kept":
                    h_ = hr[i_ % 2]
                    dve.wait_ge(fc_sum, NE * n + i_ + 1)
                    dve.wait_ge(sel_pe, NE * n + i_ + 1)
                    dve.tensor_tensor(h_[:, :], banks[1][2 + i_ % 2], h_[:, :], ALU.mult).then_inc(fc_mask, 1)
                elif family == "x6":
                    if i_ == 0:
                        dve.wait_ge(moe_pe, NE * n + NE)
                    add_product(1, i_, x6_ready)

            def position_rows(part, c, g, n):
                m3 = lambda j: mrow[:, j, :].rearrange("p (b t) -> p b t", b=GB)
                z3 = lambda j: zrow[:, j, :].rearrange("p (b t) -> p b t", b=GB)
                J = jrow[:, 0:1, c * P:(c + 1) * P].broadcast_to([1, GB, P])
                RJ = jrow[:, 1:2, c * P:(c + 1) * P].broadcast_to([1, GB, P])
                if part == 2:
                    dve.wait_ge(z_pe, n + 1)
                    dve.tensor_scalar(m3(0)[:, :, 1:P + 1], qc[0:1, :].rearrange("p (b t) -> p b t", b=GB), 0.0, None, ALU.max)
                    dve.memset(m3(0)[:, :, 0:1], 0.0)
                    dve.tensor_copy(m3(1)[:, :, 0:1], mcarry[:, bass.ds(GB * g, GB)].rearrange("p (b o) -> p b o", o=1))
                    dve.tensor_scalar(zrow[:, 1, :], qc[32:33, :], 0.0, 1.0 / S, ALU.max, ALU.mult)
                    dve.tensor_scalar(zrow[:, 2, :], qc[64:65, :], 0.0, None, ALU.max).then_inc(z_small, 1)
                    dve.wait_ge(z_small, 5 * n + 1)
                    dve.tensor_tensor(z3(2), z3(2), J, ALU.mult).then_inc(z_small, 1)
                    dve.wait_ge(z_small, 5 * n + 2)
                    dve.tensor_tensor(m3(1)[:, :, 1:P + 1], z3(1), z3(2), ALU.add).then_inc(z_small, 1)
                    return
                dve.wait_ge(z_small, 5 * n + 3)
                dve.tensor_tensor_scan(mrow[:, 2, :], mrow[:, 0, :], mrow[:, 1, :], 0.0, ALU.mult, ALU.add).then_inc(z_small, 1)
                dve.wait_ge(z_exp, n + 1)
                dve.tensor_scalar(zrow[:, 0, :], zrow[:, 0, :], 1.0, 0.5 ** 0.5, ALU.add, ALU.mult).then_inc(z_small, 1)
                dve.wait_ge(z_small, 5 * n + 4)
                dve.tensor_scalar(mcarry[:, bass.ds(GB * g, GB)].rearrange("p (b o) -> p b o", o=1), m3(2)[:, :, P:P + 1],
                                  1.0, None, ALU.mult)
                dve.wait_ge(z_small, 5 * n + 5)
                dve.tensor_tensor(urow[0:1, :].rearrange("p (b t) -> p b t", b=GB), z3(0), RJ, ALU.mult).then_inc(u_rows, 1)
                dve.scalar_tensor_tensor(urow[32:33, :].rearrange("p (b t) -> p b t", b=GB), m3(2)[:, :, 1:P + 1], -1.0,
                                         z3(0), ALU.mult, ALU.mult).then_inc(u_rows, 1)
                dve.wait_ge(u_rows, 2 * n + 2)

            def dve_lstm(family, s, c, time, k, pieces):
                k = k + s
                if family == "cell":
                    dve.wait_ge(l_tanh, k + 1)
                    dve.scalar_tensor_tensor(uprod[:, :], gates[:, 0:40], 1.0, gates[:, 60:100], ALU.add, ALU.mult).then_inc(l_u, 1)
                    dve.wait_ge(l_u, k + 1)
                    dve.scalar_tensor_tensor(gates[:, 80:100], uprod[:, 20:40], 0.5, uprod[:, 0:20], ALU.mult,
                                             ALU.add).then_inc(l_c, 1)
                    return
                dve.wait_ge(l_tc, k + 1)
                dve.scalar_tensor_tensor(hnew[0:B, 0:PE_], gates[:, 40:60], 1.0, tcell[:, :], ALU.add,
                                         ALU.mult).then_inc(l_h, 1)
                dve.wait_ge(l_h, k + 1)
                if s % STEPS == STEPS - 1:
                    dve.transpose(slots[96:128, 0:2, :].rearrange("p s b -> p (s b)"), hnew[:, :])
                dve.transpose(slots[96:128, s % STEPS + 1:s % STEPS + 3, :].rearrange("p s b -> p (s b)"), hnew[:, :]).then_inc(l_t, 1)
                if s % 8 == 7:
                    dve.wait_ge(l_t, k + 2)
                    dve.tensor_scalar(R[96:128, :, bass.ds((c % 3) * P + time + s - 7, 8)].rearrange("p b t -> p t b"),
                                      slots[96:128, s % STEPS - 6:s % STEPS + 2, :], 1.0, None, ALU.mult).then_inc(l_out, 1)

            run_stages(dve, "dve", dve_step, dve_lstm)

        @block.gpsimd
        def _(pool):
            pool.wait_ge(prep_done, 1)

            def add_row(l, row, done):
                w = tiles[l]
                pool.tensor_tensor(w.xres[:, :, :], w.xres[:, :, :],
                                   row[:, :].rearrange("p (o d) -> p o d", o=1).broadcast_to([P, GB, D]),
                                   ALU.add).then_inc(done, 1)

            def pool_lstm(family, i_, c, time, k, pieces):
                if i_ == 0:
                    for lane in range(2):
                        pool.wait_ge(scans[lane].xg_ready, chunks_done(lane, c))
                if positive(k - 24 + 8 * i_):
                    pool.wait_ge(l_pe, k - 24 + 8 * i_)
                at_ = 8 * (i_ % (STEPS // 8))
                pool.tensor_copy(slots[0:96, at_:at_ + 8, :],
                                 R[0:96, :, bass.ds((c % 3) * P + time + 8 * i_, 8)].rearrange("p b t -> p t b")
                                 ).then_inc(l_in, 1)

            def pool_step(lane, layer, family, i_, c, g, n, m):
                t, w, l0, s = at[lane], tiles[lane], scans[lane], ln[lane]
                b, j = divmod(i_, 2)
                N = 2 * GB * m + i_
                if family == "root":
                    if i_ == 8:
                        pool.wait_ge(n_a, n + 1)
                        pool.tensor_tensor(nrm[:, 1, :], nrm[:, 0, :], neghalf[:, :], ALU.pow).then_inc(n_b, 1)
                    elif i_ == 9:
                        pool.wait_ge(s.small, s.before_small(0, n, 0) + 8)
                        pool.tensor_tensor(s.rstd[:, 1, :], s.ve[:, 1, :], neghalf[:, :], ALU.pow).then_inc(s.inv, 1)
                    else:
                        pool.wait_ge(s.small, s.before_small(layer, n, i_) + 5)
                        pool.tensor_tensor(s.rstd[:, 0, :], s.ve[:, 0, :], neghalf[:, :], ALU.pow).then_inc(s.inv, 1)
                elif family == "brow":
                    pool.wait_ge(l0.base_ready, n + 1)
                    add_row(lane, rowOut, l0.f_base)
                elif family == "frow":
                    pool.wait_ge(s.normed, 2 * s.before(0, n, 3))
                    add_row(lane, rowF, l0.f_base)
                elif family == "orow":
                    add_row(lane, rowO[layer], t.base)
                elif family == "keys":
                    if i_ == 0:
                        pool.wait_ge(t.m_load, 32 * n + 32 if layer == 0 else 32 * LAYER0_UNITS[lane] + 48 * n + 48)
                    if positive(N - 3):
                        pool.wait_ge(t.scores, N - 3)
                    pool.tensor_tensor(
                        w.kbd[b % 2][:, j, :, :], w.kg[:, j, b:b + 1, :].broadcast_to([P, NE, SK]),
                        headmask[:, :].rearrange("p (a o) -> p a o", o=1).broadcast_to([P, NE, SK]), ALU.mult
                    ).then_inc(t.kbd, 1)
                elif family == "shift":
                    ex = w.ex[b % 2][:, NE * j:NE * j + NE, :]
                    pool.wait_ge(t.top, N + 1)
                    pool.tensor_tensor(ex, ex, w.mx[:, i_ % 4, :].rearrange("p (a o) -> p a o", o=1).broadcast_to([P, NE, SK]),
                                       ALU.subtract).then_inc(t.shifted, 1)
                elif family == "gate":
                    ex = w.ex[b % 2][:, NE * j:NE * j + NE, :]
                    pool.wait_ge(t.summed, 2 * GB * n + i_ + 1)
                    pool.tensor_tensor(ex, ex, gp[:, b:b + 1, :].broadcast_to([P, NE, SK]), ALU.mult).then_inc(t.gated, 1)
                elif family == "weight2":
                    k = positions(c, g) + i_
                    wt, sq = wT[i_ % 2], wsq[i_ % 2]
                    pool.wait_ge(pos_w, k + 1)
                    if i_ == c:
                        w3 = wt[:, :].rearrange("p (b t) -> p b t", b=GB)
                        pool.tensor_tensor(w3, w3, tri[:, :].rearrange("p (o t) -> p o t", o=1).broadcast_to([P, GB, P]),
                                           ALU.mult).then_inc(pos_m, 1)
                        pool.wait_ge(pos_m, n + 1)
                    pool.tensor_tensor(sq[:, :], wt[:, :], wt[:, :], ALU.mult).then_inc(pos_w2, 1)

            run_stages(pool, "pool", pool_step, pool_lstm)


def _constants():
    import numpy as np
    p = np.arange(P)
    gatesel = np.zeros((80, 80), np.float32)
    for j in range(PE_):
        gatesel[j, j] = gatesel[20 + j, 20 + j] = gatesel[60 + j, 40 + j] = 0.5
        gatesel[40 + j, 60 + j] = 1.0
    posl = np.zeros((64, NC_, P), np.float32)
    posl[0] = np.arange(S).reshape(NC_, P)
    posl[32] = 1.0
    j = np.arange(1, S + 1, dtype=np.float32)
    sel = np.repeat(np.eye(NE, dtype=np.float32)[:, :, None], P, axis=2)
    return {
        "c_ident": np.eye(P, dtype=np.float32), "c_tri": (p[:, None] <= p[None, :]).astype(np.float32),
        "c_headmask": (p[:, None] // HD == np.arange(NE)[None, :]).astype(np.float32),
        "c_rank": np.tile(np.arange(NE, 0, -1, dtype=np.float32), (P, 1)),
        "c_sel": sel, "c_posl": posl, "c_jrow": np.stack([j / np.float32(S), np.float32(1.0) / j])[None],
        "c_gatesel": gatesel,
    }


def kernel(**inputs):
    import numpy as _np
    import concourse.bacc as _bacc
    from concourse import mybir as _mybir
    from concourse.bass_utils import run_bass_kernel_spmd as _run

    i = {k: _np.asarray(v) for k, v in inputs.items()}
    columns = lambda v: v.reshape(NH, P).T
    w_ih = _np.zeros((D, 96), _np.float32)
    w_ih[:, 0:80] = i["L1_attn_W_ih"].T
    w_hh = i["L1_attn_W_hh"].T[:, [*range(0, 40), *range(60, 80), *range(40, 60)]]
    b_gates = _np.zeros((96, 2), _np.float32)
    b_gates[0:80, 0], b_gates[0:80, 1], b_gates[80, 0] = i["L1_attn_b_ih"], i["L1_attn_b_hh"], 1.0
    w_mu_sig, b_mu_sig = _np.zeros((PE_, P), _np.float32), _np.zeros((1, P), _np.float32)
    w_mu_sig[:, 0:96:32], w_mu_sig[:, 96:97] = i["L1_attn_W_mu"].T, i["L1_attn_W_sig"].T
    b_mu_sig[0, 0:96:32], b_mu_sig[0, 96:97] = i["L1_attn_b_mu"], i["L1_attn_b_sig"]
    data = {
        "x": i["x"], "ctx": i["ctx_1024"].transpose(2, 0, 1), "fside": i["fside_BxSxS2_0"],
        "mask0": i["mask_BxSxS2_bf1"].view(_np.uint8), "mask1": i["mask_BxSxS2_ik1"],
        "norm_w": columns(i["L0_attn_norm_w"]), "A_w": i["L0_attn_A_w"].T, "A_b": columns(i["L0_attn_A_b"]), "B_w": i["L0_attn_B_w"].T,
        "C_w": i["L0_attn_C_w"].T, "D_w": i["L0_attn_D_w"].T, "out_w": i["L0_attn_out_w"].T, "out_b": i["L0_attn_out_b"],
        "Wq": i["L0_xattn_Wq"].T, "bq": columns(i["L0_xattn_bq"]), "Wk": i["L0_xattn_Wk"].T, "bk": columns(i["L0_xattn_bk"]),
        "Wv": i["L0_xattn_Wv"].T, "bv": i["L0_xattn_bv"], "Wo": i["L0_xattn_Wo"].T, "bo": i["L0_xattn_bo"],
        "W": i["L0_ffn_W"].T, "b": i["L0_ffn_b"], "V_r": i["L0_ffn_V_r"].T, "C": i["L0_ffn_C"].T,
        "W_ih": w_ih, "W_hh": w_hh, "b_gates": b_gates, "W_mu_sig": w_mu_sig, "b_mu_sig": b_mu_sig,
        "wq_k": i["L1_xattn_wq_k"], "wq_b": columns(i["L1_xattn_wq_b"]), "wk_k": i["L1_xattn_wk_k"], "wk_b": columns(i["L1_xattn_wk_b"]),
        "wv_k": i["L1_xattn_wv_k"], "wv_b": i["L1_xattn_wv_b"], "wo_k": i["L1_xattn_wo_k"], "wo_b": i["L1_xattn_wo_b"],
        "w_router": i["L1_ffn_w_router"].T,
        "w_fc": i["L1_ffn_w_fc"].transpose(2, 0, 1).reshape(D, NE * P),
        "w_proj": i["L1_ffn_w_proj"].transpose(2, 0, 1),
    }
    data.update(_constants())
    nc = _bacc.Bacc("TRN2", target_bir_lowering=False, num_devices=1)
    arrays, args = {}, {}
    for name, v in data.items():
        v = _np.ascontiguousarray(v)
        arrays[f"in_{name}"] = v
        args[name] = nc.dram_tensor(f"in_{name}", v.shape, _mybir.dt.from_np(v.dtype), kind="ExternalInput").ap()
    out = nc.dram_tensor("out_0", (B, S, D), F32, kind="ExternalOutput").ap()
    decoder_program(nc, args, out)
    r = _run(nc, [arrays], core_ids=[0])
    return r.results[0]["out_0"]
```
